# Optimizing a Trainium2 kernel written in Bass

```python
import numpy as np
import jax
import jax.numpy as jnp

def _softmax(x, axis=-1):
    return jax.nn.softmax(x, axis=axis)

def _gelu(x):
    return jax.nn.gelu(x, approximate=True)

def _silu(x):
    return jax.nn.silu(x)

def _sigmoid(x):
    return jax.nn.sigmoid(x)

def _layernorm(x, axis=-1, eps=1e-05):
    m = jnp.mean(x, axis=axis, keepdims=True)
    v = jnp.var(x, axis=axis, keepdims=True)
    return (x - m) / jnp.sqrt(v + eps)

def _scatter_add(tgt, idx, src, axis=0):
    return tgt.at[idx].add(src)

def _segment_sum(src, seg, n):
    return jax.ops.segment_sum(src, seg, n)
kernel_name = 'mk_seq_preln_d1_jaxref_r8_418462'

def setup_inputs(seed: int=0):
    np.random.seed(seed)
    _w = jnp.asarray

    def _L0_attn_setup():
        import jax, jax.numpy as jnp
        import numpy as np
        key = jax.random.key(seed)
        k1, k2, k3 = jax.random.split(key, 3)
        B, S, D, N = (2, 256, 128, 16)
        H = D // N
        x = jax.random.normal(k1, (B, S, D), dtype=jnp.float32)
        W_qkv = jax.random.normal(k2, (N, D, 3 * H), dtype=jnp.float32) / np.sqrt(D).astype(np.float32)
        W_out = jax.random.normal(k3, (N, H, D), dtype=jnp.float32) / np.sqrt(D).astype(np.float32)
        return {'x': x, 'W_qkv': W_qkv, 'W_out': W_out}
    _L0_attn_in = _L0_attn_setup()

    def _L0_ffn_setup():
        import jax, jax.numpy as jnp
        import numpy as np
        E, K = (8, 2)
        B, S, H, F = (2, 256, 128, 512)
        EPS = 1e-12

        def _expert_ffn(xf, Wi_e, bi_e, Wg_e, bg_e, Wo_e, bo_e, g_e, b_e):
            h = jax.nn.gelu(xf @ Wi_e + bi_e, approximate=False) * jax.nn.sigmoid(xf @ Wg_e + bg_e)
            r = xf + (h @ Wo_e + bo_e)
            mu = jnp.mean(r, axis=-1, keepdims=True)
            var = jnp.mean(jnp.square(r - mu), axis=-1, keepdims=True)
            return (r - mu) * jax.lax.rsqrt(var + EPS) * g_e + b_e
        key = jax.random.key(seed)
        ks = jax.random.split(key, 8)
        s = 0.02
        return {'x': jax.random.normal(ks[0], (B, S, H), jnp.float32), 'Wr': jax.random.normal(ks[1], (H, E), jnp.float32) * s, 'br': jnp.zeros((E,), jnp.float32), 'Wi': jax.random.normal(ks[2], (E, H, F), jnp.float32) * s, 'bi': jnp.zeros((E, F), jnp.float32), 'Wg': jax.random.normal(ks[3], (E, H, F), jnp.float32) * s, 'bg': jnp.zeros((E, F), jnp.float32), 'Wo': jax.random.normal(ks[4], (E, F, H), jnp.float32) * s, 'bo': jnp.zeros((E, H), jnp.float32), 'gamma': jnp.ones((E, H), jnp.float32), 'beta': jnp.zeros((E, H), jnp.float32)}
    _L0_ffn_in = _L0_ffn_setup()
    _d = {'L0_attn_x': _L0_attn_in['x'], 'L0_attn_W_qkv': _L0_attn_in['W_qkv'], 'L0_attn_W_out': _L0_attn_in['W_out'], 'L0_ffn_Wr': _L0_ffn_in['Wr'], 'L0_ffn_br': _L0_ffn_in['br'], 'L0_ffn_Wi': _L0_ffn_in['Wi'], 'L0_ffn_bi': _L0_ffn_in['bi'], 'L0_ffn_Wg': _L0_ffn_in['Wg'], 'L0_ffn_bg': _L0_ffn_in['bg'], 'L0_ffn_Wo': _L0_ffn_in['Wo'], 'L0_ffn_bo': _L0_ffn_in['bo'], 'L0_ffn_gamma': _L0_ffn_in['gamma'], 'L0_ffn_beta': _L0_ffn_in['beta']}
    _x0 = _d['L0_attn_x']
    _d['L0_attn_x'] = jax.random.normal(jax.random.fold_in(jax.random.key(seed), 1), (16, 512, 128), dtype=_x0.dtype)
    del _x0
    return _d

def reference(L0_attn_x, L0_attn_W_qkv, L0_attn_W_out, L0_ffn_Wr, L0_ffn_br, L0_ffn_Wi, L0_ffn_bi, L0_ffn_Wg, L0_ffn_bg, L0_ffn_Wo, L0_ffn_bo, L0_ffn_gamma, L0_ffn_beta):

    def _L0_attn_ref(x, W_qkv, W_out):
        import jax, jax.numpy as jnp
        import numpy as np
        B, S, D = x.shape
        head_dim = W_qkv.shape[-1] // 3
        qkv = jnp.einsum('bsd,ndh->bnsh', x, W_qkv)
        q, k, v = jnp.split(qkv, 3, axis=-1)
        scale = jnp.asarray(1.0 / np.sqrt(head_dim), dtype=x.dtype)
        attn = jnp.einsum('bnqh,bnkh->bnqk', q, k) * scale
        mask = jnp.asarray(-10000000000.0, dtype=x.dtype) * (1.0 - jnp.tril(jnp.ones((S, S), dtype=x.dtype)))
        attn = jax.nn.softmax(attn + mask, axis=-1)
        out = jnp.einsum('bnqk,bnkh->bnqh', attn, v)
        out = out.reshape(B, -1, S)
        return jnp.einsum('bds,nhd->bsd', out, W_out)

    def _L0_ffn_ref(x, Wr, br, Wi, bi, Wg, bg, Wo, bo, gamma, beta):
        import jax, jax.numpy as jnp
        import numpy as np
        E, K = (8, 2)
        B, S, H, F = (2, 256, 128, 512)
        EPS = 1e-12

        def _expert_ffn(xf, Wi_e, bi_e, Wg_e, bg_e, Wo_e, bo_e, g_e, b_e):
            h = jax.nn.gelu(xf @ Wi_e + bi_e, approximate=False) * jax.nn.sigmoid(xf @ Wg_e + bg_e)
            r = xf + (h @ Wo_e + bo_e)
            mu = jnp.mean(r, axis=-1, keepdims=True)
            var = jnp.mean(jnp.square(r - mu), axis=-1, keepdims=True)
            return (r - mu) * jax.lax.rsqrt(var + EPS) * g_e + b_e
        b, s, h = x.shape
        T = b * s
        xf = x.reshape(T, h)
        probs = jax.nn.softmax(xf @ Wr + br, axis=-1)
        topw, topi = jax.lax.top_k(probs, K)
        topw = topw / jnp.sum(topw, axis=-1, keepdims=True)
        c = jnp.zeros((T, E), x.dtype).at[jnp.arange(T)[:, None], topi].set(topw)
        y = jax.vmap(_expert_ffn, in_axes=(None, 0, 0, 0, 0, 0, 0, 0, 0))(xf, Wi, bi, Wg, bg, Wo, bo, gamma, beta)
        out = jnp.einsum('te,eth->th', c, y)
        return out.reshape(b, s, h)
    x = L0_attn_x
    x = x + _L0_attn_ref(_layernorm(x, axis=-1), L0_attn_W_qkv, L0_attn_W_out)
    x = x + _L0_ffn_ref(_layernorm(x, axis=-1), L0_ffn_Wr, L0_ffn_br, L0_ffn_Wi, L0_ffn_bi, L0_ffn_Wg, L0_ffn_bg, L0_ffn_Wo, L0_ffn_bo, L0_ffn_gamma, L0_ffn_beta)
    return x

_drawn_inputs = setup_inputs


def setup_inputs(seed=0):
    import zlib

    import numpy as np

    out = dict(_drawn_inputs(seed))
    spreads = {'L0_ffn_br': (0.0, 0.1),
     'L0_ffn_bi': (0.0, 0.8),
     'L0_ffn_bg': (0.0, 0.8),
     'L0_ffn_bo': (0.0, 0.34),
     'L0_ffn_gamma': (1.0, 0.2),
     'L0_ffn_beta': (0.0, 0.1)}
    factors = {'L0_ffn_Wi': 5.908, 'L0_ffn_Wg': 8.0, 'L0_ffn_Wo': 5.387}
    for name, (base, spread) in spreads.items():
        noise = np.random.default_rng([zlib.crc32(name.encode()), seed]).standard_normal(out[name].shape)
        drawn = base * np.exp(spread * noise) if base else spread * noise
        out[name] = jnp.asarray(drawn.astype(out[name].dtype))
    for name, factor in factors.items():
        out[name] = (out[name] * factor).astype(out[name].dtype)
    return out
```

```python
import concourse.bass as bass
from concourse import mybir
from contextlib import ExitStack


def attention_and_routed_experts(nc, x, w_qkv, w_out, wr, br, wi, bi, wg, bg, wo, bo, gamma, beta, out,
                                 BATCHES=16):
    F32, F32R, BF16, I32 = mybir.dt.float32, mybir.dt.float32r, mybir.dt.bfloat16, mybir.dt.int32
    ALU, ACT, AX = mybir.AluOpType, mybir.ActivationFunctionType, mybir.AxisListType

    B, S, D = x.shape
    NH, _, HD3 = w_qkv.shape
    HD = HD3 // 3
    E, _, F = wi.shape
    P = 128
    NT = S // P
    G = 4
    NG = NH // G
    TERMS = 3
    MROW = TERMS * G * HD
    SCALE = float(HD) ** -0.5
    LN_EPS, EXPERT_EPS = 1e-5, 1e-12
    MASK = -1e10

    ctx = ExitStack()
    with ctx:
        part = ctx

        def sb(name, shape, dt=F32):
            return part.enter_context(nc.sbuf_tensor(name, shape, dt))

        def pb(name, shape, dt=F32):
            return part.enter_context(nc.psum_tensor(name, shape, dt))

        def sem(name):
            return ctx.enter_context(nc.semaphore(name))

        x1_d = nc.dram_tensor("x1_scratch", (BATCHES * S, D), F32).ap()
        xn2_d = nc.dram_tensor("xn2_scratch", (BATCHES * S, D), F32).ap()

        ident = sb("ident", [P, P])
        identb = sb("identb", [P, P], BF16)
        maskneg = sb("maskneg", [P, P], BF16)
        fold = sb("fold", [P, P // 2])
        ones_col = sb("ones_col", [P, 1])
        rowmask = sb("rowmask", [P, G])
        rowsel = sb("rowsel", [P, P])
        wq = sb("wq", [P, P])
        wk = sb("wk", [P, P])
        wv = sb("wv", [P, P])
        wout = sb("wout", [P, D])
        wsum = sb("wsum", [P, 1])
        zeros = sb("zeros", [P, S])
        minus_half = sb("minus_half", [P, 2 * NT])
        wr_sb = sb("wr_sb", [P, E])
        br_bc = sb("br_bc", [P, E])

        logits = sb("logits", [P, BATCHES * NT, E])

        part = attention = ExitStack()
        x_in = sb("x_in", [P, NT, D])
        x_res = sb("x_res", [P, NT, D])
        stats = sb("stats", [P, NT, 6])
        mv = sb("mv", [P, NT, 2])
        rstd = sb("rstd", [P, NT])
        xn = sb("xn", [P, NT, D])
        xnT = sb("xnT", [P, S])
        q_hi = sb("q_hi", [P, S], F32R)
        q_lo = sb("q_lo", [P, S], F32R)
        k_hi = sb("k_hi", [P, S], F32R)
        k_lo = sb("k_lo", [P, S], F32R)
        q_stack = sb("q_stack", [P, NG, S], F32R)
        k_stack = sb("k_stack", [P, NG, S], F32R)
        k_pad = sb("k_pad", [P, NH, S], F32R)
        v_aug = sb("v_aug", [P, NT, NH, 32])
        neg_max = sb("neg_max", [P, 2, NT, MROW + G])
        PT_OFF = [0, 512, 1024, 896]
        PT_COLS = 1280
        probs = sb("probs", [P, 2, G, PT_COLS])
        pv_sb = sb("pv_sb", [P, S])
        rden = sb("rden", [P, NT, G])
        o_masked = sb("o_masked", [P, HD, NH, NT, 2])
        attn_T = sb("attn_T", [P, S])
        x1 = sb("x1_sb", [P, NT, D])
        stats2 = sb("stats2", [P, NT, 6])
        mv2 = sb("mv2", [P, NT, 2])
        rstd2 = sb("rstd2", [P, NT])
        xn2 = sb("xn2", [P, NT, D])
        xn2T = sb("xn2T", [P, S])
        sa = pb("sa", [P, 2, 2, S])
        st = pb("st", [P, 2, S])
        pv = pb("pv", [P, S])
        misc = pb("misc", [P, S])

        w_loaded = sem("w_loaded")
        const_a = sem("const_a")
        consts = sem("consts")
        vconst = sem("vconst")
        x_loaded = sem("x_loaded")
        xres_loaded = sem("xres_loaded")
        ln1_done = sem("ln1_done")
        x1_done = sem("x1_done")
        ln2_done = sem("ln2_done")
        misc_written = sem("misc_written")
        misc_read = sem("misc_read")
        hi_done = sem("hi_done")
        lo_done = sem("lo_done")
        q_stacked = [sem(f"q_stacked{g}") for g in range(NG)]
        k_stacked = [sem(f"k_stacked{g}") for g in range(NG)]
        kpad_done = sem("kpad_done")
        var1_done, rstd1_done = sem("var1_done"), sem("rstd1_done")
        var2_done, rstd2_done = sem("var2_done"), sem("rstd2_done")
        sa_written = sem("sa_written")
        sa_read = sem("sa_read")
        st_written = sem("st_written")
        exp_done = sem("exp_done")
        masked = sem("masked")
        pv_written = sem("pv_written")
        pv_read = sem("pv_read")
        vaug_done = sem("vaug_done")
        act_sb = sem("act_sb")
        om_done = sem("om_done")
        logits_done = sem("logits_done")
        dve_chain = sem("dve_chain")
        x1_stored = sem("x1_stored")
        xn2_stored = sem("xn2_stored")

        MISC = {n: k for k, n in enumerate(
            ["mT0", "mT1", "OT0", "xnT", "Q", "K", "mT2", "OT1", "mT3", "OT2",
             "V", "OT3", "RT", "R2", "XT", "LG"])}
        HEAD = ["xnT", "Q", "K", "V"]
        MISC_LAST = {n: k for k, n in enumerate([n for n in MISC if n not in HEAD])}

        def use(name, b):
            if isinstance(b, int) and b < 0:
                return HEAD.index(name) + 1
            order = MISC_LAST if isinstance(b, int) and b == BATCHES - 1 else MISC
            return b * len(MISC) + (len(HEAD) + order[name] + 1)

        NA, NB_ = 2 * NT, 3 * G

        PHASE = [("A", 0), ("A", 1), ("mT", 0), ("PV", 0), ("B", 0), ("PV", 1), ("B", 1), ("A", 2),
                 ("PV", 2), ("B", 2), ("PV", 3), ("B", 3), ("A", 3), ("B", 4), ("B", 5), ("OT", 0),
                 ("A", 4), ("B", 6), ("B", 7), ("A", 5), ("B", 8), ("B", 9), ("A", 6), ("B", 10),
                 ("A", 7), ("B", 11)]
        LAST = [("A", 0), ("PV", 0), ("PV", 1), ("PV", 2), ("PV", 3), ("A", 1), ("V", 0), ("A", 2),
                ("OT", 0), ("A", 3), ("RT", 0), ("A", 4), ("R2", 0), ("A", 5), ("A", 6), ("XT", 0),
                ("A", 7), ("LG", 0)]
        OUTPUT = [i for i in LAST if i[0] not in ("A", "V")]

        def phases(last):
            yield 1, 0, None, False, PHASE
            yield 2, 1, 0, False, PHASE
            yield 3, 2, 1, not last, PHASE
            yield None, 3, 2, False, PHASE
            yield (None if last else 0), None, 3, False, (OUTPUT if last else LAST)

        def items(phase):
            a, bg_, pvg, _, order = phase
            for kind, k in order:
                if kind == "A" and a is None or kind in ("B", "mT") and bg_ is None \
                        or kind in ("PV", "OT") and pvg is None:
                    continue
                yield kind, k

        def passes(eng, body, n):
            if n > 1:
                with eng.Fori(0, n - 1) as b:
                    body(b, False)
            body(n - 1, True)

        def wait_apart(eng, sem_, value):
            if not isinstance(value, int):
                value = eng.to_reg(value)
                eng.wait_ge(consts, 1)
            eng.wait_ge(sem_, value)

        block = attention.enter_context(nc.Block())

        @block.sync
        def _(sp):
            qkv_v = w_qkv.rearrange("n d h -> d n h")
            for w, c in ((wq, 0), (wk, 1), (wv, 2)):
                sp.dma_start(w[:, :].rearrange("d (n h) -> d n h", h=HD),
                             qkv_v[:, :, c * HD:(c + 1) * HD]).then_inc(w_loaded, 16)
            sp.dma_start(wout[:, :], w_out.rearrange("n h d -> (n h) d")).then_inc(w_loaded, 16)
            sp.dma_start(wr_sb[:, :], wr).then_inc(w_loaded, 16)
            sp.dma_start(br_bc[:, :], br.rearrange("(a e) -> a e", a=1).broadcast_to([P, E])).then_inc(w_loaded, 16)

            def load_x(nb):
                if not (isinstance(nb, int) and nb == 0):
                    wait_apart(sp, ln1_done, nb)
                sp.dma_start(x_in[:, :, :], x[nb, :, :].rearrange("(i p) d -> p i d", p=P)).then_inc(x_loaded, 16)

            def stack(nb, first):
                for g in range(NG):
                    if g == 0:
                        wait_apart(sp, hi_done, 2 * nb + 2)
                        wait_apart(sp, lo_done, 2 * nb + 2)
                    if not first:
                        wait_apart(sp, st_written, (nb - 1) * (NG * NB_) + NB_ * (g + 1))
                        wait_apart(sp, kpad_done, (nb - 1) * NH + G * (g + 1))
                    sp.dma_start(q_stack[MROW:P, g, :].bitcast(F32), zeros[MROW:P, :]).then_inc(q_stacked[g], 16)
                    for c in range(TERMS):
                        rows = slice(32 * c, 32 * c + 32)
                        src = slice(32 * g, 32 * g + 32)
                        sp.dma_start(q_stack[rows, g, :].bitcast(F32), (q_hi, q_lo, q_hi)[c][src, :].bitcast(F32)).then_inc(q_stacked[g], 16)
                        sp.dma_start(k_stack[rows, g, :].bitcast(F32), (k_hi, k_hi, k_lo)[c][src, :].bitcast(F32)).then_inc(k_stacked[g], 16)

            def body(b, last):
                wait_apart(sp, x1_done, b + 1)
                sp.dma_start(x_res[:, :, :], x[b, :, :].rearrange("(i p) d -> p i d", p=P)).then_inc(xres_loaded, 16)
                if not last:
                    load_x(b + 1)
                    stack(b + 1, False)
                rows = x1_d.rearrange("(b i p) d -> b p i d", p=P, i=NT)
                rows2 = xn2_d.rearrange("(b i p) d -> b p i d", p=P, i=NT)
                wait_apart(sp, x1_done, b + 2)
                sp.dma_start(rows[b, :, :, :], x1[:, :, :]).then_inc(x1_stored, 16)
                wait_apart(sp, ln2_done, b + 1)
                sp.dma_start(rows2[b, :, :, :], xn2[:, :, :]).then_inc(xn2_stored, 16)

            sp.wait_ge(consts, 1)
            load_x(0)
            stack(0, True)
            passes(sp, body, BATCHES)
            sp.wait_ge(x1_stored, 16 * BATCHES + 1)
            sp.wait_ge(xn2_stored, 16 * BATCHES + 1)

        @block.gpsimd
        def _(pool):
            n = 0

            def c_(ins):
                nonlocal n
                n += 1
                ins.then_inc(const_a, 1)
                pool.wait_ge(const_a, n)

            c_(pool.memset(ident[:, :], 0.0))
            c_(pool.affine_select(out=ident[:, :], in_=ident[:, :], compare_op=ALU.not_equal, fill=1.0, base=0,
                                  pattern=[[-1, P]], channel_multiplier=1))
            c_(pool.tensor_copy(identb[:, :], ident[:, :]))
            c_(pool.memset(maskneg[:, :], 0.0))
            c_(pool.affine_select(out=maskneg[:, :], in_=maskneg[:, :], compare_op=ALU.is_ge, fill=MASK, base=0,
                                  pattern=[[-1, P]], channel_multiplier=1))
            c_(pool.memset(fold[:, :], 0.0))
            for half in (0, -P // 2):
                c_(pool.affine_select(out=fold[:, :], in_=fold[:, :], compare_op=ALU.not_equal, fill=1.0, base=half,
                                      pattern=[[-1, P // 2]], channel_multiplier=1))
            c_(pool.memset(ones_col[:, :], 1.0))
            c_(pool.memset(rowmask[:, :], 1.0))
            for c in range(TERMS):
                part = rowmask[32 * c:32 * c + 32, :]
                c_(pool.affine_select(out=part, in_=part, compare_op=ALU.is_ge, fill=0.0, base=0,
                                      pattern=[[-HD, G]], channel_multiplier=1))
                c_(pool.affine_select(out=part, in_=part, compare_op=ALU.is_ge, fill=0.0, base=HD - 1,
                                      pattern=[[HD, G]], channel_multiplier=-1))
            part = rowmask[MROW:P, :]
            c_(pool.memset(part, 0.0))
            c_(pool.affine_select(out=part, in_=part, compare_op=ALU.not_equal, fill=1.0, base=0,
                                  pattern=[[-1, G]], channel_multiplier=1))
            c_(pool.memset(k_stack[MROW:P, :, :].bitcast(F32), 1.0))
            c_(pool.memset(neg_max[:, :, :, :], 0.0))
            c_(pool.memset(v_aug[:, :, :, :], 0.0))
            c_(pool.memset(v_aug[:, :, :, HD:HD + 1], 1.0))
            c_(pool.memset(zeros[:, :], 0.0))
            c_(pool.memset(minus_half[:, :], -0.5))
            pool.memset(o_masked[:, :, :, :, :], 0.0).then_inc(consts, 1)
            pool.wait_ge(consts, 1)

            def causal_zeros(b, g):
                for j in range(G):
                    wait_apart(pool, exp_done, b * (NG * NB_) + NB_ * g + 3 * (j + 1))
                    for off, n_ in ((PT_OFF[0], 1), (PT_OFF[1], 1), (PT_OFF[3], 2)):
                        blk = probs[:, g % 2, j, off:off + n_ * P].rearrange("p (a q) -> p a q", q=P)
                        pool.affine_select(out=blk, in_=blk, compare_op=ALU.is_ge, fill=0.0, base=0,
                                           pattern=[[0, n_], [1, P]], channel_multiplier=-1).then_inc(masked, 1)

            def inverse_deviation(batch, var_done, rstd_done, rs_):
                pool.wait_ge(var_done, batch + 1)
                pool.tensor_tensor(rs_[:, :], rs_[:, :], minus_half[:, 0:NT], ALU.pow).then_inc(rstd_done, 1)

            inverse_deviation(0, var1_done, rstd1_done, rstd)
            def body(b, last):
                causal_zeros(b, 0)
                causal_zeros(b, 1)
                if not last:
                    inverse_deviation(b + 1, var1_done, rstd1_done, rstd)
                causal_zeros(b, 2)
                causal_zeros(b, 3)
                inverse_deviation(b, var2_done, rstd2_done, rstd2)

            passes(pool, body, BATCHES)

        @block.tensor
        def _(pe):
            pe.wait_ge(w_loaded, 16 * 6)
            pe.wait_ge(consts, 1)

            def misc_free(name, b):
                pe.wait_ge(misc_read, use(name, b) - 1)

            def prep(b):
                pe.wait_ge(ln1_done, b + 2)
                misc_free("xnT", b)
                for i in range(NT):
                    last = nc.tensor.transpose(misc[:, i * P:(i + 1) * P], xn[:, i, :], ident[:, :])
                last.then_inc(misc_written, 1)
                for name, w in (("Q", wq), ("K", wk)):
                    misc_free(name, b)
                    nc.tensor.matmul(misc[:, :], w[:, :], xnT[:, :], start=True, stop=True).then_inc(misc_written, 1)

            def values(b):
                misc_free("V", b)
                for i in range(NT):
                    last = nc.tensor.matmul(misc[:, i * P:(i + 1) * P], xnT[:, i * P:(i + 1) * P], wv[:, :],
                                            start=True, stop=True)
                last.then_inc(misc_written, 1)

            def a_step(nb, g, s):
                i, pair = s // 2, s % 2
                n = nb * (NG * NA) + NA * g + s
                if s == 0:
                    pe.wait_ge(q_stacked[g], 16 * (TERMS + 1) * (nb + 1))
                if i == 0:
                    pe.wait_ge(kpad_done, nb * NH + G * g + 2 * pair + 2)
                if not (isinstance(nb, int) and nb == 0 and g == 0 and s < 2):
                    pe.wait_ge(sa_read, n - 1)
                width = max(2 * P, P * (i + 1))
                for h in range(2):
                    nc.tensor.matmul(sa[:, s % 2, h, 0:width], q_stack[:, g, i * P:(i + 1) * P],
                                     k_pad[:, G * g + 2 * pair + h, 0:width], start=True, stop=True)
                    last = nc.tensor.matmul(sa[:, s % 2, h, i * P:(i + 1) * P], identb[:, :], maskneg[:, :],
                                            start=False, stop=True, skip_group_check=True)
                last.then_inc(sa_written, 1)

            def b_step(b, g, t):
                j, part = t // 3, t % 3
                n = b * (NG * NB_) + NB_ * g + t
                if t == 0:
                    pe.wait_ge(act_sb, b * NG + g + 1)
                if g > 0 or t >= 2:
                    pe.wait_ge(exp_done, n - 1)
                h = G * g + j
                buf = st[:, t % 2, :]
                if part == 0:
                    mm = [(0, 0, 512)]
                elif part == 1:
                    mm = [(1, 0, 384)]
                else:
                    mm = [(3, 0, 256), (2, 256, 256)]
                for kk, at, w in mm:
                    last = nc.tensor.matmul(buf[:, at:at + w], k_pad[:, h, kk * P:(kk + 1) * P],
                                            q_stack[:, g, S - w:S], start=True, stop=True)
                last.then_inc(st_written, 1)

            def pv_part(b, g, kk):
                if kk == 0:
                    pe.wait_ge(masked, b * (NG * NB_) + NB_ * (g + 1))
                    pe.wait_ge(vaug_done, b + 1)
                    pe.wait_ge(pv_read, b * NG + g + 1)
                for j in range(G):
                    w = S - kk * P
                    last = nc.tensor.matmul(pv[32 * j:32 * j + 32, kk * P:S], v_aug[:, kk, G * g + j, :],
                                            probs[:, g % 2, j, PT_OFF[kk]:PT_OFF[kk] + w],
                                            start=(kk == 0), stop=True, skip_group_check=True)
                if kk == NT - 1:
                    last.then_inc(pv_written, 1)

            def body(b, last_pass):
                for phase in phases(last_pass):
                    a, bg_, pvg, with_prep, _ = phase
                    if with_prep:
                        prep(b)
                    for kind, k in items(phase):
                        if kind == "A":
                            a_step(b + 1 if a == 0 else b, a, k)
                        elif kind == "mT":
                            misc_free(f"mT{bg_}", b)
                            pe.wait_ge(sa_read, b * (NG * NA) + NA * (bg_ + 1))
                            for i in range(NT):
                                last = nc.tensor.transpose(misc[0:MROW + G, i * P:(i + 1) * P],
                                                           neg_max[:, bg_ % 2, i, :], ident[:, :])
                            last.then_inc(misc_written, 1)
                        elif kind == "B":
                            b_step(b, bg_, k)
                        elif kind == "PV":
                            pv_part(b, pvg, k)
                        elif kind == "V":
                            values(b)
                        elif kind == "OT":
                            misc_free(f"OT{pvg}", b)
                            pe.wait_ge(pv_read, b * NG + pvg + 2)
                            for i in range(NT):
                                last = nc.tensor.transpose(misc[:, i * P:(i + 1) * P], pv_sb[:, i * P:(i + 1) * P],
                                                           ident[:, :])
                            last.then_inc(misc_written, 1)
                        elif kind == "RT":
                            misc_free("RT", b)
                            pe.wait_ge(om_done, (b + 1) * NG)
                            for h in range(HD):
                                last = nc.tensor.matmul(misc[:, h * (P // 2):(h + 1) * (P // 2)],
                                                        o_masked[:, h, :, :, :].rearrange("p n i c -> p (n i c)"),
                                                        fold[:, :], start=True, stop=True)
                            last.then_inc(misc_written, 1)
                        elif kind == "R2":
                            misc_free("R2", b)
                            for i in range(NT):
                                last = nc.tensor.transpose(misc[:, i * P:(i + 1) * P], attn_T[:, i * P:(i + 1) * P],
                                                           ident[:, :])
                            last.then_inc(misc_written, 1)
                        elif kind == "XT":
                            misc_free("XT", b)
                            pe.wait_ge(ln2_done, b + 1)
                            for i in range(NT):
                                last = nc.tensor.transpose(misc[:, i * P:(i + 1) * P], xn2[:, i, :], ident[:, :])
                            last.then_inc(misc_written, 1)
                        elif kind == "LG":
                            misc_free("LG", b)
                            for i in range(NT):
                                last = nc.tensor.matmul(misc[:, i * E:(i + 1) * E], xn2T[:, i * P:(i + 1) * P],
                                                        wr_sb[:, :], start=True, stop=True)
                            last.then_inc(misc_written, 1)

            nc.tensor.matmul(st[:, 1, 0:1], wout[:, :], ones_col[:, :], start=True, stop=True).then_inc(vconst, 1)
            prep(-1)
            values(-1)
            pe.wait_ge(consts, 2)
            for s in range(NA):
                a_step(0, 0, s)
            passes(pe, body, BATCHES)

        @block.scalar
        def _(act):
            act.wait_ge(consts, 1)

            def copy_misc(name, b, out_, in_, scale=1.0, extra=None):
                act.wait_ge(misc_written, use(name, b))
                ins = nc.scalar.activation(out_, in_, ACT.Copy, scale=scale)
                ins.then_inc(misc_read, 1)
                return ins

            def hi_part(name, b, out_, scale):
                act.wait_ge(misc_written, use(name, b))
                nc.scalar.activation(out_, misc[:, :], ACT.Copy, scale=scale).then_inc(hi_done, 1)

            def prep(b):
                copy_misc("xnT", b, xnT[:, :], misc[:, :])
                for c in range(NG):
                    if not (isinstance(b, int) and b < 0):
                        act.wait_ge(q_stacked[c], 16 * (TERMS + 1) * (b + 1))
                        act.wait_ge(k_stacked[c], 16 * TERMS * (b + 1))
                hi_part("Q", b, q_hi[:, :], SCALE)
                hi_part("K", b, k_hi[:, :], 1.0)

            def values(b):
                act.wait_ge(misc_written, use("V", b))
                if not (isinstance(b, int) and b < 0):
                    act.wait_ge(pv_written, (b + 1) * NG)
                nc.scalar.activation(v_aug[:, :, :, 0:HD],
                                     misc[:, :].rearrange("p (i n h) -> p i n h", i=NT, h=HD),
                                     ACT.Copy).then_inc(vaug_done, 1)
                act.wait_ge(vaug_done, b + 2)
                act.sem_inc(misc_read, 1)

            act.sem_inc(pv_read, 1)
            act.sem_inc(x1_done, 1)
            act.sem_inc(x1_stored, 1)
            act.sem_inc(xn2_stored, 1)
            prep(-1)
            values(-1)

            def body(b, last_pass):
                for phase in phases(last_pass):
                    a, bg_, pvg, with_prep, _ = phase
                    if with_prep:
                        prep(b)
                    for kind, k in items(phase):
                        if kind == "mT":
                            act.wait_ge(misc_written, use(f"mT{bg_}", b))
                            nc.scalar.activation(q_stack[MROW:MROW + G, bg_, :], misc[MROW:MROW + G, :],
                                                 ACT.Copy).then_inc(act_sb, 1)
                            act.wait_ge(act_sb, b * NG + bg_ + 1)
                            act.sem_inc(misc_read, 1)
                        elif kind == "B":
                            j, part = k // 3, k % 3
                            n = b * (NG * NB_) + NB_ * bg_ + k + 1
                            act.wait_ge(st_written, n)
                            if k == 0 and bg_ >= 2:
                                act.wait_ge(pv_written, b * NG + bg_ - 1)
                            lo, w, at = ((0, 512, 0), (512, 384, 0), (896, 384, 128))[part]
                            nc.scalar.activation(probs[:, bg_ % 2, j, lo:lo + w], st[:, k % 2, at:at + w],
                                                 ACT.Exp).then_inc(exp_done, 1)
                        elif kind == "PV" and k == NT - 1:
                            act.wait_ge(pv_written, b * NG + pvg + 1)
                            if pvg > 0:
                                act.wait_ge(misc_written, use(f"OT{pvg - 1}", b))
                            nc.scalar.activation(pv_sb[:, :], pv[:, :], ACT.Copy).then_inc(pv_read, 1)
                        elif kind == "V":
                            values(b)
                        elif kind == "RT":
                            act.wait_ge(misc_written, use("RT", b))
                            nc.scalar.activation(attn_T[:, :].rearrange("p (r h) -> p h r", h=HD),
                                                 misc[:, :].rearrange("p (h r) -> p h r", h=HD),
                                                 ACT.Copy, scale=wsum[:, 0:1]).then_inc(misc_read, 1)
                        elif kind == "XT":
                            copy_misc("XT", b, xn2T[:, :], misc[:, :])

            passes(act, body, BATCHES)

        @block.vector
        def _(dve):
            dve.wait_ge(consts, 1)
            dve.wait_ge(vconst, 1)
            nc.vector.tensor_copy(wsum[:, :], st[:, 1, 0:1]).then_inc(consts, 1)

            BEFORE, PER_PASS = 2, 2 + NG + 2
            done = [0]

            def link(ins, b, apart=False):
                done[0] += 1
                ins.then_inc(dve_chain, 1)
                if isinstance(b, int) and b < 0:
                    dve.wait_ge(dve_chain, done[0])
                elif apart:
                    wait_apart(dve, dve_chain, b * PER_PASS + (BEFORE + done[0]))
                else:
                    dve.wait_ge(dve_chain, b * PER_PASS + (BEFORE + done[0]))

            def layernorm(src, dst, st_, mv_, rs_, b, var_done, rstd_done, batch, ready):
                for i in range(NT):
                    last = nc.vector.bn_stats(st_[:, i, :], src[:, i, :])
                link(last, b, apart=True)
                for i in range(NT):
                    last = nc.vector.bn_aggr(mv_[:, i, :], st_[:, i, :])
                link(last, b)
                nc.vector.tensor_scalar(rs_[:, :], mv_[:, :, 1], LN_EPS, None, ALU.add).then_inc(var_done, 1)
                dve.wait_ge(rstd_done, batch + 1)
                for i in range(NT):
                    last = nc.vector.tensor_scalar(dst[:, i, :], src[:, i, :], mv_[:, i, 0:1], rs_[:, i:i + 1],
                                                   ALU.subtract, ALU.mult)
                last.then_inc(ready, 1)

            def prep(b):
                dve.wait_ge(x_loaded, 16 * (b + 2))
                layernorm(x_in, xn, stats, mv, rstd, b, var1_done, rstd1_done, b + 1, ln1_done)
                for c in range(NG):
                    if not (isinstance(b, int) and b < 0):
                        dve.wait_ge(q_stacked[c], 16 * (TERMS + 1) * (b + 1))
                        dve.wait_ge(k_stacked[c], 16 * TERMS * (b + 1))
                for name, hi, lo, scale, k in (("Q", q_hi, q_lo, SCALE, 1), ("K", k_hi, k_lo, 1.0, 2)):
                    dve.wait_ge(hi_done, 2 * (b + 1) + k)
                    nc.vector.scalar_tensor_tensor(lo[:, :], misc[:, :], scale, hi[:, :].bitcast(F32),
                                                   ALU.mult, ALU.subtract).then_inc(lo_done, 1)
                    dve.wait_ge(lo_done, 2 * (b + 1) + k)
                    dve.sem_inc(misc_read, 1)

            def pad_keys(nb, g, first):
                dve.wait_ge(k_stacked[g], 16 * TERMS * (nb + 1))
                if not first:
                    dve.wait_ge(st_written, (nb - 1) * (NG * NB_) + NB_ * (g + 1))
                for j in range(G):
                    nc.vector.tensor_scalar(k_pad[:, G * g + j, :], k_stack[:, g, :].bitcast(F32), rowmask[:, j:j + 1],
                                       None, ALU.mult).then_inc(kpad_done, 1)

            def reduce_step(nb, g, s):
                i, pair = s // 2, s % 2
                n = nb * (NG * NA) + NA * g + s + 1
                dve.wait_ge(sa_written, n)
                nc.vector.tensor_reduce(neg_max[:, g % 2, i, MROW + 2 * pair:MROW + 2 * pair + 2],
                                        sa[:, s % 2, :, 0:(i + 1) * P], AX.X, ALU.max,
                                        negate=True).then_inc(sa_read, 1)

            prep(-1)
            pad_keys(0, 0, True)
            pad_keys(0, 1, True)
            done[0] = 0
            for s in range(NA):
                reduce_step(0, 0, s)

            def body(b, last_pass):
                done[0] = 0
                k_ = [0]
                for phase in phases(last_pass):
                    a, bg_, pvg, with_prep, _ = phase
                    if with_prep:
                        prep(b)
                    if bg_ in (0, 1):
                        pad_keys(b, bg_ + 2, True)
                    if bg_ == 3 and not last_pass:
                        pad_keys(b + 1, 0, False)
                    if pvg == 3 and not last_pass:
                        pad_keys(b + 1, 1, False)
                    for kind, k in items(phase):
                        if kind == "A":
                            nb = b + 1 if a == 0 else b
                            if k == 0:
                                if a >= 2:
                                    dve.wait_ge(misc_written, use(f"mT{a - 2}", b))
                                elif a == 0:
                                    dve.wait_ge(misc_written, use("mT2", b))
                            reduce_step(nb, a, k)
                        elif kind == "OT":
                            dve.wait_ge(misc_written, use(f"OT{pvg}", b))
                            ot = misc[:, :].rearrange("p (i j c) -> p i j c", i=NT, j=G)
                            link(nc.vector.reciprocal(rden[:, :, :], ot[:, :, :, HD]), b)
                            if pvg == 0 and (not isinstance(b, int) or b > 0):
                                dve.wait_ge(misc_written, use("RT", b - 1))
                            for c in range(2):
                                half = slice(c * (P // 2), (c + 1) * (P // 2))
                                dst = o_masked[half, :, G * pvg:G * pvg + G, :, c].rearrange("p h j i -> p i j h")
                                last = nc.vector.tensor_tensor(
                                    dst, ot[half, :, :, 0:HD],
                                    rden[half, :, :].unsqueeze(3).broadcast_to([P // 2, NT, G, HD]), ALU.mult)
                            last.then_inc(om_done, 1)
                            dve.wait_ge(om_done, b * NG + pvg + 1)
                            dve.sem_inc(misc_read, 1)
                        elif kind == "R2":
                            dve.wait_ge(misc_written, use("R2", b))
                            dve.wait_ge(xres_loaded, 16 * (b + 1))
                            if not isinstance(b, int) or b > 0:
                                dve.wait_ge(x1_stored, 16 * b + 1)
                                dve.wait_ge(xn2_stored, 16 * b + 1)
                            nc.vector.tensor_tensor(x1[:, :, :], misc[:, :].rearrange("p (i d) -> p i d", i=NT),
                                                    x_res[:, :, :], ALU.add).then_inc(x1_done, 1)
                            dve.wait_ge(x1_done, b + 2)
                            dve.sem_inc(misc_read, 1)
                            layernorm(x1, xn2, stats2, mv2, rstd2, b, var2_done, rstd2_done, b, ln2_done)
                        elif kind == "LG":
                            dve.wait_ge(misc_written, use("LG", b))
                            nc.vector.tensor_tensor(logits[:, bass.ds(b * NT, NT), :],
                                                    misc[:, 0:NT * E].rearrange("p (i e) -> p i e", i=NT),
                                                    br_bc[:, :].unsqueeze(1).broadcast_to([P, NT, E]),
                                                    ALU.add).then_inc(logits_done, 1)
                            dve.wait_ge(logits_done, b + 1)
                            dve.sem_inc(misc_read, 1)
                assert last_pass or done[0] == PER_PASS, done

            passes(dve, body, BATCHES)

        attention.close()
        part = ctx
        TT = BATCHES * NT
        NTOK = TT * P
        UNROLL = 8
        TILES = -(-(2 * TT + E - 1) // UNROLL) * UNROLL
        FC = F // P
        BIG = 2.0 * E
        OH = 4

        y2_d = nc.dram_tensor("y2_scratch", (2 * NTOK + TILES * P, D), F32).ap()

        w_hi = [sb(n, [P, E * F], F32R) for n in ("wi_hi", "wg_hi")]
        w_lo = [sb(n, [P, E * F], F32R) for n in ("wi_lo", "wg_lo")]
        wo_sb = sb("wo_sb", [P, E * FC * D])
        stage = sb("stage", [P, 4, F])
        b_all = sb("b_all", [P, F])
        b_rest = sb("b_rest", [P, F])
        b_part = sb("b_part", [P, 3, F], BF16)
        b_stack = sb("b_stack", [P, F], BF16)
        b_sel = sb("b_sel", [P, 3 * E * P], BF16)
        upper = sb("upper", [P, P], BF16)
        onesb = sb("onesb", [P, P], BF16)
        iota_e = sb("iota_e", [P, E])
        iota_p = sb("iota_p", [P, P])
        iota_s = sb("iota_s", [P, TILES])
        iota_t = sb("iota_t", [P, TT])
        value = sb("value", [P, TT, 2])
        slot_id = sb("slot_id", [P, TILES])
        weight = sb("weight", [P, TT, 2])
        row_f = sb("row_f", [P, TT * 2])
        tile_f = sb("tile_f", [P, TT * 2])
        one_r = sb("one_r", [P, OH, P])
        one_s = sb("one_s", [P, OH, TILES])
        table = sb("table", [P, TILES, 2], I32)
        expert = sb("expert", [P, TILES], I32)

        route = part = ExitStack()
        iota_i = sb("iota_i", [P, max(2 * TT, TILES, P)], I32)
        shifted = sb("shifted", [P, TT, E])
        ex = sb("ex", [P, TT, E])
        pr = sb("pr", [P, TT, E])
        pr2 = sb("pr2", [P, TT, E])
        tmp = sb("tmp", [P, TT, E])
        oh = [sb(f"oh{c}", [P, TT, E]) for c in range(2)]
        chosen = sb("chosen", [P, TT, E], BF16)
        mx = sb("mx", [P, TT])
        sm = sb("sm", [P, TT])
        pm = sb("pm", [P, TT, 2])
        first = sb("first", [P, TT])
        tot = sb("tot", [P, E, TT])
        cum = sb("cum", [P, E, TT])
        cmp_ = sb("cmp_", [P, E, TT])
        one_t = sb("one_t", [P, E * TT])
        slot = sb("slot", [P, E, TT])
        count = sb("count", [P, E])
        start = sb("start", [P, E])
        ntile = sb("ntile", [P, E])
        tend = sb("tend", [P, E])
        base = sb("base", [P, E])
        slot2 = sb("slot2", [P, TT, 2])
        slot_i = sb("slot_i", [P, TT, 2], I32)
        part_i = sb("part_i", [P, TT, 2], I32)
        cmp_s = sb("cmp_s", [P, TILES, E])
        exp_f = sb("exp_f", [P, TILES])
        tab_f = sb("tab_f", [P, 3, TILES])
        tab_i = sb("tab_i", [P, TILES], I32)

        counts_ps = pb("counts_ps", [P, 2, TT * E])
        table_ps = pb("table_ps", [P, TILES])

        r_const = sem("r_const")
        r_ready = sem("r_ready")
        stage_loaded = [sem(f"stage_loaded{k}") for k in range(4)]
        w_hi_done = sem("w_hi_done")
        w_lo_done = sem("w_lo_done")
        bias_loaded = sem("bias_loaded")
        ffn_loaded = sem("ffn_loaded")
        bias_done = sem("bias_done")
        r_chain = sem("r_chain")
        shifted_done = sem("shifted_done")
        exp_ready = sem("exp_ready")
        chosen_done = sem("chosen_done")
        counts_done = sem("counts_done")
        onehot_done = sem("onehot_done")
        onehot_used = sem("onehot_used")
        table_done = sem("table_done")
        table_zero = sem("table_zero")

        block = route.enter_context(nc.Block())

        @block.sync
        def _(sp):
            for k in range(2 * E):
                m, e = k // E, k % E
                if k >= 4:
                    sp.wait_ge(w_lo_done, k - 3)
                sp.dma_start(stage[:, k % 4, :], (wi, wg)[m][e, :, :]).then_inc(stage_loaded[k % 4], 16)
                if k == 3:
                    sp.wait_ge(bias_done, 1)
                    for c in range(3):
                        sp.dma_start(b_all[32 * c:32 * c + E, :], bi).then_inc(bias_loaded, 16)
                        sp.dma_start(b_all[32 * c + E:32 * c + 2 * E, :], bg).then_inc(bias_loaded, 16)
                        for m, src in enumerate((bo, gamma, beta)):
                            sp.dma_start(b_all[32 * c + 2 * E:32 * c + 3 * E, m * D:(m + 1) * D], src)\
                                .then_inc(bias_loaded, 16)
            for e in range(E):
                sp.dma_start(wo_sb[:, e * FC * D:(e + 1) * FC * D].rearrange("p (c d) -> p c d", c=FC),
                             wo[e, :, :].rearrange("(c p) d -> p c d", p=P)).then_inc(ffn_loaded, 16)
            sp.wait_ge(ffn_loaded, 16 * E)

        @block.gpsimd
        def _(pool):
            n = 0

            def c_(ins):
                nonlocal n
                n += 1
                ins.then_inc(r_const, 1)
                pool.wait_ge(r_const, n)

            def iota(dst, width, step, base_, mult):
                c_(pool.iota(iota_i[:, 0:width], pattern=[[step, width]], base=base_, channel_multiplier=mult))
                c_(pool.tensor_copy(dst, iota_i[:, 0:width]))

            iota(iota_e[:, :], E, 1, 0, 0)
            c_(pool.memset(upper[:, :], 1.0))
            c_(pool.affine_select(out=upper[:, :], in_=upper[:, :], compare_op=ALU.is_gt, fill=0.0, base=0,
                                  pattern=[[1, P]], channel_multiplier=-1))
            c_(pool.memset(onesb[:, :], 1.0))
            c_(pool.memset(one_t[:, :], 1.0))
            iota(iota_t[:, :], TT, P, 0, 0)
            iota(iota_p[:, :], P, 1, 0, 0)
            iota(iota_s[:, :], TILES, 1, 0, 0)
            c_(pool.iota(iota_i[:, 0:2 * TT], pattern=[[2 * P, TT], [1, 2]], base=1, channel_multiplier=2))
            c_(pool.tensor_copy(value[:, :, :].rearrange("p t c -> p (t c)"), iota_i[:, 0:2 * TT]))
            iota(slot_id[:, :], TILES, P, 2 * NTOK + 1, 1)
            c_(pool.memset(b_sel[:, :], 0.0))
            for c in range(3):
                rows = b_sel[32 * c:32 * c + 32, :].rearrange("r (m q) -> r m q", q=P)
                c_(pool.affine_select(out=rows, in_=rows, compare_op=ALU.not_equal, fill=1.0, base=0,
                                      pattern=[[-1, 3 * E], [0, P]], channel_multiplier=1))
            c_(pool.memset(b_stack[:, :], 0.0))
            pool.memset(iota_i[:, 0:1], 0).then_inc(r_ready, 1)

        @block.scalar
        def _(act):
            act.wait_ge(shifted_done, 1)
            nc.scalar.activation(ex[:, :, :], shifted[:, :, :], ACT.Exp).then_inc(exp_ready, 1)
            for k in range(2 * E):
                m, e = k // E, k % E
                act.wait_ge(stage_loaded[k % 4], 16 * (k // 4 + 1))
                nc.scalar.activation(w_hi[m][:, e * F:(e + 1) * F], stage[:, k % 4, :],
                                     ACT.Copy).then_inc(w_hi_done, 1)

        @block.tensor
        def _(pe):
            pe.wait_ge(r_ready, 1)
            pe.wait_ge(chosen_done, 1)
            rhs = chosen[:, :, :].rearrange("p t e -> p (t e)")
            nc.tensor.matmul(counts_ps[:, 0, :], upper[:, :], rhs, start=True, stop=True)
            nc.tensor.matmul(counts_ps[:, 1, :], onesb[:, :], rhs, start=True, stop=True).then_inc(counts_done, 1)
            pe.wait_ge(table_zero, 1)
            for c in range(OH):
                nc.tensor.matmul(table_ps[:, :], one_r[:, 0, :], one_s[:, 0, :], start=(c == 0), stop=True,
                                 skip_group_check=True).then_inc(onehot_used, 1)
            with pe.Fori(0, 2 * TT // OH) as t:
                for c in range(OH):
                    pe.wait_ge(onehot_done, OH * t + (c + 1))
                    nc.tensor.matmul(table_ps[:, :], one_r[:, c, :], one_s[:, c, :], start=False, stop=True,
                                     skip_group_check=True).then_inc(onehot_used, 1)

        @block.vector
        def _(dve):
            V = nc.vector
            n = 0

            def link(ins):
                nonlocal n
                n += 1
                ins.then_inc(r_chain, 1)
                dve.wait_ge(r_chain, n)

            def low_part(k):
                m, e = k // E, k % E
                dve.wait_ge(w_hi_done, k + 1)
                V.tensor_tensor(w_lo[m][:, e * F:(e + 1) * F], stage[:, k % 4, :],
                                w_hi[m][:, e * F:(e + 1) * F].bitcast(F32), ALU.subtract).then_inc(w_lo_done, 1)

            def over_e(ap):
                return ap.unsqueeze(2).broadcast_to([P, TT, E])

            ie = iota_e[:, :].unsqueeze(1).broadcast_to([P, TT, E])
            V.memset(b_all[:, :], 0.0).then_inc(bias_done, 1)
            link(V.tensor_reduce(mx[:, :], logits[:, :, :], AX.X, ALU.max))
            V.tensor_tensor(shifted[:, :, :], logits[:, :, :], over_e(mx[:, :]), ALU.subtract).then_inc(shifted_done, 1)
            dve.wait_ge(r_ready, 1)
            dve.wait_ge(exp_ready, 1)
            link(V.tensor_reduce(sm[:, :], ex[:, :, :], AX.X, ALU.add))
            link(V.reciprocal(sm[:, :], sm[:, :]))
            link(V.tensor_tensor(pr[:, :, :], ex[:, :, :], over_e(sm[:, :]), ALU.mult))
            src = pr
            for c in range(2):
                link(V.tensor_reduce(pm[:, :, c], src[:, :, :], AX.X, ALU.max))
                link(V.tensor_tensor(tmp[:, :, :], src[:, :, :], over_e(pm[:, :, c]), ALU.is_lt))
                link(V.scalar_tensor_tensor(tmp[:, :, :], tmp[:, :, :], BIG, ie, ALU.mult, ALU.add))
                link(V.tensor_reduce(first[:, :], tmp[:, :, :], AX.X, ALU.min))
                link(V.tensor_tensor(oh[c][:, :, :], ie, over_e(first[:, :]), ALU.is_equal))
                if c == 0:
                    link(V.scalar_tensor_tensor(pr2[:, :, :], oh[0][:, :, :], -2.0, pr[:, :, :], ALU.mult, ALU.add))
                    src = pr2
            V.tensor_tensor(chosen[:, :, :], oh[0][:, :, :], oh[1][:, :, :], ALU.add).then_inc(chosen_done, 1)
            link(V.tensor_tensor(sm[:, :], pm[:, :, 0], pm[:, :, 1], ALU.add))
            link(V.reciprocal(sm[:, :], sm[:, :]))
            V.tensor_tensor(weight[:, :, :], pm[:, :, :], sm[:, :].unsqueeze(2).broadcast_to([P, TT, 2]), ALU.mult)
            dve.wait_ge(counts_done, 1)
            within = counts_ps[:, 0, :].rearrange("p (t e) -> p e t", e=E)
            total = counts_ps[:, 1, :].rearrange("p (t e) -> p e t", e=E)
            link(V.tensor_copy(tot[:, :, :], total))
            flat = "p e t -> p (e t)"
            link(V.tensor_tensor_scan(cum[:, :, :].rearrange(flat), one_t[:, :], tot[:, :, :].rearrange(flat), 0.0,
                                      ALU.mult, ALU.add))
            link(V.memset(start[:, 0:1], 0.0))
            link(V.tensor_copy(start[:, 1:E], cum[:, 0:E - 1, TT - 1]))
            link(V.tensor_tensor(count[:, :], cum[:, :, TT - 1], start[:, :], ALU.subtract))
            link(V.tensor_tensor(cmp_[:, :, :], count[:, :].unsqueeze(2).broadcast_to([P, E, TT]),
                                 iota_t[:, :].unsqueeze(1).broadcast_to([P, E, TT]), ALU.is_gt))
            link(V.tensor_reduce(ntile[:, :], cmp_[:, :, :], AX.X, ALU.add))
            link(V.tensor_tensor_scan(tend[:, :], one_t[:, 0:E], ntile[:, :], 0.0, ALU.mult, ALU.add))
            link(V.tensor_tensor(base[:, :], tend[:, :], ntile[:, :], ALU.subtract))
            link(V.scalar_tensor_tensor(base[:, :], base[:, :], float(P), start[:, :], ALU.mult, ALU.subtract))
            link(V.tensor_tensor(slot[:, :, :], cum[:, :, :], tot[:, :, :], ALU.subtract))
            link(V.tensor_tensor(slot[:, :, :], slot[:, :, :], base[:, :].unsqueeze(2).broadcast_to([P, E, TT]),
                                 ALU.add))
            link(V.tensor_tensor(slot[:, :, :], slot[:, :, :], within, ALU.add))
            for c in range(2):
                link(V.tensor_tensor(tmp[:, :, :], oh[c][:, :, :], slot[:, :, :].rearrange("p e t -> p t e"), ALU.mult))
                link(V.tensor_reduce(slot2[:, :, c], tmp[:, :, :], AX.X, ALU.add))
            link(V.tensor_copy(slot_i[:, :, :], slot2[:, :, :]))
            link(V.tensor_single_scalar(part_i[:, :, :], slot_i[:, :, :], P - 1, ALU.bitwise_and))
            link(V.tensor_copy(row_f[:, :], part_i[:, :, :].rearrange("p t c -> p (t c)")))
            link(V.tensor_single_scalar(part_i[:, :, :], slot_i[:, :, :], P.bit_length() - 1, ALU.logical_shift_right))
            link(V.tensor_copy(tile_f[:, :], part_i[:, :, :].rearrange("p t c -> p (t c)")))
            link(V.tensor_tensor(cmp_s[:, :, :], iota_s[:, :].unsqueeze(2).broadcast_to([P, TILES, E]),
                                 tend[:, :].unsqueeze(1).broadcast_to([P, TILES, E]), ALU.is_ge))
            link(V.tensor_reduce(exp_f[:, :], cmp_s[:, :, :], AX.X, ALU.add))
            link(V.tensor_scalar(exp_f[:, :], exp_f[:, :], float(E - 1), None, ALU.min))
            link(V.tensor_copy(expert[:, :], exp_f[:, :]))
            link(V.memset(one_r[:, 0, :], 0.0))
            V.memset(one_s[:, 0, :], 0.0).then_inc(table_zero, 1)

            vals = value[:, :, :].rearrange("p t c -> p (t c)")
            dve.wait_ge(onehot_used, OH)
            with dve.Fori(0, 2 * TT // OH) as t:
                for c in range(OH):
                    dve.wait_ge(onehot_used, OH * t + c + 1)
                    V.tensor_scalar(one_r[:, c, :], iota_p[:, :], row_f[:, bass.ds(OH * t + c, 1)], None,
                                    ALU.is_equal)
                    V.tensor_scalar(one_s[:, c, :], iota_s[:, :], tile_f[:, bass.ds(OH * t + c, 1)],
                                    vals[:, bass.ds(OH * t + c, 1)], ALU.is_equal, ALU.mult).then_inc(onehot_done, 1)
            for k in range(2 * E):
                low_part(k)
            dve.wait_ge(bias_loaded, 16 * 15)
            link(V.tensor_copy(b_part[:, 0, :], b_all[:, :]))
            link(V.tensor_tensor(b_rest[:, :], b_all[:, :], b_part[:, 0, :], ALU.subtract))
            link(V.tensor_copy(b_part[:, 1, :], b_rest[:, :]))
            link(V.tensor_tensor(b_all[:, :], b_rest[:, :], b_part[:, 1, :], ALU.subtract))
            link(V.tensor_copy(b_part[:, 2, :], b_all[:, :]))
            for c in range(3):
                V.tensor_copy(b_stack[32 * c:32 * c + 3 * E, :], b_part[32 * c:32 * c + 3 * E, c, :])

            dve.wait_ge(onehot_used, 2 * TT + OH)
            link(V.tensor_copy(tab_f[:, 0, :], table_ps[:, :]))
            link(V.tensor_scalar(tab_f[:, 1, :], tab_f[:, 0, :], 0.5, None, ALU.is_lt))
            link(V.tensor_tensor(tab_f[:, 1, :], tab_f[:, 1, :], slot_id[:, :], ALU.mult))
            link(V.tensor_scalar(tab_f[:, 0, :], tab_f[:, 0, :], 1.0, None, ALU.subtract))
            link(V.tensor_tensor(tab_f[:, 1, :], tab_f[:, 0, :], tab_f[:, 1, :], ALU.add))
            link(V.tensor_copy(table[:, :, 1], tab_f[:, 1, :]))
            link(V.tensor_scalar(tab_f[:, 2, :], tab_f[:, 0, :], 0.0, None, ALU.max))
            link(V.tensor_copy(tab_i[:, :], tab_f[:, 2, :]))
            V.tensor_single_scalar(table[:, :, 0], tab_i[:, :], 1, ALU.logical_shift_right).then_inc(table_done, 1)
            dve.wait_ge(table_done, 1)

        route.close()
        part = ctx

        NX, NR = 8, 4
        from_row = sb("from_row", [P, NX], I32)
        to_row = sb("to_row", [P, NR], I32)
        xg = sb("xg", [P, NX, D])
        xg_hi = sb("xg_hi", [P, 2, P], F32R)
        xg_lo = sb("xg_lo", [P, 2, P], F32R)
        gelu = sb("gelu", [P, 2, F])
        gate = sb("gate", [P, 2, F])
        hid = sb("hid", [P, 2, F])
        hidT = sb("hidT", [P, 2, F])
        res = sb("res", [P, NR, D])
        st6 = sb("st6", [P, 2, 6])
        mean_var = sb("mean_var", [P, NR, 2])
        inv_dev = sb("inv_dev", [P, NR])
        z = sb("z", [P, NR, D])
        y1 = sb("y1", [P, 2, NT, D])
        y2 = sb("y2", [P, 2, NT, 2 * D])
        acc = sb("acc", [P, 2, NT, D])

        up_i = pb("up_i", [P, 2, F])
        up_g = pb("up_g", [P, 2, F])
        ht_ps = pb("ht_ps", [P, F])
        y_ps = pb("y_ps", [P, D])
        xt_ps = pb("xt_ps", [P, P])
        gb_ps = pb("gb_ps", [P, 2 * D])

        idx_done = sem("idx_done")
        gathered = [sem(f"gathered{u}") for u in range(NX)]
        scattered = [sem(f"scattered{u}") for u in range(NR)]
        xt_written, xhi_done, xlo_done = sem("xt_written"), sem("xhi_done"), sem("xlo_done")
        up_written, gelu_done, gate_done = sem("up_written"), sem("gelu_done"), sem("gate_done")
        hid_done, ht_written, hidT_done = sem("hid_done"), sem("ht_written"), sem("hidT_done")
        y_written, res_done, ve_done, dev_done = sem("y_written"), sem("res_done"), sem("ve_done"), sem("dev_done")
        gb_written = sem("gb_written")
        z_done, x_chain, z_chain = sem("z_done"), sem("x_chain"), sem("z_chain")
        comb_loaded = [sem(f"comb_loaded{u}") for u in range(2)]
        comb_done, c_chain, out_stored = sem("comb_done"), sem("c_chain"), [sem(f"out_stored{u}") for u in range(2)]

        experts = ExitStack()
        block = experts.enter_context(nc.Block())

        def rounds(s, u, n):
            return 16 * (s // n + 1) if isinstance(s, int) else (s - u % n) * (16 // n) + 16

        def stages(eng, stage_fns):
            most = max(lag for lag, _ in stage_fns)

            def step(s, u):
                for lag, fn in stage_fns:
                    if isinstance(s, int) and not 0 <= s - lag < TILES:
                        continue
                    fn(s - lag, (u - lag) % UNROLL)

            least = min(lag for lag, _ in stage_fns)
            for u in range(least, UNROLL):
                step(u, u % UNROLL)
            peel_last = least < 0
            full = TILES // UNROLL - (1 if peel_last else 0)
            if full > 1:
                with eng.Fori(1, full) as k:
                    for u in range(UNROLL):
                        step(k * UNROLL + u, u)
            for s in range(max(full, 1) * UNROLL, TILES + most):
                step(s, s % UNROLL)

        @block.gpsimd
        def _(pool):
            def gather(s, u):
                wait_apart(pool, idx_done, s + 1)
                pool.indirect_dma_start(xg[:, u, :], None, xn2_d[0:NTOK, :],
                                        bass.IndirectOffsetOnAxis(from_row[:, u:u + 1], 0)).then_inc(gathered[u], 16)

            def deviation(s, u):
                pool.wait_ge(ve_done, s + 1)
                r = u % NR
                pool.tensor_tensor(inv_dev[:, r:r + 1], inv_dev[:, r:r + 1], minus_half[:, 0:1],
                                   ALU.pow).then_inc(dev_done, 1)

            def scatter(s, u):
                wait_apart(pool, z_done, s + 1)
                pool.indirect_dma_start(y2_d, bass.IndirectOffsetOnAxis(to_row[:, u % NR:u % NR + 1], 0), z[:, u % NR, :], None)\
                    .then_inc(scattered[u % NR], 16)

            stages(pool, [(3, deviation), (4, scatter), (-3, gather)])
            for r in range(NR):
                pool.wait_ge(scattered[r], 16 * (TILES // NR))

        @block.tensor
        def _(pe):
            def transpose_x(s, u):
                pe.wait_ge(gathered[u], rounds(s, u, NX))
                if not (isinstance(s, int) and s < 1):
                    pe.wait_ge(xlo_done, s)
                nc.tensor.transpose(xt_ps[:, :], xg[:, u, :], ident[:, :]).then_inc(xt_written, 1)

            e_reg = [pe.alloc_register(f"expert_of_tile{u}") for u in range(UNROLL)]

            def load_expert(s, u):
                pe.reg_load(e_reg[u], expert[0:1, bass.ds(s, 1)])

            def expert_of(u):
                return pe.snap(e_reg[u], min_val=0, max_val=E - 1)

            def up(s, u):
                b2 = u % 2
                if isinstance(s, int) and s == 0:
                    load_expert(s, u)
                e = expert_of(u)
                pe.wait_ge(xlo_done, s + 1)
                pe.wait_ge(xhi_done, s + 1)
                if not (isinstance(s, int) and s < 2):
                    pe.wait_ge(gate_done, s - 1)
                for m, dst in ((0, up_i), (1, up_g)):
                    nc.tensor.matmul(dst[:, b2, :], b_sel[:, bass.ds(e * P + m * E * P, P)], b_stack[:, :],
                                     start=True, stop=False)
                    hi = w_hi[m][:, bass.ds(e * F, F)]
                    lo = w_lo[m][:, bass.ds(e * F, F)]
                    nc.tensor.matmul(dst[:, b2, :], xg_hi[:, b2, :], lo, start=False, stop=False)
                    nc.tensor.matmul(dst[:, b2, :], xg_lo[:, b2, :], hi, start=False, stop=False)
                    last = nc.tensor.matmul(dst[:, b2, :], xg_hi[:, b2, :], hi, start=False, stop=True)
                last.then_inc(up_written, 1)

            def down(s, u):
                e = expert_of(u)
                pe.wait_ge(hidT_done, s + 1)
                if not (isinstance(s, int) and s < 1):
                    pe.wait_ge(res_done, s)
                nc.tensor.matmul(y_ps[:, :], b_sel[:, bass.ds(e * P + 2 * E * P, P)], b_stack[:, 0:D],
                                 start=True, stop=False)
                for c in range(FC):
                    last = nc.tensor.matmul(y_ps[:, :], hidT[:, u % 2, c * P:(c + 1) * P],
                                            wo_sb[:, bass.ds(e * (FC * D) + c * D, D)],
                                            start=False, stop=(c == FC - 1))
                last.then_inc(y_written, 1)

            def gamma_beta(s, u):
                e = expert_of(u)
                if not (isinstance(s, int) and s < 1):
                    pe.wait_ge(z_done, s)
                nc.tensor.matmul(gb_ps[:, :], b_sel[:, bass.ds(e * P + 2 * E * P, P)], b_stack[:, D:3 * D],
                                 start=True, stop=True).then_inc(gb_written, 1)

            def transpose_h(s, u):
                pe.wait_ge(hid_done, s + 1)
                if not (isinstance(s, int) and s < 1):
                    pe.wait_ge(hidT_done, s)
                for c in range(FC):
                    last = nc.tensor.transpose(ht_ps[:, c * P:(c + 1) * P], hid[:, u % 2, c * P:(c + 1) * P],
                                               ident[:, :])
                last.then_inc(ht_written, 1)

            stages(pe, [(0, up), (-1, load_expert), (2, down), (1, transpose_h), (-2, transpose_x),
                        (3, gamma_beta)])

        @block.scalar
        def _(act):
            def activations(s, u):
                act.wait_ge(up_written, s + 1)
                if not (isinstance(s, int) and s < 2):
                    act.wait_ge(hid_done, s - 1)
                nc.scalar.activation(gelu[:, u % 2, :], up_i[:, u % 2, :], ACT.Gelu).then_inc(gelu_done, 1)
                nc.scalar.activation(gate[:, u % 2, :], up_g[:, u % 2, :], ACT.Tanh, scale=0.5)\
                    .then_inc(gate_done, 1)

            def evacuate_h(s, u):
                act.wait_ge(ht_written, s + 1)
                if not (isinstance(s, int) and s < 2):
                    act.wait_ge(y_written, s - 1)
                nc.scalar.activation(hidT[:, u % 2, :], ht_ps[:, :], ACT.Copy, scale=0.5).then_inc(hidT_done, 1)

            def high_x(s, u):
                act.wait_ge(xt_written, s + 1)
                if not (isinstance(s, int) and s < 2):
                    act.wait_ge(up_written, s - 1)
                nc.scalar.activation(xg_hi[:, u % 2, :], xt_ps[:, :], ACT.Copy).then_inc(xhi_done, 1)

            stages(act, [(0, activations), (1, evacuate_h), (-2, high_x)])

        @block.vector
        def _(dve):
            V = nc.vector

            def product(s, u):
                dve.wait_ge(gelu_done, s + 1)
                dve.wait_ge(gate_done, s + 1)
                if not (isinstance(s, int) and s < 2):
                    dve.wait_ge(ht_written, s - 1)
                V.scalar_tensor_tensor(hid[:, u % 2, :], gate[:, u % 2, :], 1.0, gelu[:, u % 2, :], ALU.add,
                                       ALU.mult).then_inc(hid_done, 1)

            def low_x(s, u):
                dve.wait_ge(xhi_done, s + 1)
                if not (isinstance(s, int) and s < 2):
                    dve.wait_ge(up_written, s - 1)
                V.tensor_tensor(xg_lo[:, u % 2, :], xt_ps[:, :], xg_hi[:, u % 2, :].bitcast(F32),
                                ALU.subtract).then_inc(xlo_done, 1)

            def take_rows(s, u):
                V.tensor_copy(from_row[:, u:u + 1], table[:, bass.ds(s, 1), 0]).then_inc(idx_done, 1)

            def residual(s, u):
                dve.wait_ge(gathered[u], rounds(s, u, NX))
                dve.wait_ge(y_written, s + 1)
                V.tensor_tensor(res[:, u % NR, :], y_ps[:, :], xg[:, u, :], ALU.add).then_inc(res_done, 1)

            def statistics(s, u):
                dve.wait_ge(res_done, s + 1)
                V.bn_stats(st6[:, u % 2, :], res[:, u % NR, :]).then_inc(x_chain, 1)

            def mean_and_variance(s, u):
                wait_apart(dve, x_chain, 2 * s + 1)
                V.bn_aggr(mean_var[:, u % NR, :], st6[:, u % 2, :]).then_inc(x_chain, 1)

            def add_epsilon(s, u):
                dve.wait_ge(x_chain, 2 * s + 2)
                V.tensor_scalar(inv_dev[:, u % NR:u % NR + 1], mean_var[:, u % NR, 1:2], EXPERT_EPS, None, ALU.add)\
                    .then_inc(ve_done, 1)

            def scale(s, u):
                r = u % NR
                if not (isinstance(s, int) and s < NR):
                    dve.wait_ge(scattered[r], rounds(s, u, NR) - 16)
                V.tensor_copy(to_row[:, r:r + 1], table[:, bass.ds(s, 1), 1])
                dve.wait_ge(gb_written, s + 1)
                V.scalar_tensor_tensor(z[:, r, :], res[:, r, :], mean_var[:, r, 0:1], gb_ps[:, 0:D], ALU.subtract,
                                       ALU.mult).then_inc(z_chain, 1)

            def shift(s, u):
                r = u % NR
                dve.wait_ge(z_chain, s + 1)
                dve.wait_ge(dev_done, s + 1)
                V.scalar_tensor_tensor(z[:, r, :], z[:, r, :], inv_dev[:, r:r + 1], gb_ps[:, D:2 * D], ALU.mult,
                                       ALU.add).then_inc(z_done, 1)

            stages(dve, [(4, scale), (-4, take_rows), (3, mean_and_variance), (4, shift), (3, add_epsilon),
                         (0, product), (2, residual), (-2, low_x), (2, statistics)])

        experts.close()
        block2 = ctx.enter_context(nc.Block())
        GROUPS = TT // NT

        @block2.sync
        def _(sp):
            x1_v = x1_d.rearrange("(g i p) d -> g p i d", p=P, i=NT)
            y2_v = y2_d[0:2 * NTOK, :].rearrange("(g i p c) d -> g p i (c d)", p=P, i=NT, c=2)

            def load(g, u):
                sp.dma_start(y1[:, u, :, :], x1_v[g, :, :, :]).then_inc(comb_loaded[u], 16)
                sp.dma_start(y2[:, u, :, :], y2_v[g, :, :, :]).then_inc(comb_loaded[u], 16)

            out_v = out.rearrange("b (i p) d -> b p i d", p=P)

            def store(g, u):
                sp.wait_ge(comb_done, g + 1)
                sp.dma_start(out_v[g, :, :, :], acc[:, u, :, :]).then_inc(out_stored[u], 16)

            for u in range(2):
                load(u, u)
            for g in range(GROUPS):
                store(g, g % 2)
                if g + 2 < GROUPS:
                    load(g + 2, g % 2)
            for u in range(2):
                sp.wait_ge(out_stored[u], 16 * (GROUPS // 2))

        @block2.vector
        def _(dve):
            V = nc.vector
            for g in range(GROUPS):
                u = g % 2
                dve.wait_ge(comb_loaded[u], 32 * (g // 2 + 1))
                if g >= 2:
                    dve.wait_ge(out_stored[u], 16 * (g // 2))
                for i in range(NT):
                    t = g * NT + i
                    last = V.scalar_tensor_tensor(acc[:, u, i, :], y2[:, u, i, 0:D], weight[:, t, 0:1],
                                                  y1[:, u, i, :], ALU.mult, ALU.add)
                last.then_inc(c_chain, 1)
                dve.wait_ge(c_chain, g + 1)
                for i in range(NT):
                    t = g * NT + i
                    last = V.scalar_tensor_tensor(acc[:, u, i, :], y2[:, u, i, D:2 * D], weight[:, t, 1:2],
                                                  acc[:, u, i, :], ALU.mult, ALU.add)
                last.then_inc(comb_done, 1)


_INS = ["L0_attn_x", "L0_attn_W_qkv", "L0_attn_W_out", "L0_ffn_Wr", "L0_ffn_br", "L0_ffn_Wi", "L0_ffn_bi",
        "L0_ffn_Wg", "L0_ffn_bg", "L0_ffn_Wo", "L0_ffn_bo", "L0_ffn_gamma", "L0_ffn_beta"]


def kernel(**inputs):
    import numpy as _np
    import concourse.bacc as _bacc
    from concourse import mybir as _mybir
    from concourse.bass_utils import run_bass_kernel_spmd as _run

    nc = _bacc.Bacc("TRN2", target_bir_lowering=False, num_devices=1)
    arrays, args = {}, []
    for name in _INS:
        a = _np.ascontiguousarray(inputs[name])
        arrays[name] = a
        args.append(nc.dram_tensor(name, a.shape, _mybir.dt.from_np(a.dtype), kind="ExternalInput").ap())
    shape = arrays["L0_attn_x"].shape
    out = nc.dram_tensor("out", shape, _mybir.dt.float32, kind="ExternalOutput").ap()
    attention_and_routed_experts(nc, *args, out)
    r = _run(nc, [arrays], core_ids=[0])
    return r.results[0]["out"]
```

```python
import concourse.bass as bass
from concourse import mybir
from contextlib import ExitStack


def attention_and_routed_experts(nc, x, w_qkv, w_out, wr, br, wi, bi, wg, bg, wo, bo, gamma, beta, out,
                                 BATCHES=16):
    F32, F32R, BF16, I32 = mybir.dt.float32, mybir.dt.float32r, mybir.dt.bfloat16, mybir.dt.int32
    ALU, ACT, AX = mybir.AluOpType, mybir.ActivationFunctionType, mybir.AxisListType

    B, S, D = x.shape
    NH, _, HD3 = w_qkv.shape
    HD = HD3 // 3
    E, _, F = wi.shape
    P = 128
    NT = S // P
    G = 4
    NG = NH // G
    TERMS = 3
    MROW = TERMS * G * HD
    SCALE = float(HD) ** -0.5
    LN_EPS, EXPERT_EPS = 1e-5, 1e-12
    MASK = -1e10

    ctx = ExitStack()
    with ctx:
        part = ctx

        def sb(name, shape, dt=F32):
            return part.enter_context(nc.sbuf_tensor(name, shape, dt))

        def pb(name, shape, dt=F32):
            return part.enter_context(nc.psum_tensor(name, shape, dt))

        def sem(name):
            return ctx.enter_context(nc.semaphore(name))

        xn2_d = nc.dram_tensor("xn2_scratch", (BATCHES * S, D), F32).ap()

        ident = sb("ident", [P, P])
        identb = sb("identb", [P, P], BF16)
        maskneg = sb("maskneg", [P, P], BF16)
        fold = sb("fold", [P, P // 2])
        ones_col = sb("ones_col", [P, 1])
        rowmask = sb("rowmask", [P, G])
        rowsel = sb("rowsel", [P, P])
        wq = sb("wq", [P, P])
        wk = sb("wk", [P, P])
        wv = sb("wv", [P, P])
        wout = sb("wout", [P, D])
        wsum = sb("wsum", [P, 1])
        zeros = sb("zeros", [P, S])
        minus_half = sb("minus_half", [P, 2 * NT])
        wr_sb = sb("wr_sb", [P, E])
        br_bc = sb("br_bc", [P, E])

        logits_all = sb("logits", [P, (1 + BATCHES) * NT, E])
        x_all = sb("x_all", [P, BATCHES * NT, D])

        part = attention = ExitStack()
        stats = sb("stats", [P, NT, 6])
        mv = sb("mv", [P, NT, 2])
        rstd = sb("rstd", [P, NT])
        xn = sb("xn", [P, NT, D])
        xnT = sb("xnT", [P, S])
        q_hi = sb("q_hi", [P, S], F32R)
        q_lo = sb("q_lo", [P, S], F32R)
        k_hi = sb("k_hi", [P, S], F32R)
        k_lo = sb("k_lo", [P, S], F32R)
        q_stack = sb("q_stack", [P, NG, S], F32R)
        k_stack = sb("k_stack", [P, NG, S], F32R)
        k_pad = sb("k_pad", [P, NH, S], F32R)
        v_aug = sb("v_aug", [P, NT, NH, 32])
        neg_max = sb("neg_max", [P, 2, NT, MROW + G])
        PT_OFF = [0, 512, 1024, 896]
        PT_COLS = 1280
        probs = sb("probs", [P, 2, G, PT_COLS])
        pv_sb = sb("pv_sb", [P, S])
        rden = sb("rden", [P, NT, G])
        o_masked = sb("o_masked", [P, HD, NH, NT, 2])
        attn_T = sb("attn_T", [P, S])
        stats2 = sb("stats2", [P, NT, 6])
        mv2 = sb("mv2", [P, NT, 2])
        rstd2 = sb("rstd2", [P, NT])
        xn2 = sb("xn2", [P, NT, D])
        xn2T = sb("xn2T", [P, S])
        sa = pb("sa", [P, 2, 2, S])
        st = pb("st", [P, 2, S])
        pv = pb("pv", [P, S])
        misc = pb("misc", [P, S])

        w_loaded = sem("w_loaded")
        const_a = sem("const_a")
        consts = sem("consts")
        vconst = sem("vconst")
        x_first = sem("x_first")
        x_rest = sem("x_rest")
        ln1_done = sem("ln1_done")
        x1_done = sem("x1_done")
        ln2_done = sem("ln2_done")
        misc_written = sem("misc_written")
        misc_read = sem("misc_read")
        hi_done = sem("hi_done")
        lo_done = sem("lo_done")
        q_stacked = [sem(f"q_stacked{g}") for g in range(NG)]
        k_stacked = [sem(f"k_stacked{g}") for g in range(NG)]
        kpad_done = sem("kpad_done")
        var1_done, rstd1_done = sem("var1_done"), sem("rstd1_done")
        var2_done, rstd2_done = sem("var2_done"), sem("rstd2_done")
        sa_written = sem("sa_written")
        sa_read = sem("sa_read")
        st_written = sem("st_written")
        exp_done = sem("exp_done")
        masked = sem("masked")
        pv_written = sem("pv_written")
        pv_read = sem("pv_read")
        vaug_done = sem("vaug_done")
        act_sb = sem("act_sb")
        om_done = sem("om_done")
        logits_done = sem("logits_done")
        dve_chain = sem("dve_chain")
        xn2_stored = sem("xn2_stored")

        PHASE1 = ("ln A0 mT PV0 B0 A1 B1 xn PV1 A2 PV2 B2 PV3 xT B3 A3 B4 Q B5 A4 pad0 B6 B7 OT A5 pad1 "
                  "B8 B9 pad2 A6 K pad3 B10 A7 B11")
        PHASE2 = ("A0 A1 mT PV0 B0 A2 B1 PV1 PV2 B2 PV3 zT B3 A3 B4 OT pad0 B5 B6 A4 B7 LG A5 B8 B9 "
                  "pad1 A6 pad2 B10 pad3 B11 A7")
        PHASE3 = ("A0 A1 mT PV0 B0 A2 PV1 B1 PV2 B2 PV3 B3 A3 B4 OT B5 A4 pad0 B6 B7 A5 B8 B9 pad1 B10 "
                  "A6 pad2 pad3 A7 B11")
        PHASE4 = ("A0 PV0 PV1 PV2 PV3 A1 mT B0 OT B1 A2 V B2 B3 RT A3 A4 B4 B5 out B6 B7 A5 pad0 B8 "
                  "pad1 B9 A6 pad2 zn B10 pad3 A7 B11")
        PHASES = [((0, 2), (0, 1), (0, 0), (0, 3), PHASE1),
                  ((0, 3), (0, 2), (0, 1), (1, 0), PHASE2),
                  ((1, 0), (0, 3), (0, 2), (1, 1), PHASE3),
                  ((1, 1), (1, 0), (0, 3), (1, 2), PHASE4)]
        NEXT_BATCH = ("ln", "xn", "xT", "Q", "K", "V")

        def schedule(part):
            for a, b_, pv_, pad_, order in (PHASES[3:] if part == "head" else PHASES):
                for token in order.split():
                    kind = token.rstrip("0123456789")
                    k = int(token[len(kind):] or 0)
                    ahead, g = {"A": a, "B": b_, "mT": b_, "PV": pv_, "OT": pv_, "pad": pad_}.get(kind, (0, 0))
                    if part == "last" and (ahead or kind in NEXT_BATCH):
                        continue
                    if part == "head" and not (ahead or kind == "V"):
                        continue
                    yield kind, k, ahead, g
            if part == "last":
                yield "zT", 0, 1, 0
                yield "LG", 0, 1, 0

        def misc_uses(part):
            return [kind + str(g if kind in ("mT", "OT") else ahead) for kind, _, ahead, g in schedule(part)
                    if kind in ("mT", "OT", "xT", "Q", "K", "V", "RT", "out", "zT", "LG")]

        HEAD = ["xT0", "Q0", "K0"] + misc_uses("head")
        MISC, MISC_LAST = misc_uses("loop"), misc_uses("last")

        def use(name, b):
            if isinstance(b, int) and b < 0:
                return HEAD.index(name) + 1
            order = MISC_LAST if isinstance(b, int) and b == BATCHES - 1 else MISC
            return b * len(MISC) + (len(HEAD) + order.index(name) + 1)

        NA, NB_ = 2 * NT, 3 * G

        def passes(eng, body, n):
            body(-1, "head")
            if n > 1:
                with eng.Fori(0, n - 1) as b:
                    body(b, "loop")
            body(n - 1, "last")

        def wait_apart(eng, sem_, value):
            if not isinstance(value, int):
                value = eng.to_reg(value)
                eng.wait_ge(consts, 1)
            eng.wait_ge(sem_, value)

        block = attention.enter_context(nc.Block())

        @block.sync
        def _(sp):
            def load_x(batch, loaded):
                sp.dma_start(x_all[:, batch * NT:(batch + 1) * NT, :],
                             x[batch, :, :].rearrange("(i p) d -> p i d", p=P)).then_inc(loaded, 16)

            load_x(0, x_first)
            qkv_v = w_qkv.rearrange("n d h -> d n h")
            for w, c in ((wq, 0), (wk, 1), (wv, 2)):
                sp.dma_start(w[:, :].rearrange("d (n h) -> d n h", h=HD),
                             qkv_v[:, :, c * HD:(c + 1) * HD]).then_inc(w_loaded, 16)
            sp.dma_start(wout[:, :], w_out.rearrange("n h d -> (n h) d")).then_inc(w_loaded, 16)
            sp.dma_start(wr_sb[:, :], wr).then_inc(w_loaded, 16)
            sp.dma_start(br_bc[:, :], br.rearrange("(a e) -> a e", a=1).broadcast_to([P, E])).then_inc(w_loaded, 16)

            def stack(nb, first):
                for g in range(NG):
                    if g == 0:
                        wait_apart(sp, hi_done, 2 * nb + 2)
                        wait_apart(sp, lo_done, 2 * nb + 2)
                    if not first:
                        wait_apart(sp, st_written, (nb - 1) * (NG * NB_) + NB_ * (g + 1))
                        wait_apart(sp, kpad_done, (nb - 1) * NH + G * (g + 1))
                    for c in range(TERMS):
                        rows = slice(32 * c, 32 * c + 32)
                        src = slice(32 * g, 32 * g + 32)
                        sp.dma_start(k_stack[rows, g, :].bitcast(F32), (k_hi, k_hi, k_lo)[c][src, :].bitcast(F32)).then_inc(k_stacked[g], 16)
                    sp.dma_start(q_stack[MROW:P, g, :].bitcast(F32), zeros[MROW:P, :]).then_inc(q_stacked[g], 16)
                    for c in range(TERMS):
                        rows = slice(32 * c, 32 * c + 32)
                        src = slice(32 * g, 32 * g + 32)
                        sp.dma_start(q_stack[rows, g, :].bitcast(F32), (q_hi, q_lo, q_hi)[c][src, :].bitcast(F32)).then_inc(q_stacked[g], 16)

            def body(b, part):
                if part == "head":
                    return
                if part == "loop":
                    stack(b + 1, False)
                rows = xn2_d.rearrange("(b i p) d -> b p i d", p=P, i=NT)
                wait_apart(sp, ln2_done, b + 2)
                sp.dma_start(rows[b, :, :, :], xn2[:, :, :]).then_inc(xn2_stored, 16)

            sp.wait_ge(consts, 1)
            stack(0, True)
            for batch in range(1, BATCHES):
                load_x(batch, x_rest)
            passes(sp, body, BATCHES)
            sp.wait_ge(xn2_stored, 16 * BATCHES + 1)

        @block.gpsimd
        def _(pool):
            n = 0

            def c_(ins):
                nonlocal n
                n += 1
                ins.then_inc(const_a, 1)
                pool.wait_ge(const_a, n)

            c_(pool.memset(ident[:, :], 0.0))
            c_(pool.affine_select(out=ident[:, :], in_=ident[:, :], compare_op=ALU.not_equal, fill=1.0, base=0,
                                  pattern=[[-1, P]], channel_multiplier=1))
            c_(pool.tensor_copy(identb[:, :], ident[:, :]))
            c_(pool.memset(maskneg[:, :], 0.0))
            c_(pool.affine_select(out=maskneg[:, :], in_=maskneg[:, :], compare_op=ALU.is_ge, fill=MASK, base=0,
                                  pattern=[[-1, P]], channel_multiplier=1))
            c_(pool.memset(fold[:, :], 0.0))
            for half in (0, -P // 2):
                c_(pool.affine_select(out=fold[:, :], in_=fold[:, :], compare_op=ALU.not_equal, fill=1.0, base=half,
                                      pattern=[[-1, P // 2]], channel_multiplier=1))
            c_(pool.memset(ones_col[:, :], 1.0))
            c_(pool.memset(rowmask[:, :], 1.0))
            for c in range(TERMS):
                part = rowmask[32 * c:32 * c + 32, :]
                c_(pool.affine_select(out=part, in_=part, compare_op=ALU.is_ge, fill=0.0, base=0,
                                      pattern=[[-HD, G]], channel_multiplier=1))
                c_(pool.affine_select(out=part, in_=part, compare_op=ALU.is_ge, fill=0.0, base=HD - 1,
                                      pattern=[[HD, G]], channel_multiplier=-1))
            part = rowmask[MROW:P, :]
            c_(pool.memset(part, 0.0))
            c_(pool.affine_select(out=part, in_=part, compare_op=ALU.not_equal, fill=1.0, base=0,
                                  pattern=[[-1, G]], channel_multiplier=1))
            c_(pool.memset(k_stack[MROW:P, :, :].bitcast(F32), 1.0))
            c_(pool.memset(neg_max[:, :, :, :], 0.0))
            c_(pool.memset(v_aug[:, :, :, :], 0.0))
            c_(pool.memset(v_aug[:, :, :, HD:HD + 1], 1.0))
            c_(pool.memset(zeros[:, :], 0.0))
            c_(pool.memset(minus_half[:, :], -0.5))
            c_(pool.memset(xn2[:, :, :], 0.0))
            pool.memset(o_masked[:, :, :, :, :], 0.0).then_inc(consts, 1)
            pool.wait_ge(consts, 1)

            def causal_zeros(nb, g, j):
                wait_apart(pool, exp_done, nb * (NG * NB_) + NB_ * g + 3 * (j + 1))
                for off, n_ in ((PT_OFF[0], 1), (PT_OFF[1], 1), (PT_OFF[3], 2)):
                    blk = probs[:, g % 2, j, off:off + n_ * P].rearrange("p (a q) -> p a q", q=P)
                    pool.affine_select(out=blk, in_=blk, compare_op=ALU.is_ge, fill=0.0, base=0,
                                       pattern=[[0, n_], [1, P]], channel_multiplier=-1).then_inc(masked, 1)

            def inverse_deviation(batch, var_done, rstd_done, rs_):
                pool.wait_ge(var_done, batch + 1)
                pool.tensor_tensor(rs_[:, :], rs_[:, :], minus_half[:, 0:NT], ALU.pow).then_inc(rstd_done, 1)

            def body(b, part):
                for kind, k, ahead, g in schedule(part):
                    if kind == "ln":
                        inverse_deviation(b + 1, var1_done, rstd1_done, rstd)
                    elif kind == "B" and k % 3 == 2:
                        causal_zeros(b + ahead, g, k // 3)
                    elif kind == "out":
                        inverse_deviation(b, var2_done, rstd2_done, rstd2)

            inverse_deviation(0, var1_done, rstd1_done, rstd)
            passes(pool, body, BATCHES)

        @block.tensor
        def _(pe):
            pe.wait_ge(w_loaded, 16 * 6)
            pe.wait_ge(consts, 1)

            def misc_free(name, b):
                pe.wait_ge(misc_read, use(name, b) - 1)

            def transposes(src):
                for i in range(NT):
                    last = nc.tensor.transpose(misc[:, i * P:(i + 1) * P], src(i), ident[:, :])
                last.then_inc(misc_written, 1)

            def transpose_xn(b):
                if not (isinstance(b, int) and b < 0):
                    misc_free("xT0", b)
                pe.wait_ge(ln1_done, b + 2)
                transposes(lambda i: xn[:, i, :])

            def project(name, w, b):
                misc_free(name, b)
                nc.tensor.matmul(misc[:, :], w[:, :], xnT[:, :], start=True, stop=True).then_inc(misc_written, 1)

            def a_step(nb, g, s):
                i, pair = NT - 1 - s // 2, s % 2
                n = nb * (NG * NA) + NA * g + s
                if s == 0:
                    pe.wait_ge(q_stacked[g], 16 * (TERMS + 1) * (nb + 1))
                if s < 2:
                    pe.wait_ge(kpad_done, nb * NH + G * g + 2 * pair + 2)
                if not (isinstance(nb, int) and nb == 0 and g == 0 and s < 2):
                    pe.wait_ge(sa_read, n - 1)
                width = max(2 * P, P * (i + 1))
                for h in range(2):
                    nc.tensor.matmul(sa[:, s % 2, h, 0:width], q_stack[:, g, i * P:(i + 1) * P],
                                     k_pad[:, G * g + 2 * pair + h, 0:width], start=True, stop=True)
                    last = nc.tensor.matmul(sa[:, s % 2, h, i * P:(i + 1) * P], identb[:, :], maskneg[:, :],
                                            start=False, stop=True, skip_group_check=True)
                last.then_inc(sa_written, 1)

            def b_step(nb, g, t):
                j, part = t // 3, t % 3
                n = nb * (NG * NB_) + NB_ * g + t
                if t == 0:
                    pe.wait_ge(act_sb, nb * NG + g + 1)
                if not (isinstance(nb, int) and nb == 0 and g == 0 and t < 2):
                    pe.wait_ge(exp_done, n - 1)
                h = G * g + j
                buf = st[:, t % 2, :]
                if part == 0:
                    mm = [(0, 0, 512)]
                elif part == 1:
                    mm = [(1, 0, 384)]
                else:
                    mm = [(3, 0, 256), (2, 256, 256)]
                for kk, at, w in mm:
                    last = nc.tensor.matmul(buf[:, at:at + w], k_pad[:, h, kk * P:(kk + 1) * P],
                                            q_stack[:, g, S - w:S], start=True, stop=True)
                last.then_inc(st_written, 1)

            def pv_part(b, g, kk):
                if kk == 0:
                    pe.wait_ge(masked, b * (NG * NB_) + NB_ * (g + 1))
                    pe.wait_ge(vaug_done, b + 1)
                    pe.wait_ge(pv_read, b * NG + g + 1)
                for j in range(G):
                    w = S - kk * P
                    last = nc.tensor.matmul(pv[32 * j:32 * j + 32, kk * P:S], v_aug[:, kk, G * g + j, :],
                                            probs[:, g % 2, j, PT_OFF[kk]:PT_OFF[kk] + w],
                                            start=(kk == 0), stop=True, skip_group_check=True)
                if kk == NT - 1:
                    last.then_inc(pv_written, 1)

            def body(b, part):
                for kind, k, ahead, g in schedule(part):
                    if kind == "A":
                        a_step(b + ahead, g, k)
                    elif kind == "mT":
                        misc_free(f"mT{g}", b)
                        pe.wait_ge(sa_read, (b + ahead) * (NG * NA) + NA * (g + 1))
                        for i in range(NT):
                            last = nc.tensor.transpose(misc[0:MROW + G, i * P:(i + 1) * P],
                                                       neg_max[:, g % 2, i, :], ident[:, :])
                        last.then_inc(misc_written, 1)
                    elif kind == "B":
                        b_step(b + ahead, g, k)
                    elif kind == "PV":
                        pv_part(b, g, k)
                    elif kind == "xT":
                        transpose_xn(b)
                    elif kind in ("Q", "K"):
                        project(kind + "0", wq if kind == "Q" else wk, b)
                    elif kind == "V":
                        misc_free("V0", b)
                        for i in range(NT):
                            last = nc.tensor.matmul(misc[:, i * P:(i + 1) * P], xnT[:, i * P:(i + 1) * P], wv[:, :],
                                                    start=True, stop=True)
                        last.then_inc(misc_written, 1)
                    elif kind == "OT":
                        misc_free(f"OT{g}", b)
                        pe.wait_ge(pv_read, b * NG + g + 2)
                        transposes(lambda i: pv_sb[:, i * P:(i + 1) * P])
                    elif kind == "RT":
                        misc_free("RT0", b)
                        pe.wait_ge(om_done, (b + 1) * NG)
                        for h in range(HD):
                            last = nc.tensor.matmul(misc[:, h * (P // 2):(h + 1) * (P // 2)],
                                                    o_masked[:, h, :, :, :].rearrange("p n i c -> p (n i c)"),
                                                    fold[:, :], start=True, stop=True)
                        last.then_inc(misc_written, 1)
                    elif kind == "out":
                        misc_free("out0", b)
                        transposes(lambda i: attn_T[:, i * P:(i + 1) * P])
                    elif kind == "zT":
                        misc_free(f"zT{ahead}", b)
                        pe.wait_ge(ln2_done, b + ahead + 1)
                        transposes(lambda i: xn2[:, i, :])
                    elif kind == "LG":
                        misc_free(f"LG{ahead}", b)
                        for i in range(NT):
                            last = nc.tensor.matmul(misc[:, i * E:(i + 1) * E], xn2T[:, i * P:(i + 1) * P],
                                                    wr_sb[:, :], start=True, stop=True)
                        last.then_inc(misc_written, 1)

            nc.tensor.matmul(st[:, 1, 0:1], wout[:, :], ones_col[:, :], start=True, stop=True).then_inc(vconst, 1)
            transpose_xn(-1)
            project("Q0", wq, -1)
            project("K0", wk, -1)
            pe.wait_ge(consts, 2)
            for s in range(NA):
                a_step(0, 0, s)
            passes(pe, body, BATCHES)

        @block.scalar
        def _(act):
            act.wait_ge(consts, 1)

            def copy_misc(name, b, out_):
                act.wait_ge(misc_written, use(name, b))
                nc.scalar.activation(out_, misc[:, :], ACT.Copy).then_inc(misc_read, 1)

            def high_part(name, b, out_, scale):
                act.wait_ge(misc_written, use(name, b))
                nc.scalar.activation(out_, misc[:, :], ACT.Copy, scale=scale).then_inc(hi_done, 1)

            def body(b, part):
                for kind, k, ahead, g in schedule(part):
                    if kind == "xT":
                        copy_misc("xT0", b, xnT[:, :])
                    elif kind in ("Q", "K"):
                        if kind == "Q":
                            for c in range(NG):
                                act.wait_ge(q_stacked[c], 16 * (TERMS + 1) * (b + 1))
                                act.wait_ge(k_stacked[c], 16 * TERMS * (b + 1))
                        high_part(kind + "0", b, *((q_hi[:, :], SCALE) if kind == "Q" else (k_hi[:, :], 1.0)))
                    elif kind == "V":
                        act.wait_ge(misc_written, use("V0", b))
                        if part != "head":
                            act.wait_ge(pv_written, (b + 1) * NG)
                        nc.scalar.activation(v_aug[:, :, :, 0:HD],
                                             misc[:, :].rearrange("p (i n h) -> p i n h", i=NT, h=HD),
                                             ACT.Copy).then_inc(vaug_done, 1)
                        act.wait_ge(vaug_done, b + 2)
                        act.sem_inc(misc_read, 1)
                    elif kind == "mT":
                        act.wait_ge(misc_written, use(f"mT{g}", b))
                        nc.scalar.activation(q_stack[MROW:MROW + G, g, :], misc[MROW:MROW + G, :],
                                             ACT.Copy).then_inc(act_sb, 1)
                        act.wait_ge(act_sb, (b + ahead) * NG + g + 1)
                        act.sem_inc(misc_read, 1)
                    elif kind == "B":
                        j, third = k // 3, k % 3
                        act.wait_ge(st_written, (b + ahead) * (NG * NB_) + NB_ * g + k + 1)
                        lo, w, at = ((0, 512, 0), (512, 384, 0), (896, 384, 128))[third]
                        nc.scalar.activation(probs[:, g % 2, j, lo:lo + w], st[:, k % 2, at:at + w],
                                             ACT.Exp).then_inc(exp_done, 1)
                    elif kind == "PV" and k == NT - 1:
                        act.wait_ge(pv_written, b * NG + g + 1)
                        if g > 0:
                            act.wait_ge(misc_written, use(f"OT{g - 1}", b))
                        nc.scalar.activation(pv_sb[:, :], pv[:, :], ACT.Copy).then_inc(pv_read, 1)
                    elif kind == "RT":
                        act.wait_ge(misc_written, use("RT0", b))
                        nc.scalar.activation(attn_T[:, :].rearrange("p (r h) -> p h r", h=HD),
                                             misc[:, :].rearrange("p (h r) -> p h r", h=HD),
                                             ACT.Copy, scale=wsum[:, 0:1]).then_inc(misc_read, 1)
                    elif kind == "zT":
                        copy_misc(f"zT{ahead}", b, xn2T[:, :])

            act.sem_inc(pv_read, 1)
            act.sem_inc(xn2_stored, 1)
            act.sem_inc(ln2_done, 1)
            copy_misc("xT0", -1, xnT[:, :])
            high_part("Q0", -1, q_hi[:, :], SCALE)
            high_part("K0", -1, k_hi[:, :], 1.0)
            passes(act, body, BATCHES)

        @block.vector
        def _(dve):
            dve.wait_ge(consts, 1)
            dve.wait_ge(vconst, 1)
            nc.vector.tensor_copy(wsum[:, :], st[:, 1, 0:1]).then_inc(consts, 1)

            BEFORE, PER_PASS = 2, 2 + NG + 2
            done = [0]

            def link(ins, b, apart=False):
                done[0] += 1
                ins.then_inc(dve_chain, 1)
                if isinstance(b, int) and b < 0:
                    dve.wait_ge(dve_chain, done[0])
                elif apart:
                    wait_apart(dve, dve_chain, b * PER_PASS + (BEFORE + done[0]))
                else:
                    dve.wait_ge(dve_chain, b * PER_PASS + (BEFORE + done[0]))

            def x_of(batch, i):
                return x_all[:, bass.ds(batch * NT + i, 1), :].rearrange("p a d -> p (a d)")

            def statistics(batch, st_, mv_, rs_, b, var_done):
                for i in range(NT):
                    last = nc.vector.bn_stats(st_[:, i, :], x_of(batch, i))
                link(last, b, apart=True)
                for i in range(NT):
                    last = nc.vector.bn_aggr(mv_[:, i, :], st_[:, i, :])
                link(last, b)
                nc.vector.tensor_scalar(rs_[:, :], mv_[:, :, 1], LN_EPS, None, ALU.add).then_inc(var_done, 1)

            def normalise(batch, dst, mv_, rs_, rstd_done, ready):
                dve.wait_ge(rstd_done, batch + 1)
                for i in range(NT):
                    last = nc.vector.tensor_scalar(dst[:, i, :], x_of(batch, i), mv_[:, i, 0:1], rs_[:, i:i + 1],
                                                   ALU.subtract, ALU.mult)
                last.then_inc(ready, 1)

            def low_part(name, b):
                hi, lo, scale, k = (q_hi, q_lo, SCALE, 1) if name == "Q" else (k_hi, k_lo, 1.0, 2)
                dve.wait_ge(hi_done, 2 * (b + 1) + k)
                nc.vector.scalar_tensor_tensor(lo[:, :], misc[:, :], scale, hi[:, :].bitcast(F32),
                                               ALU.mult, ALU.subtract).then_inc(lo_done, 1)
                dve.wait_ge(lo_done, 2 * (b + 1) + k)
                dve.sem_inc(misc_read, 1)

            def pad_key(nb, g, j):
                if j == 0:
                    dve.wait_ge(k_stacked[g], 16 * TERMS * (nb + 1))
                nc.vector.tensor_scalar(k_pad[:, G * g + j, :], k_stack[:, g, :].bitcast(F32), rowmask[:, j:j + 1],
                                        None, ALU.mult).then_inc(kpad_done, 1)

            def reduce_step(nb, g, s):
                i, pair = NT - 1 - s // 2, s % 2
                if s == 0 and not (isinstance(nb, int) and nb == 0 and g < 2):
                    dve.wait_ge(act_sb, nb * NG + g - 1)
                dve.wait_ge(sa_written, nb * (NG * NA) + NA * g + s + 1)
                nc.vector.tensor_reduce(neg_max[:, g % 2, i, MROW + 2 * pair:MROW + 2 * pair + 2],
                                        sa[:, s % 2, :, 0:(i + 1) * P], AX.X, ALU.max,
                                        negate=True).then_inc(sa_read, 1)

            def body(b, part):
                done[0] = 0
                for kind, k, ahead, g in schedule(part):
                    if kind == "A":
                        reduce_step(b + ahead, g, k)
                    elif kind == "pad":
                        pad_key(b + ahead, g, k)
                    elif kind == "ln":
                        dve.wait_ge(x_rest, 16 * (BATCHES - 1))
                        statistics(b + 1, stats, mv, rstd, b, var1_done)
                    elif kind == "xn":
                        normalise(b + 1, xn, mv, rstd, rstd1_done, ln1_done)
                    elif kind in ("Q", "K"):
                        low_part(kind, b)
                    elif kind == "OT":
                        dve.wait_ge(misc_written, use(f"OT{g}", b))
                        ot = misc[:, :].rearrange("p (i j c) -> p i j c", i=NT, j=G)
                        link(nc.vector.reciprocal(rden[:, :, :], ot[:, :, :, HD]), b)
                        for c in range(2):
                            half = slice(c * (P // 2), (c + 1) * (P // 2))
                            dst = o_masked[half, :, G * g:G * g + G, :, c].rearrange("p h j i -> p i j h")
                            last = nc.vector.tensor_tensor(
                                dst, ot[half, :, :, 0:HD],
                                rden[half, :, :].unsqueeze(3).broadcast_to([P // 2, NT, G, HD]), ALU.mult)
                        last.then_inc(om_done, 1)
                        dve.wait_ge(om_done, b * NG + g + 1)
                        dve.sem_inc(misc_read, 1)
                    elif kind == "out":
                        dve.wait_ge(misc_written, use("out0", b))
                        rows = x_all[:, bass.ds(b * NT, NT), :]
                        nc.vector.tensor_tensor(rows, misc[:, :].rearrange("p (i d) -> p i d", i=NT),
                                                rows, ALU.add).then_inc(x1_done, 1)
                        wait_apart(dve, x1_done, b + 1)
                        dve.sem_inc(misc_read, 1)
                        statistics(b, stats2, mv2, rstd2, b, var2_done)
                    elif kind == "zn":
                        dve.wait_ge(xn2_stored, 16 * b + 1)
                        normalise(b, xn2, mv2, rstd2, rstd2_done, ln2_done)
                    elif kind == "LG":
                        dve.wait_ge(misc_written, use(f"LG{ahead}", b))
                        nc.vector.tensor_tensor(logits_all[:, bass.ds((b + ahead) * NT, NT), :],
                                                misc[:, 0:NT * E].rearrange("p (i e) -> p i e", i=NT),
                                                br_bc[:, :].unsqueeze(1).broadcast_to([P, NT, E]),
                                                ALU.add).then_inc(logits_done, 1)
                        dve.wait_ge(logits_done, b + ahead + 1)
                        dve.sem_inc(misc_read, 1)
                assert part != "loop" or done[0] == PER_PASS, done

            dve.wait_ge(x_first, 16)
            statistics(0, stats, mv, rstd, -1, var1_done)
            normalise(0, xn, mv, rstd, rstd1_done, ln1_done)
            low_part("Q", -1)
            low_part("K", -1)
            for g in range(2):
                for j in range(G):
                    pad_key(0, g, j)
            for s in range(NA):
                reduce_step(0, 0, s)
            passes(dve, body, BATCHES)

        attention.close()
        part = ctx
        logits = logits_all[:, NT:, :]
        TT = BATCHES * NT
        NTOK = TT * P
        UNROLL = 8
        TILES = -(-(2 * TT + E - 1) // UNROLL) * UNROLL
        FC = F // P
        BIG = 2.0 * E
        OH, NOH = 4, 4

        y2_d = nc.dram_tensor("y2_scratch", (2 * NTOK + TILES * P, D), F32).ap()

        w_hi = [sb(n, [P, E * F], F32R) for n in ("wi_hi", "wg_hi")]
        w_lo = [sb(n, [P, E * F], F32R) for n in ("wi_lo", "wg_lo")]
        wo_sb = sb("wo_sb", [P, E * FC * D])
        b_stack = sb("b_stack", [P, F], BF16)
        b_sel = sb("b_sel", [P, 3 * E * P], BF16)
        upper = sb("upper", [P, P], BF16)
        onesb = sb("onesb", [P, P], BF16)
        iota_e = sb("iota_e", [P, E])
        iota_p = sb("iota_p", [P, P])
        iota_s = sb("iota_s", [P, TILES])
        iota_t = sb("iota_t", [P, TT])
        value = sb("value", [P, TT, 2])
        slot_id = sb("slot_id", [P, TILES])
        weight = sb("weight", [P, TT, 2])
        row_f = sb("row_f", [P, TT * 2])
        tile_f = sb("tile_f", [P, TT * 2])
        table = sb("table", [P, TILES, 2], I32)
        expert = sb("expert", [P, TILES], I32)

        route = part = ExitStack()
        one_r = sb("one_r", [P, NOH, OH, P])
        one_s = sb("one_s", [P, NOH, OH, TILES], BF16)
        one_v = sb("one_v", [P, NOH, OH, TILES])
        b_all = sb("b_all", [P, F])
        b_part = sb("b_part", [P, 3, F], BF16)
        b_rest = sb("b_rest", [P, F])
        stage = sb("stage", [P, 4, F])
        iota_i = sb("iota_i", [P, max(2 * TT, TILES, P)], I32)
        shifted = sb("shifted", [P, TT, E])
        ex = sb("ex", [P, TT, E])
        pr = sb("pr", [P, TT, E])
        pr2 = sb("pr2", [P, TT, E])
        tmp = sb("tmp", [P, TT, E])
        oh = [sb(f"oh{c}", [P, TT, E]) for c in range(2)]
        chosen = sb("chosen", [P, TT, E], BF16)
        mx = sb("mx", [P, TT])
        sm = sb("sm", [P, TT])
        pm = sb("pm", [P, TT, 2])
        first = sb("first", [P, TT])
        tot = sb("tot", [P, E, TT])
        cum = sb("cum", [P, E, TT])
        cmp_ = sb("cmp_", [P, E, TT])
        one_t = sb("one_t", [P, E * TT])
        slot = sb("slot", [P, E, TT])
        count = sb("count", [P, E])
        start = sb("start", [P, E])
        ntile = sb("ntile", [P, E])
        tend = sb("tend", [P, E])
        base = sb("base", [P, E])
        slot2 = sb("slot2", [P, TT, 2])
        slot_i = sb("slot_i", [P, TT, 2], I32)
        part_i = sb("part_i", [P, TT, 2], I32)
        cmp_s = sb("cmp_s", [P, TILES, E])
        exp_f = sb("exp_f", [P, TILES])
        tab_f = sb("tab_f", [P, 3, TILES])
        tab_i = sb("tab_i", [P, TILES], I32)

        counts_ps = pb("counts_ps", [P, 2, TT * E])
        table_ps = pb("table_ps", [P, TILES])

        r_const = sem("r_const")
        stage_loaded = [sem(f"stage_loaded{k}") for k in range(4)]
        w_hi_done = sem("w_hi_done")
        w_lo_done = sem("w_lo_done")
        bias_loaded = sem("bias_loaded")
        ffn_loaded = sem("ffn_loaded")
        bias_done = sem("bias_done")
        r_chain = sem("r_chain")
        shifted_done = sem("shifted_done")
        exp_ready = sem("exp_ready")
        chosen_done = sem("chosen_done")
        counts_done = sem("counts_done")
        onehot_done = sem("onehot_done")
        onehot_scaled = sem("onehot_scaled")
        onehot_used = sem("onehot_used")
        table_done = sem("table_done")
        table_zero = sem("table_zero")

        made = {}

        block = route.enter_context(nc.Block())

        @block.sync
        def _(sp):
            for k in range(2 * E):
                m, e = k // E, k % E
                if k >= 4:
                    sp.wait_ge(w_lo_done, k - 3)
                sp.dma_start(stage[:, k % 4, :], (wi, wg)[m][e, :, :]).then_inc(stage_loaded[k % 4], 16)
                if k == 3:
                    sp.wait_ge(bias_done, 1)
                    for c in range(3):
                        sp.dma_start(b_all[32 * c:32 * c + E, :], bi).then_inc(bias_loaded, 16)
                        sp.dma_start(b_all[32 * c + E:32 * c + 2 * E, :], bg).then_inc(bias_loaded, 16)
                        for m, src in enumerate((bo, gamma, beta)):
                            sp.dma_start(b_all[32 * c + 2 * E:32 * c + 3 * E, m * D:(m + 1) * D], src)\
                                .then_inc(bias_loaded, 16)
            for e in range(E):
                sp.dma_start(wo_sb[:, e * FC * D:(e + 1) * FC * D].rearrange("p (c d) -> p c d", c=FC),
                             wo[e, :, :].rearrange("(c p) d -> p c d", p=P)).then_inc(ffn_loaded, 16)
            sp.wait_ge(ffn_loaded, 16 * E)

        @block.gpsimd
        def _(pool):
            n = 0

            def c_(ins):
                nonlocal n
                n += 1
                ins.then_inc(r_const, 1)
                pool.wait_ge(r_const, n)

            def iota(dst, width, step, base_, mult):
                c_(pool.iota(iota_i[:, 0:width], pattern=[[step, width]], base=base_, channel_multiplier=mult))
                c_(pool.tensor_copy(dst, iota_i[:, 0:width]))

            iota(iota_e[:, :], E, 1, 0, 0)
            made["iota_e"] = n
            c_(pool.memset(upper[:, :], 1.0))
            c_(pool.affine_select(out=upper[:, :], in_=upper[:, :], compare_op=ALU.is_gt, fill=0.0, base=0,
                                  pattern=[[1, P]], channel_multiplier=-1))
            c_(pool.memset(onesb[:, :], 1.0))
            made["upper, onesb"] = n
            c_(pool.memset(one_t[:, :], 1.0))
            iota(iota_t[:, :], TT, P, 0, 0)
            made["one_t, iota_t"] = n
            iota(iota_p[:, :], P, 1, 0, 0)
            iota(iota_s[:, :], TILES, 1, 0, 0)
            c_(pool.iota(iota_i[:, 0:2 * TT], pattern=[[2 * P, TT], [1, 2]], base=1, channel_multiplier=2))
            c_(pool.tensor_copy(value[:, :, :].rearrange("p t c -> p (t c)"), iota_i[:, 0:2 * TT]))
            made["iota_p, iota_s, value"] = n
            for k in range(2 * E):
                m, e = k // E, k % E
                pool.wait_ge(w_hi_done, k + 1)
                pool.tensor_tensor(w_lo[m][:, e * F:(e + 1) * F], stage[:, k % 4, :],
                                   w_hi[m][:, e * F:(e + 1) * F].bitcast(F32), ALU.subtract).then_inc(w_lo_done, 1)
            c_(pool.memset(b_stack[:, :], 0.0))
            pool.wait_ge(bias_loaded, 16 * 15)
            c_(pool.tensor_copy(b_part[:, 0, :], b_all[:, :]))
            c_(pool.tensor_tensor(b_rest[:, :], b_all[:, :], b_part[:, 0, :], ALU.subtract))
            c_(pool.tensor_copy(b_part[:, 1, :], b_rest[:, :]))
            c_(pool.tensor_tensor(b_all[:, :], b_rest[:, :], b_part[:, 1, :], ALU.subtract))
            c_(pool.tensor_copy(b_part[:, 2, :], b_all[:, :]))
            for c in range(3):
                c_(pool.tensor_copy(b_stack[32 * c:32 * c + 3 * E, :], b_part[32 * c:32 * c + 3 * E, c, :]))
            c_(pool.memset(b_sel[:, :], 0.0))
            for c in range(3):
                rows = b_sel[32 * c:32 * c + 32, :].rearrange("r (m q) -> r m q", q=P)
                c_(pool.affine_select(out=rows, in_=rows, compare_op=ALU.not_equal, fill=1.0, base=0,
                                      pattern=[[-1, 3 * E], [0, P]], channel_multiplier=1))
            iota(slot_id[:, :], TILES, P, 2 * NTOK + 1, 1)
            made["slot_id"] = n

        @block.scalar
        def _(act):
            act.wait_ge(shifted_done, 1)
            nc.scalar.activation(ex[:, :, :], shifted[:, :, :], ACT.Exp).then_inc(exp_ready, 1)

            def high_part(k):
                m, e = k // E, k % E
                act.wait_ge(stage_loaded[k % 4], 16 * (k // 4 + 1))
                nc.scalar.activation(w_hi[m][:, e * F:(e + 1) * F], stage[:, k % 4, :],
                                     ACT.Copy).then_inc(w_hi_done, 1)

            for k in range(2 * E):
                high_part(k)
            vals = value[:, :, :].rearrange("p t c -> p (t c)")
            with act.Fori(0, 2 * TT // (NOH * OH)) as t:
                for u in range(NOH):
                    act.wait_ge(onehot_done, NOH * t + (u + 1))
                    for j in range(OH):
                        last = nc.scalar.activation(one_v[:, u, j, :], one_s[:, u, j, :], ACT.Copy,
                                                    scale=vals[:, bass.ds(t * (NOH * OH) + (u * OH + j), 1)])
                    last.then_inc(onehot_scaled, 1)

        @block.tensor
        def _(pe):
            pe.wait_ge(r_const, made["upper, onesb"])
            pe.wait_ge(chosen_done, 1)
            rhs = chosen[:, :, :].rearrange("p t e -> p (t e)")
            nc.tensor.matmul(counts_ps[:, 0, :], upper[:, :], rhs, start=True, stop=True)
            nc.tensor.matmul(counts_ps[:, 1, :], onesb[:, :], rhs, start=True, stop=True).then_inc(counts_done, 1)
            pe.wait_ge(table_zero, 1)
            for u in range(NOH):
                nc.tensor.matmul(table_ps[:, :], one_r[:, 0, 0, :], one_v[:, 0, 0, :], start=(u == 0), stop=True,
                                 skip_group_check=True).then_inc(onehot_used, 1)
            with pe.Fori(0, 2 * TT // (NOH * OH)) as t:
                for u in range(NOH):
                    pe.wait_ge(onehot_scaled, NOH * t + (u + 1))
                    for j in range(OH):
                        last = nc.tensor.matmul(table_ps[:, :], one_r[:, u, j, :], one_v[:, u, j, :], start=False,
                                                stop=True, skip_group_check=True)
                    last.then_inc(onehot_used, 1)

        @block.vector
        def _(dve):
            V = nc.vector
            n = 0

            def link(ins):
                nonlocal n
                n += 1
                ins.then_inc(r_chain, 1)
                dve.wait_ge(r_chain, n)

            def over_e(ap):
                return ap.unsqueeze(2).broadcast_to([P, TT, E])

            ie = iota_e[:, :].unsqueeze(1).broadcast_to([P, TT, E])
            V.memset(b_all[:, :], 0.0).then_inc(bias_done, 1)
            link(V.tensor_reduce(mx[:, :], logits[:, :, :], AX.X, ALU.max))
            V.tensor_tensor(shifted[:, :, :], logits[:, :, :], over_e(mx[:, :]), ALU.subtract).then_inc(shifted_done, 1)
            dve.wait_ge(r_const, made["iota_e"])
            dve.wait_ge(exp_ready, 1)
            link(V.tensor_reduce(sm[:, :], ex[:, :, :], AX.X, ALU.add))
            link(V.reciprocal(sm[:, :], sm[:, :]))
            link(V.tensor_tensor(pr[:, :, :], ex[:, :, :], over_e(sm[:, :]), ALU.mult))
            src = pr
            for c in range(2):
                link(V.tensor_reduce(pm[:, :, c], src[:, :, :], AX.X, ALU.max))
                link(V.tensor_tensor(tmp[:, :, :], src[:, :, :], over_e(pm[:, :, c]), ALU.is_lt))
                link(V.scalar_tensor_tensor(tmp[:, :, :], tmp[:, :, :], BIG, ie, ALU.mult, ALU.add))
                link(V.tensor_reduce(first[:, :], tmp[:, :, :], AX.X, ALU.min))
                link(V.tensor_tensor(oh[c][:, :, :], ie, over_e(first[:, :]), ALU.is_equal))
                if c == 0:
                    link(V.scalar_tensor_tensor(pr2[:, :, :], oh[0][:, :, :], -2.0, pr[:, :, :], ALU.mult, ALU.add))
                    src = pr2
            V.tensor_tensor(chosen[:, :, :], oh[0][:, :, :], oh[1][:, :, :], ALU.add).then_inc(chosen_done, 1)
            link(V.tensor_tensor(sm[:, :], pm[:, :, 0], pm[:, :, 1], ALU.add))
            link(V.reciprocal(sm[:, :], sm[:, :]))
            V.tensor_tensor(weight[:, :, :], pm[:, :, :], sm[:, :].unsqueeze(2).broadcast_to([P, TT, 2]), ALU.mult)
            dve.wait_ge(r_const, made["one_t, iota_t"])
            dve.wait_ge(counts_done, 1)
            within = counts_ps[:, 0, :].rearrange("p (t e) -> p e t", e=E)
            total = counts_ps[:, 1, :].rearrange("p (t e) -> p e t", e=E)
            link(V.tensor_copy(tot[:, :, :], total))
            flat = "p e t -> p (e t)"
            link(V.tensor_tensor_scan(cum[:, :, :].rearrange(flat), one_t[:, :], tot[:, :, :].rearrange(flat), 0.0,
                                      ALU.mult, ALU.add))
            link(V.memset(start[:, 0:1], 0.0))
            link(V.tensor_copy(start[:, 1:E], cum[:, 0:E - 1, TT - 1]))
            link(V.tensor_tensor(count[:, :], cum[:, :, TT - 1], start[:, :], ALU.subtract))
            link(V.tensor_tensor(cmp_[:, :, :], count[:, :].unsqueeze(2).broadcast_to([P, E, TT]),
                                 iota_t[:, :].unsqueeze(1).broadcast_to([P, E, TT]), ALU.is_gt))
            link(V.tensor_reduce(ntile[:, :], cmp_[:, :, :], AX.X, ALU.add))
            link(V.tensor_tensor_scan(tend[:, :], one_t[:, 0:E], ntile[:, :], 0.0, ALU.mult, ALU.add))
            link(V.tensor_tensor(base[:, :], tend[:, :], ntile[:, :], ALU.subtract))
            link(V.scalar_tensor_tensor(base[:, :], base[:, :], float(P), start[:, :], ALU.mult, ALU.subtract))
            link(V.tensor_tensor(slot[:, :, :], cum[:, :, :], tot[:, :, :], ALU.subtract))
            link(V.tensor_tensor(slot[:, :, :], slot[:, :, :], base[:, :].unsqueeze(2).broadcast_to([P, E, TT]),
                                 ALU.add))
            link(V.tensor_tensor(slot[:, :, :], slot[:, :, :], within, ALU.add))
            for c in range(2):
                link(V.tensor_tensor(tmp[:, :, :], oh[c][:, :, :], slot[:, :, :].rearrange("p e t -> p t e"), ALU.mult))
                link(V.tensor_reduce(slot2[:, :, c], tmp[:, :, :], AX.X, ALU.add))
            link(V.tensor_copy(slot_i[:, :, :], slot2[:, :, :]))
            link(V.tensor_single_scalar(part_i[:, :, :], slot_i[:, :, :], P - 1, ALU.bitwise_and))
            link(V.tensor_copy(row_f[:, :], part_i[:, :, :].rearrange("p t c -> p (t c)")))
            link(V.tensor_single_scalar(part_i[:, :, :], slot_i[:, :, :], P.bit_length() - 1, ALU.logical_shift_right))
            link(V.tensor_copy(tile_f[:, :], part_i[:, :, :].rearrange("p t c -> p (t c)")))
            dve.wait_ge(r_const, made["iota_p, iota_s, value"])
            link(V.tensor_tensor(cmp_s[:, :, :], iota_s[:, :].unsqueeze(2).broadcast_to([P, TILES, E]),
                                 tend[:, :].unsqueeze(1).broadcast_to([P, TILES, E]), ALU.is_ge))
            link(V.tensor_reduce(exp_f[:, :], cmp_s[:, :, :], AX.X, ALU.add))
            link(V.tensor_scalar(exp_f[:, :], exp_f[:, :], float(E - 1), None, ALU.min))
            link(V.tensor_copy(expert[:, :], exp_f[:, :]))
            link(V.memset(one_r[:, 0, 0, :], 0.0))
            V.memset(one_v[:, 0, 0, :], 0.0).then_inc(table_zero, 1)

            dve.wait_ge(onehot_used, NOH)
            with dve.Fori(0, 2 * TT // (NOH * OH)) as t:
                for u in range(NOH):
                    dve.wait_ge(onehot_used, NOH * t + (u + 1))
                    for dst, ids, of, width in ((one_r, iota_p, row_f, P), (one_s, iota_s, tile_f, TILES)):
                        last = V.tensor_tensor(dst[:, u, :, :],
                                               ids[:, :].unsqueeze(1).broadcast_to([P, OH, width]),
                                               of[:, bass.ds(t * (NOH * OH) + u * OH, OH)].unsqueeze(2)
                                               .broadcast_to([P, OH, width]), ALU.is_equal)
                    last.then_inc(onehot_done, 1)

            dve.wait_ge(r_const, made["slot_id"])
            dve.wait_ge(onehot_used, 2 * TT // OH + NOH)
            link(V.tensor_copy(tab_f[:, 0, :], table_ps[:, :]))
            link(V.tensor_scalar(tab_f[:, 1, :], tab_f[:, 0, :], 0.5, None, ALU.is_lt))
            link(V.tensor_tensor(tab_f[:, 1, :], tab_f[:, 1, :], slot_id[:, :], ALU.mult))
            link(V.tensor_scalar(tab_f[:, 0, :], tab_f[:, 0, :], 1.0, None, ALU.subtract))
            link(V.tensor_tensor(tab_f[:, 1, :], tab_f[:, 0, :], tab_f[:, 1, :], ALU.add))
            link(V.tensor_copy(table[:, :, 1], tab_f[:, 1, :]))
            link(V.tensor_scalar(tab_f[:, 2, :], tab_f[:, 0, :], 0.0, None, ALU.max))
            link(V.tensor_copy(tab_i[:, :], tab_f[:, 2, :]))
            V.tensor_single_scalar(table[:, :, 0], tab_i[:, :], 1, ALU.logical_shift_right).then_inc(table_done, 1)
            dve.wait_ge(table_done, 1)

        route.close()
        part = ctx

        NX, NR = 8, 4
        from_row = sb("from_row", [P, NX], I32)
        to_row = sb("to_row", [P, NR], I32)
        xg = sb("xg", [P, NX, D])
        xg_hi = sb("xg_hi", [P, 2, P], F32R)
        xg_lo = sb("xg_lo", [P, 2, P], F32R)
        gelu = sb("gelu", [P, 2, F])
        gate = sb("gate", [P, 2, F])
        hid = sb("hid", [P, 2, F])
        hidT = sb("hidT", [P, 2, F])
        res = sb("res", [P, NR, D])
        st6 = sb("st6", [P, 2, 6])
        mean_var = sb("mean_var", [P, NR, 2])
        inv_dev = sb("inv_dev", [P, NR])
        z = sb("z", [P, NR, D])
        NY = 4
        y2 = sb("y2", [P, NY, NT, 2 * D])

        up_i = pb("up_i", [P, 2, F])
        up_g = pb("up_g", [P, 2, F])
        ht_ps = pb("ht_ps", [P, F])
        y_ps = pb("y_ps", [P, D])
        xt_ps = pb("xt_ps", [P, P])
        gb_ps = pb("gb_ps", [P, 2 * D])

        idx_done = sem("idx_done")
        gathered = [sem(f"gathered{u}") for u in range(NX)]
        scattered = [sem(f"scattered{u}") for u in range(NR)]
        xt_written, xhi_done, xlo_done = sem("xt_written"), sem("xhi_done"), sem("xlo_done")
        up_written, gelu_done, gate_done = sem("up_written"), sem("gelu_done"), sem("gate_done")
        hid_done, ht_written, hidT_done = sem("hid_done"), sem("ht_written"), sem("hidT_done")
        y_written, res_done, ve_done, dev_done = sem("y_written"), sem("res_done"), sem("ve_done"), sem("dev_done")
        gb_written = sem("gb_written")
        z_done, x_chain, z_chain = sem("z_done"), sem("x_chain"), sem("z_chain")
        comb_loaded = [sem(f"comb_loaded{u}") for u in range(NY)]
        comb_done, c_chain, out_stored = sem("comb_done"), sem("c_chain"), sem("out_stored")

        experts = ExitStack()
        block = experts.enter_context(nc.Block())

        def rounds(s, u, n):
            return 16 * (s // n + 1) if isinstance(s, int) else (s - u % n) * (16 // n) + 16

        def stages(eng, stage_fns):
            most = max(lag for lag, _ in stage_fns)

            def step(s, u):
                for lag, fn in stage_fns:
                    if isinstance(s, int) and not 0 <= s - lag < TILES:
                        continue
                    fn(s - lag, (u - lag) % UNROLL)

            least = min(lag for lag, _ in stage_fns)
            for u in range(least, UNROLL):
                step(u, u % UNROLL)
            peel_last = least < 0
            full = TILES // UNROLL - (1 if peel_last else 0)
            if full > 1:
                with eng.Fori(1, full) as k:
                    for u in range(UNROLL):
                        step(k * UNROLL + u, u)
            for s in range(max(full, 1) * UNROLL, TILES + most):
                step(s, s % UNROLL)

        @block.gpsimd
        def _(pool):
            def gather(s, u):
                wait_apart(pool, idx_done, s + 1)
                pool.indirect_dma_start(xg[:, u, :], None, xn2_d[0:NTOK, :],
                                        bass.IndirectOffsetOnAxis(from_row[:, u:u + 1], 0)).then_inc(gathered[u], 16)

            def deviation(s, u):
                pool.wait_ge(ve_done, s + 1)
                r = u % NR
                pool.tensor_tensor(inv_dev[:, r:r + 1], inv_dev[:, r:r + 1], minus_half[:, 0:1],
                                   ALU.pow).then_inc(dev_done, 1)

            def scatter(s, u):
                wait_apart(pool, z_done, s + 1)
                pool.indirect_dma_start(y2_d, bass.IndirectOffsetOnAxis(to_row[:, u % NR:u % NR + 1], 0), z[:, u % NR, :], None)\
                    .then_inc(scattered[u % NR], 16)

            stages(pool, [(3, deviation), (4, scatter), (-3, gather)])
            for r in range(NR):
                pool.wait_ge(scattered[r], 16 * (TILES // NR))

        @block.tensor
        def _(pe):
            def transpose_x(s, u):
                pe.wait_ge(gathered[u], rounds(s, u, NX))
                if not (isinstance(s, int) and s < 1):
                    pe.wait_ge(xlo_done, s)
                nc.tensor.transpose(xt_ps[:, :], xg[:, u, :], ident[:, :]).then_inc(xt_written, 1)

            e_reg = [pe.alloc_register(f"expert_of_tile{u}") for u in range(UNROLL)]

            def load_expert(s, u):
                pe.reg_load(e_reg[u], expert[0:1, bass.ds(s, 1)])

            def expert_of(u):
                return pe.snap(e_reg[u], min_val=0, max_val=E - 1)

            def up(s, u):
                b2 = u % 2
                if isinstance(s, int) and s == 0:
                    load_expert(s, u)
                e = expert_of(u)
                pe.wait_ge(xlo_done, s + 1)
                pe.wait_ge(xhi_done, s + 1)
                if not (isinstance(s, int) and s < 2):
                    pe.wait_ge(gate_done, s - 1)
                for m, dst in ((0, up_i), (1, up_g)):
                    nc.tensor.matmul(dst[:, b2, :], b_sel[:, bass.ds(e * P + m * E * P, P)], b_stack[:, :],
                                     start=True, stop=False)
                    hi = w_hi[m][:, bass.ds(e * F, F)]
                    lo = w_lo[m][:, bass.ds(e * F, F)]
                    nc.tensor.matmul(dst[:, b2, :], xg_hi[:, b2, :], lo, start=False, stop=False)
                    nc.tensor.matmul(dst[:, b2, :], xg_lo[:, b2, :], hi, start=False, stop=False)
                    last = nc.tensor.matmul(dst[:, b2, :], xg_hi[:, b2, :], hi, start=False, stop=True)
                last.then_inc(up_written, 1)

            def down(s, u):
                e = expert_of(u)
                pe.wait_ge(hidT_done, s + 1)
                if not (isinstance(s, int) and s < 1):
                    pe.wait_ge(res_done, s)
                nc.tensor.matmul(y_ps[:, :], b_sel[:, bass.ds(e * P + 2 * E * P, P)], b_stack[:, 0:D],
                                 start=True, stop=False)
                for c in range(FC):
                    last = nc.tensor.matmul(y_ps[:, :], hidT[:, u % 2, c * P:(c + 1) * P],
                                            wo_sb[:, bass.ds(e * (FC * D) + c * D, D)],
                                            start=False, stop=(c == FC - 1))
                last.then_inc(y_written, 1)

            def gamma_beta(s, u):
                e = expert_of(u)
                if not (isinstance(s, int) and s < 1):
                    pe.wait_ge(z_done, s)
                nc.tensor.matmul(gb_ps[:, :], b_sel[:, bass.ds(e * P + 2 * E * P, P)], b_stack[:, D:3 * D],
                                 start=True, stop=True).then_inc(gb_written, 1)

            def transpose_h(s, u):
                pe.wait_ge(hid_done, s + 1)
                if not (isinstance(s, int) and s < 1):
                    pe.wait_ge(hidT_done, s)
                for c in range(FC):
                    last = nc.tensor.transpose(ht_ps[:, c * P:(c + 1) * P], hid[:, u % 2, c * P:(c + 1) * P],
                                               ident[:, :])
                last.then_inc(ht_written, 1)

            stages(pe, [(0, up), (-1, load_expert), (2, down), (1, transpose_h), (-2, transpose_x),
                        (3, gamma_beta)])

        @block.scalar
        def _(act):
            def activations(s, u):
                act.wait_ge(up_written, s + 1)
                if not (isinstance(s, int) and s < 2):
                    act.wait_ge(hid_done, s - 1)
                nc.scalar.activation(gelu[:, u % 2, :], up_i[:, u % 2, :], ACT.Gelu).then_inc(gelu_done, 1)
                nc.scalar.activation(gate[:, u % 2, :], up_g[:, u % 2, :], ACT.Tanh, scale=0.5)\
                    .then_inc(gate_done, 1)

            def evacuate_h(s, u):
                act.wait_ge(ht_written, s + 1)
                if not (isinstance(s, int) and s < 2):
                    act.wait_ge(y_written, s - 1)
                nc.scalar.activation(hidT[:, u % 2, :], ht_ps[:, :], ACT.Copy, scale=0.5).then_inc(hidT_done, 1)

            def high_x(s, u):
                act.wait_ge(xt_written, s + 1)
                if not (isinstance(s, int) and s < 2):
                    act.wait_ge(up_written, s - 1)
                nc.scalar.activation(xg_hi[:, u % 2, :], xt_ps[:, :], ACT.Copy).then_inc(xhi_done, 1)

            stages(act, [(0, activations), (1, evacuate_h), (-2, high_x)])

        @block.vector
        def _(dve):
            V = nc.vector

            def product(s, u):
                dve.wait_ge(gelu_done, s + 1)
                dve.wait_ge(gate_done, s + 1)
                if not (isinstance(s, int) and s < 2):
                    dve.wait_ge(ht_written, s - 1)
                V.scalar_tensor_tensor(hid[:, u % 2, :], gate[:, u % 2, :], 1.0, gelu[:, u % 2, :], ALU.add,
                                       ALU.mult).then_inc(hid_done, 1)

            def low_x(s, u):
                dve.wait_ge(xhi_done, s + 1)
                if not (isinstance(s, int) and s < 2):
                    dve.wait_ge(up_written, s - 1)
                V.tensor_tensor(xg_lo[:, u % 2, :], xt_ps[:, :], xg_hi[:, u % 2, :].bitcast(F32),
                                ALU.subtract).then_inc(xlo_done, 1)

            def take_rows(s, u):
                V.tensor_copy(from_row[:, u:u + 1], table[:, bass.ds(s, 1), 0]).then_inc(idx_done, 1)

            def residual(s, u):
                dve.wait_ge(gathered[u], rounds(s, u, NX))
                dve.wait_ge(y_written, s + 1)
                V.tensor_tensor(res[:, u % NR, :], y_ps[:, :], xg[:, u, :], ALU.add).then_inc(res_done, 1)

            def statistics(s, u):
                dve.wait_ge(res_done, s + 1)
                V.bn_stats(st6[:, u % 2, :], res[:, u % NR, :]).then_inc(x_chain, 1)

            def mean_and_variance(s, u):
                wait_apart(dve, x_chain, 2 * s + 1)
                V.bn_aggr(mean_var[:, u % NR, :], st6[:, u % 2, :]).then_inc(x_chain, 1)

            def add_epsilon(s, u):
                dve.wait_ge(x_chain, 2 * s + 2)
                V.tensor_scalar(inv_dev[:, u % NR:u % NR + 1], mean_var[:, u % NR, 1:2], EXPERT_EPS, None, ALU.add)\
                    .then_inc(ve_done, 1)

            def scale(s, u):
                r = u % NR
                if not (isinstance(s, int) and s < NR):
                    dve.wait_ge(scattered[r], rounds(s, u, NR) - 16)
                V.tensor_copy(to_row[:, r:r + 1], table[:, bass.ds(s, 1), 1])
                dve.wait_ge(gb_written, s + 1)
                V.scalar_tensor_tensor(z[:, r, :], res[:, r, :], mean_var[:, r, 0:1], gb_ps[:, 0:D], ALU.subtract,
                                       ALU.mult).then_inc(z_chain, 1)

            def shift(s, u):
                r = u % NR
                dve.wait_ge(z_chain, s + 1)
                dve.wait_ge(dev_done, s + 1)
                V.scalar_tensor_tensor(z[:, r, :], z[:, r, :], inv_dev[:, r:r + 1], gb_ps[:, D:2 * D], ALU.mult,
                                       ALU.add).then_inc(z_done, 1)

            stages(dve, [(4, scale), (-4, take_rows), (3, mean_and_variance), (4, shift), (3, add_epsilon),
                         (0, product), (2, residual), (-2, low_x), (2, statistics)])

        experts.close()
        block2 = ctx.enter_context(nc.Block())
        GROUPS = TT // NT

        @block2.sync
        def _(sp):
            y2_v = y2_d[0:2 * NTOK, :].rearrange("(g i p c) d -> g p i (c d)", p=P, i=NT, c=2)
            for g in range(GROUPS):
                if g >= NY:
                    sp.wait_ge(comb_done, g - NY + 1)
                sp.dma_start(y2[:, g % NY, :, :], y2_v[g, :, :, :]).then_inc(comb_loaded[g % NY], 16)

        @block2.scalar
        def _(act):
            out_v = out.rearrange("b (i p) d -> b p i d", p=P)
            for g in range(GROUPS):
                act.wait_ge(comb_done, g + 1)
                act.dma_start(out_v[g, :, :, :], x_all[:, g * NT:(g + 1) * NT, :]).then_inc(out_stored, 16)
            act.wait_ge(out_stored, 16 * GROUPS)

        @block2.vector
        def _(dve):
            for g in range(GROUPS):
                dve.wait_ge(comb_loaded[g % NY], 16 * (g // NY + 1))
                for c in range(2):
                    for t in range(g * NT, (g + 1) * NT):
                        last = nc.vector.scalar_tensor_tensor(
                            x_all[:, t, :], y2[:, g % NY, t % NT, c * D:(c + 1) * D], weight[:, t, c:c + 1],
                            x_all[:, t, :], ALU.mult, ALU.add)
                    if c == 0:
                        last.then_inc(c_chain, 1)
                        dve.wait_ge(c_chain, g + 1)
                last.then_inc(comb_done, 1)


_INS = ["L0_attn_x", "L0_attn_W_qkv", "L0_attn_W_out", "L0_ffn_Wr", "L0_ffn_br", "L0_ffn_Wi", "L0_ffn_bi",
        "L0_ffn_Wg", "L0_ffn_bg", "L0_ffn_Wo", "L0_ffn_bo", "L0_ffn_gamma", "L0_ffn_beta"]


def kernel(**inputs):
    import numpy as _np
    import concourse.bacc as _bacc
    from concourse import mybir as _mybir
    from concourse.bass_utils import run_bass_kernel_spmd as _run

    nc = _bacc.Bacc("TRN2", target_bir_lowering=False, num_devices=1)
    arrays, args = {}, []
    for name in _INS:
        a = _np.ascontiguousarray(inputs[name])
        arrays[name] = a
        args.append(nc.dram_tensor(name, a.shape, _mybir.dt.from_np(a.dtype), kind="ExternalInput").ap())
    shape = arrays["L0_attn_x"].shape
    out = nc.dram_tensor("out", shape, _mybir.dt.float32, kind="ExternalOutput").ap()
    attention_and_routed_experts(nc, *args, out)
    r = _run(nc, [arrays], core_ids=[0])
    return r.results[0]["out"]
```

```python
import concourse.bass as bass
from concourse import mybir
from contextlib import ExitStack


def attention_and_routed_experts(nc, x, w_qkv, w_out, wr, br, wi, bi, wg, bg, wo, bo, gamma, beta, out,
                                 BATCHES=16):
    F32, F32R, BF16, I32 = mybir.dt.float32, mybir.dt.float32r, mybir.dt.bfloat16, mybir.dt.int32
    ALU, ACT, AX = mybir.AluOpType, mybir.ActivationFunctionType, mybir.AxisListType

    B, S, D = x.shape
    NH, _, HD3 = w_qkv.shape
    HD = HD3 // 3
    E, _, F = wi.shape
    P = 128
    NT = S // P
    G = 4
    NG = NH // G
    TERMS = 3
    MROW = TERMS * G * HD
    SCALE = float(HD) ** -0.5
    LN_EPS, EXPERT_EPS = 1e-5, 1e-12
    MASK = -1e10

    ctx = ExitStack()
    with ctx:
        part = ctx

        def sb(name, shape, dt=F32):
            return part.enter_context(nc.sbuf_tensor(name, shape, dt))

        def pb(name, shape, dt=F32):
            return part.enter_context(nc.psum_tensor(name, shape, dt))

        def sem(name):
            return ctx.enter_context(nc.semaphore(name))

        xn2_d = nc.dram_tensor("xn2_scratch", (BATCHES * S, D), F32).ap()

        ident = sb("ident", [P, P])
        identb = sb("identb", [P, P], BF16)
        maskneg = sb("maskneg", [P, P], BF16)
        fold = sb("fold", [P, P // 2])
        ones_col = sb("ones_col", [P, 1])
        rowmask = sb("rowmask", [P, G])
        wq = sb("wq", [P, P])
        wk = sb("wk", [P, P])
        wv = sb("wv", [P, P])
        wout = sb("wout", [P, D])
        wsum = sb("wsum", [P, 1])
        zeros = sb("zeros", [P, S])
        minus_half = sb("minus_half", [P, 2 * NT])
        wr_sb = sb("wr_sb", [P, E])
        br_bc = sb("br_bc", [P, E])

        logits_all = sb("logits", [P, (1 + BATCHES) * NT, E])
        x_all = sb("x_all", [P, BATCHES * NT, D])

        part = attention = ExitStack()
        stats = sb("stats", [P, NT, 6])
        mv = sb("mv", [P, NT, 2])
        rstd = sb("rstd", [P, NT])
        xn = sb("xn", [P, NT, D])
        xnT = sb("xnT", [P, S])
        q_hi = sb("q_hi", [P, S], F32R)
        q_lo = sb("q_lo", [P, S], F32R)
        k_hi = sb("k_hi", [P, S], F32R)
        k_lo = sb("k_lo", [P, S], F32R)
        q_stack = sb("q_stack", [P, NG, S], F32R)
        k_stack = sb("k_stack", [P, NG, S], F32R)
        k_pad = sb("k_pad", [P, NH, S], F32R)
        v_aug = sb("v_aug", [P, NT, NH, 32])
        neg_max = sb("neg_max", [P, 2, NT, MROW + G])
        PT_OFF = [0, 512, 1024, 896]
        PT_COLS = 1280
        probs = sb("probs", [P, 2, G, PT_COLS])
        pv_sb = sb("pv_sb", [P, S])
        rden = sb("rden", [P, NT, G])
        o_masked = sb("o_masked", [P, HD, NH, NT, 2])
        attn_T = sb("attn_T", [P, S])
        stats2 = sb("stats2", [P, NT, 6])
        mv2 = sb("mv2", [P, NT, 2])
        rstd2 = sb("rstd2", [P, NT])
        xn2 = sb("xn2", [P, NT, D])
        xn2T = sb("xn2T", [P, S])
        sa = pb("sa", [P, 2, 2, S])
        st = pb("st", [P, 2, S])
        pv = pb("pv", [P, S])
        misc = pb("misc", [P, S])

        w_loaded = sem("w_loaded")
        const_a = sem("const_a")
        consts = sem("consts")
        vconst = sem("vconst")
        v_zero = sem("v_zero")
        x_first = sem("x_first")
        x_rest = sem("x_rest")
        ln1_done = sem("ln1_done")
        x1_done = sem("x1_done")
        ln2_done = sem("ln2_done")
        misc_written = sem("misc_written")
        misc_read = sem("misc_read")
        hi_done = sem("hi_done")
        lo_done = sem("lo_done")
        q_stacked = [sem(f"q_stacked{g}") for g in range(NG)]
        k_stacked = [sem(f"k_stacked{g}") for g in range(NG)]
        kpad_done = [sem(f"kpad_done{pair}") for pair in range(2)]
        var1_done, rstd1_done = sem("var1_done"), sem("rstd1_done")
        var2_done, rstd2_done = sem("var2_done"), sem("rstd2_done")
        sa_written = sem("sa_written")
        sa_read = sem("sa_read")
        st_written = sem("st_written")
        exp_done = sem("exp_done")
        masked = sem("masked")
        pv_written = sem("pv_written")
        pv_read = sem("pv_read")
        vaug_done = sem("vaug_done")
        act_sb = sem("act_sb")
        om_done = sem("om_done")
        logits_done = sem("logits_done")
        dve_chain = sem("dve_chain")
        xn2_stored = sem("xn2_stored")

        PHASE1 = ("A0 ln A1 xn mT PV0 B0 pad0 PV1 B1 A2 B2 A3 xT B3 B4 PV2 Q B5 PV3 B6 A4 B7 OT pad2 A5 "
                  "B8 pad1 A6 pad3 B9 K B10 A7 B11")
        PHASE2 = ("A0 A1 mT PV0 B0 PV1 B1 PV2 PV3 B2 zT A2 pad0 B3 A3 B4 B5 OT B6 A4 B7 LG B8 A5 B9 B10 "
                  "pad1 pad2 A6 A7 B11 pad3")
        PHASE3 = ("A0 mT PV0 B0 A1 B1 PV1 PV2 B2 PV3 B3 pad2 A2 B4 OT A3 B5 B6 B7 A4 B8 B9 A5 pad0 pad1 "
                  "B10 pad3 B11 A6 A7")
        PHASE4 = ("A0 A1 mT PV0 PV1 PV2 PV3 B0 V OT B1 A2 B2 B3 A3 RT B4 B5 pad0 A4 out B6 B7 A5 B8 "
                  "pad1 B9 A6 B10 pad2 A7 B11 pad3 zn")
        PHASES = [((0, 2), (0, 1), (0, 0), (0, 3), PHASE1),
                  ((0, 3), (0, 2), (0, 1), (1, 0), PHASE2),
                  ((1, 0), (0, 3), (0, 2), (1, 1), PHASE3),
                  ((1, 1), (1, 0), (0, 3), (1, 2), PHASE4)]
        NEXT_BATCH = ("ln", "xn", "xT", "Q", "K", "V")

        def schedule(part):
            for a, b_, pv_, pad_, order in (PHASES[3:] if part == "head" else PHASES):
                for token in order.split():
                    kind = token.rstrip("0123456789")
                    k = int(token[len(kind):] or 0)
                    ahead, g = {"A": a, "B": b_, "mT": b_, "PV": pv_, "OT": pv_, "pad": pad_}.get(kind, (0, 0))
                    if part == "last" and (ahead or kind in NEXT_BATCH):
                        continue
                    if part == "head" and not (ahead or kind == "V"):
                        continue
                    yield kind, k, ahead, g
            if part == "last":
                yield "zT", 0, 1, 0
                yield "LG", 0, 1, 0

        def misc_uses(part):
            return [kind + str(g if kind in ("mT", "OT") else ahead) for kind, _, ahead, g in schedule(part)
                    if kind in ("mT", "OT", "xT", "Q", "K", "V", "RT", "out", "zT", "LG")]

        HEAD = ["xT0", "Q0", "K0"] + misc_uses("head")
        MISC, MISC_LAST = misc_uses("loop"), misc_uses("last")

        def use(name, b):
            if isinstance(b, int) and b < 0:
                return HEAD.index(name) + 1
            order = MISC_LAST if isinstance(b, int) and b == BATCHES - 1 else MISC
            return b * len(MISC) + (len(HEAD) + order.index(name) + 1)

        NA, NB_ = 2 * NT, 3 * G

        def passes(eng, body, n):
            body(-1, "head")
            if n > 1:
                with eng.Fori(0, n - 1) as b:
                    body(b, "loop")
            body(n - 1, "last")

        def wait_apart(eng, sem_, value):
            if not isinstance(value, int):
                value = eng.to_reg(value)
                eng.wait_ge(consts, 2)
            eng.wait_ge(sem_, value)

        block = attention.enter_context(nc.Block())

        @block.sync
        def _(sp):
            def load_x(batch, loaded):
                sp.dma_start(x_all[:, batch * NT:(batch + 1) * NT, :],
                             x[batch, :, :].rearrange("(i p) d -> p i d", p=P)).then_inc(loaded, 16)

            load_x(0, x_first)
            qkv_v = w_qkv.rearrange("n d h -> d n h")
            for w, c in ((wq, 0), (wk, 1), (wv, 2)):
                sp.dma_start(w[:, :].rearrange("d (n h) -> d n h", h=HD),
                             qkv_v[:, :, c * HD:(c + 1) * HD]).then_inc(w_loaded, 16)
            sp.dma_start(wout[:, :], w_out.rearrange("n h d -> (n h) d")).then_inc(w_loaded, 16)
            sp.dma_start(wr_sb[:, :], wr).then_inc(w_loaded, 16)
            sp.dma_start(br_bc[:, :], br.rearrange("(a e) -> a e", a=1).broadcast_to([P, E])).then_inc(w_loaded, 16)

            def stack(nb, first):
                for g in range(NG):
                    if g == 0:
                        wait_apart(sp, hi_done, 2 * nb + 2)
                        wait_apart(sp, lo_done, 2 * nb + 2)
                    if not first:
                        wait_apart(sp, st_written, (nb - 1) * (NG * NB_) + NB_ * (g + 1))
                        for done in kpad_done:
                            wait_apart(sp, done, (nb - 1) * (NH // 2) + (G // 2) * (g + 1))
                    for c in range(TERMS):
                        rows = slice(32 * c, 32 * c + 32)
                        src = slice(32 * g, 32 * g + 32)
                        sp.dma_start(k_stack[rows, g, :].bitcast(F32), (k_hi, k_hi, k_lo)[c][src, :].bitcast(F32))\
                            .then_inc(k_stacked[g], 16)
                    sp.dma_start(q_stack[MROW:P, g, :].bitcast(F32), zeros[MROW:P, :]).then_inc(q_stacked[g], 16)
                    for c in range(TERMS):
                        rows = slice(32 * c, 32 * c + 32)
                        src = slice(32 * g, 32 * g + 32)
                        sp.dma_start(q_stack[rows, g, :].bitcast(F32), (q_hi, q_lo, q_hi)[c][src, :].bitcast(F32))\
                            .then_inc(q_stacked[g], 16)

            def body(b, part):
                if part == "head":
                    return
                if part == "loop":
                    stack(b + 1, False)
                rows = xn2_d.rearrange("(b i p) d -> b p i d", p=P, i=NT)
                wait_apart(sp, ln2_done, b + 2)
                sp.dma_start(rows[b, :, :, :], xn2[:, :, :]).then_inc(xn2_stored, 16)

            sp.wait_ge(consts, 2)
            stack(0, True)
            for batch in range(1, BATCHES):
                load_x(batch, x_rest)
            passes(sp, body, BATCHES)
            sp.wait_ge(xn2_stored, 16 * BATCHES + 1)

        @block.gpsimd
        def _(pool):
            n = 0

            def c_(ins):
                nonlocal n
                n += 1
                ins.then_inc(const_a, 1)
                pool.wait_ge(const_a, n)

            c_(pool.memset(ident[:, :], 0.0))
            c_(pool.affine_select(out=ident[:, :], in_=ident[:, :], compare_op=ALU.not_equal, fill=1.0, base=0,
                                  pattern=[[-1, P]], channel_multiplier=1))
            c_(pool.tensor_copy(identb[:, :], ident[:, :]))
            c_(pool.memset(maskneg[:, :], 0.0))
            c_(pool.affine_select(out=maskneg[:, :], in_=maskneg[:, :], compare_op=ALU.is_ge, fill=MASK, base=0,
                                  pattern=[[-1, P]], channel_multiplier=1))
            c_(pool.memset(fold[:, :], 0.0))
            for half in (0, -P // 2):
                c_(pool.affine_select(out=fold[:, :], in_=fold[:, :], compare_op=ALU.not_equal, fill=1.0, base=half,
                                      pattern=[[-1, P // 2]], channel_multiplier=1))
            c_(pool.memset(ones_col[:, :], 1.0))
            c_(pool.memset(rowmask[:, :], 1.0))
            for c in range(TERMS):
                part = rowmask[32 * c:32 * c + 32, :]
                c_(pool.affine_select(out=part, in_=part, compare_op=ALU.is_ge, fill=0.0, base=0,
                                      pattern=[[-HD, G]], channel_multiplier=1))
                c_(pool.affine_select(out=part, in_=part, compare_op=ALU.is_ge, fill=0.0, base=HD - 1,
                                      pattern=[[HD, G]], channel_multiplier=-1))
            part = rowmask[MROW:P, :]
            c_(pool.memset(part, 0.0))
            c_(pool.affine_select(out=part, in_=part, compare_op=ALU.not_equal, fill=1.0, base=0,
                                  pattern=[[-1, G]], channel_multiplier=1))
            c_(pool.memset(minus_half[:, :], -0.5))
            pool.sem_inc(consts, 1)
            pool.wait_ge(consts, 2)

            def causal_zeros(nb, g, j):
                wait_apart(pool, exp_done, nb * (NG * NB_) + NB_ * g + 3 * (j + 1))
                for off, n_ in ((PT_OFF[0], 1), (PT_OFF[1], 1), (PT_OFF[3], 2)):
                    blk = probs[:, g % 2, j, off:off + n_ * P].rearrange("p (a q) -> p a q", q=P)
                    pool.affine_select(out=blk, in_=blk, compare_op=ALU.is_ge, fill=0.0, base=0,
                                       pattern=[[0, n_], [1, P]], channel_multiplier=-1).then_inc(masked, 1)

            def inverse_deviation(batch, var_done, rstd_done, rs_):
                pool.wait_ge(var_done, batch + 1)
                pool.tensor_tensor(rs_[:, :], rs_[:, :], minus_half[:, 0:NT], ALU.pow).then_inc(rstd_done, 1)

            def body(b, part):
                for kind, k, ahead, g in schedule(part):
                    if kind == "ln":
                        inverse_deviation(b + 1, var1_done, rstd1_done, rstd)
                    elif kind == "B" and k % 3 == 2:
                        causal_zeros(b + ahead, g, k // 3)
                    elif kind == "out":
                        inverse_deviation(b, var2_done, rstd2_done, rstd2)

            inverse_deviation(0, var1_done, rstd1_done, rstd)
            passes(pool, body, BATCHES)

        @block.tensor
        def _(pe):
            pe.wait_ge(w_loaded, 16 * 6)
            pe.wait_ge(consts, 2)

            def misc_free(name, b):
                pe.wait_ge(misc_read, use(name, b) - 1)

            def transposes(src):
                for i in range(NT):
                    last = nc.tensor.transpose(misc[:, i * P:(i + 1) * P], src(i), ident[:, :])
                last.then_inc(misc_written, 1)

            def transpose_xn(b):
                if not (isinstance(b, int) and b < 0):
                    misc_free("xT0", b)
                pe.wait_ge(ln1_done, b + 2)
                transposes(lambda i: xn[:, i, :])

            def project(name, w, b):
                misc_free(name, b)
                nc.tensor.matmul(misc[:, :], w[:, :], xnT[:, :], start=True, stop=True).then_inc(misc_written, 1)

            def a_step(nb, g, s):
                i, pair = NT - 1 - s // 2, s % 2
                n = nb * (NG * NA) + NA * g + s
                if s == 0:
                    pe.wait_ge(q_stacked[g], 16 * (TERMS + 1) * (nb + 1))
                if s < 2:
                    pe.wait_ge(kpad_done[pair], nb * (NH // 2) + (G // 2) * (g + 1))
                if not (isinstance(nb, int) and nb == 0 and g == 0 and s < 2):
                    pe.wait_ge(sa_read, n - 1)
                width = max(2 * P, P * (i + 1))
                for h in range(2):
                    nc.tensor.matmul(sa[:, s % 2, h, 0:width], q_stack[:, g, i * P:(i + 1) * P],
                                     k_pad[:, G * g + 2 * pair + h, 0:width], start=True, stop=True)
                    last = nc.tensor.matmul(sa[:, s % 2, h, i * P:(i + 1) * P], identb[:, :], maskneg[:, :],
                                            start=False, stop=True, skip_group_check=True)
                last.then_inc(sa_written, 1)

            def b_step(nb, g, t):
                j, part = t // 3, t % 3
                n = nb * (NG * NB_) + NB_ * g + t
                if t == 0:
                    pe.wait_ge(act_sb, nb * NG + g + 1)
                if not (isinstance(nb, int) and nb == 0 and g == 0 and t < 2):
                    pe.wait_ge(exp_done, n - 1)
                h = G * g + j
                buf = st[:, t % 2, :]
                if part == 0:
                    mm = [(0, 0, 512)]
                elif part == 1:
                    mm = [(1, 0, 384)]
                else:
                    mm = [(3, 0, 256), (2, 256, 256)]
                for kk, at, w in mm:
                    last = nc.tensor.matmul(buf[:, at:at + w], k_pad[:, h, kk * P:(kk + 1) * P],
                                            q_stack[:, g, S - w:S], start=True, stop=True)
                last.then_inc(st_written, 1)

            def pv_part(b, g, kk):
                if kk == 0:
                    pe.wait_ge(masked, b * (NG * NB_) + NB_ * (g + 1))
                    pe.wait_ge(vaug_done, b + 1)
                    pe.wait_ge(pv_read, b * NG + g + 1)
                for j in range(G):
                    w = S - kk * P
                    last = nc.tensor.matmul(pv[32 * j:32 * j + 32, kk * P:S], v_aug[:, kk, G * g + j, :],
                                            probs[:, g % 2, j, PT_OFF[kk]:PT_OFF[kk] + w],
                                            start=(kk == 0), stop=True, skip_group_check=True)
                if kk == NT - 1:
                    last.then_inc(pv_written, 1)

            def body(b, part):
                for kind, k, ahead, g in schedule(part):
                    if kind == "A":
                        a_step(b + ahead, g, k)
                    elif kind == "mT":
                        misc_free(f"mT{g}", b)
                        pe.wait_ge(sa_read, (b + ahead) * (NG * NA) + NA * (g + 1))
                        for i in range(NT):
                            last = nc.tensor.transpose(misc[0:MROW + G, i * P:(i + 1) * P],
                                                       neg_max[:, g % 2, i, :], ident[:, :])
                        last.then_inc(misc_written, 1)
                    elif kind == "B":
                        b_step(b + ahead, g, k)
                    elif kind == "PV":
                        pv_part(b, g, k)
                    elif kind == "xT":
                        transpose_xn(b)
                    elif kind in ("Q", "K"):
                        project(kind + "0", wq if kind == "Q" else wk, b)
                    elif kind == "V":
                        misc_free("V0", b)
                        for i in range(NT):
                            last = nc.tensor.matmul(misc[:, i * P:(i + 1) * P], xnT[:, i * P:(i + 1) * P], wv[:, :],
                                                    start=True, stop=True)
                        last.then_inc(misc_written, 1)
                    elif kind == "OT":
                        misc_free(f"OT{g}", b)
                        pe.wait_ge(pv_read, b * NG + g + 2)
                        transposes(lambda i: pv_sb[:, i * P:(i + 1) * P])
                    elif kind == "RT":
                        misc_free("RT0", b)
                        pe.wait_ge(om_done, (b + 1) * NG)
                        for h in range(HD):
                            last = nc.tensor.matmul(misc[:, h * (P // 2):(h + 1) * (P // 2)],
                                                    o_masked[:, h, :, :, :].rearrange("p n i c -> p (n i c)"),
                                                    fold[:, :], start=True, stop=True)
                        last.then_inc(misc_written, 1)
                    elif kind == "out":
                        misc_free("out0", b)
                        transposes(lambda i: attn_T[:, i * P:(i + 1) * P])
                    elif kind == "zT":
                        misc_free(f"zT{ahead}", b)
                        pe.wait_ge(ln2_done, b + ahead + 1)
                        transposes(lambda i: xn2[:, i, :])
                    elif kind == "LG":
                        misc_free(f"LG{ahead}", b)
                        for i in range(NT):
                            last = nc.tensor.matmul(misc[:, i * E:(i + 1) * E], xn2T[:, i * P:(i + 1) * P],
                                                    wr_sb[:, :], start=True, stop=True)
                        last.then_inc(misc_written, 1)

            nc.tensor.matmul(st[:, 1, 0:1], wout[:, :], ones_col[:, :], start=True, stop=True).then_inc(vconst, 1)
            transpose_xn(-1)
            project("Q0", wq, -1)
            project("K0", wk, -1)
            pe.wait_ge(consts, 3)
            for s in range(NA):
                a_step(0, 0, s)
            passes(pe, body, BATCHES)

        @block.scalar
        def _(act):
            act.wait_ge(consts, 2)

            def copy_misc(name, b, out_):
                act.wait_ge(misc_written, use(name, b))
                nc.scalar.activation(out_, misc[:, :], ACT.Copy).then_inc(misc_read, 1)

            def high_part(name, b, out_, scale):
                act.wait_ge(misc_written, use(name, b))
                nc.scalar.activation(out_, misc[:, :], ACT.Copy, scale=scale).then_inc(hi_done, 1)

            def body(b, part):
                for kind, k, ahead, g in schedule(part):
                    if kind == "xT":
                        copy_misc("xT0", b, xnT[:, :])
                    elif kind in ("Q", "K"):
                        if kind == "Q":
                            for c in range(NG):
                                act.wait_ge(q_stacked[c], 16 * (TERMS + 1) * (b + 1))
                                act.wait_ge(k_stacked[c], 16 * TERMS * (b + 1))
                        high_part(kind + "0", b, *((q_hi[:, :], SCALE) if kind == "Q" else (k_hi[:, :], 1.0)))
                    elif kind == "V":
                        act.wait_ge(misc_written, use("V0", b))
                        if part != "head":
                            act.wait_ge(pv_written, (b + 1) * NG)
                        nc.scalar.activation(v_aug[:, :, :, 0:HD],
                                             misc[:, :].rearrange("p (i n h) -> p i n h", i=NT, h=HD),
                                             ACT.Copy).then_inc(vaug_done, 1)
                        act.wait_ge(vaug_done, b + 2)
                        act.sem_inc(misc_read, 1)
                    elif kind == "mT":
                        act.wait_ge(misc_written, use(f"mT{g}", b))
                        nc.scalar.activation(q_stack[MROW:MROW + G, g, :], misc[MROW:MROW + G, :],
                                             ACT.Copy).then_inc(act_sb, 1)
                        act.wait_ge(act_sb, (b + ahead) * NG + g + 1)
                        act.sem_inc(misc_read, 1)
                    elif kind == "B":
                        j, third = k // 3, k % 3
                        act.wait_ge(st_written, (b + ahead) * (NG * NB_) + NB_ * g + k + 1)
                        lo, w, at = ((0, 512, 0), (512, 384, 0), (896, 384, 128))[third]
                        nc.scalar.activation(probs[:, g % 2, j, lo:lo + w], st[:, k % 2, at:at + w],
                                             ACT.Exp).then_inc(exp_done, 1)
                    elif kind == "PV" and k == NT - 1:
                        act.wait_ge(pv_written, b * NG + g + 1)
                        if g > 0:
                            act.wait_ge(misc_written, use(f"OT{g - 1}", b))
                        nc.scalar.activation(pv_sb[:, :], pv[:, :], ACT.Copy).then_inc(pv_read, 1)
                    elif kind == "RT":
                        act.wait_ge(misc_written, use("RT0", b))
                        nc.scalar.activation(attn_T[:, :].rearrange("p (r h) -> p h r", h=HD),
                                             misc[:, :].rearrange("p (h r) -> p h r", h=HD),
                                             ACT.Copy, scale=wsum[:, 0:1]).then_inc(misc_read, 1)
                    elif kind == "pad" and k >= G // 2:
                        pad_key(b + ahead, g, k)
                    elif kind == "zT":
                        copy_misc(f"zT{ahead}", b, xn2T[:, :])

            def pad_key(nb, g, j):
                if j == G // 2:
                    act.wait_ge(k_stacked[g], 16 * TERMS * (nb + 1))
                nc.scalar.activation(k_pad[:, G * g + j, :], k_stack[:, g, :].bitcast(F32), ACT.Copy,
                                     scale=rowmask[:, j:j + 1]).then_inc(kpad_done[1], 1)

            act.sem_inc(pv_read, 1)
            act.sem_inc(xn2_stored, 1)
            act.sem_inc(ln2_done, 1)
            copy_misc("xT0", -1, xnT[:, :])
            high_part("Q0", -1, q_hi[:, :], SCALE)
            high_part("K0", -1, k_hi[:, :], 1.0)
            for g in range(2):
                for j in range(G // 2, G):
                    pad_key(0, g, j)
            passes(act, body, BATCHES)

        @block.vector
        def _(dve):
            nc.vector.memset(k_stack[MROW:P, :, :].bitcast(F32), 1.0)
            nc.vector.memset(neg_max[:, :, :, :], 0.0)
            nc.vector.memset(v_aug[:, :, :, :], 0.0).then_inc(v_zero, 1)
            nc.vector.memset(xn2[:, :, :], 0.0)
            nc.vector.memset(o_masked[:, :, :, :, :], 0.0)
            dve.wait_ge(v_zero, 1)
            nc.vector.memset(v_aug[:, :, :, HD:HD + 1], 1.0)
            nc.vector.memset(zeros[:, :], 0.0).then_inc(consts, 1)
            dve.wait_ge(consts, 2)

            BEFORE, PER_PASS = 2, 2 + NG + 2
            done = [0]

            def link(ins, b, apart=False):
                done[0] += 1
                ins.then_inc(dve_chain, 1)
                if isinstance(b, int) and b < 0:
                    dve.wait_ge(dve_chain, done[0])
                elif apart:
                    wait_apart(dve, dve_chain, b * PER_PASS + (BEFORE + done[0]))
                else:
                    dve.wait_ge(dve_chain, b * PER_PASS + (BEFORE + done[0]))

            def x_of(batch, i):
                return x_all[:, bass.ds(batch * NT + i, 1), :].rearrange("p a d -> p (a d)")

            def statistics(batch, st_, mv_, rs_, b, var_done):
                for i in range(NT):
                    last = nc.vector.bn_stats(st_[:, i, :], x_of(batch, i))
                link(last, b, apart=True)
                for i in range(NT):
                    last = nc.vector.bn_aggr(mv_[:, i, :], st_[:, i, :])
                link(last, b)
                nc.vector.tensor_scalar(rs_[:, :], mv_[:, :, 1], LN_EPS, None, ALU.add).then_inc(var_done, 1)

            def normalise(batch, dst, mv_, rs_, rstd_done, ready):
                dve.wait_ge(rstd_done, batch + 1)
                for i in range(NT):
                    last = nc.vector.tensor_scalar(dst[:, i, :], x_of(batch, i), mv_[:, i, 0:1], rs_[:, i:i + 1],
                                                   ALU.subtract, ALU.mult)
                last.then_inc(ready, 1)

            def low_part(name, b):
                hi, lo, scale, k = (q_hi, q_lo, SCALE, 1) if name == "Q" else (k_hi, k_lo, 1.0, 2)
                dve.wait_ge(hi_done, 2 * (b + 1) + k)
                nc.vector.scalar_tensor_tensor(lo[:, :], misc[:, :], scale, hi[:, :].bitcast(F32),
                                               ALU.mult, ALU.subtract).then_inc(lo_done, 1)
                dve.wait_ge(lo_done, 2 * (b + 1) + k)
                dve.sem_inc(misc_read, 1)

            def pad_key(nb, g, j):
                if j == 0:
                    dve.wait_ge(k_stacked[g], 16 * TERMS * (nb + 1))
                nc.vector.tensor_scalar(k_pad[:, G * g + j, :], k_stack[:, g, :].bitcast(F32), rowmask[:, j:j + 1],
                                        None, ALU.mult).then_inc(kpad_done[0], 1)

            def reduce_step(nb, g, s):
                i, pair = NT - 1 - s // 2, s % 2
                if s == 0 and not (isinstance(nb, int) and nb == 0 and g < 2):
                    dve.wait_ge(act_sb, nb * NG + g - 1)
                dve.wait_ge(sa_written, nb * (NG * NA) + NA * g + s + 1)
                nc.vector.tensor_reduce(neg_max[:, g % 2, i, MROW + 2 * pair:MROW + 2 * pair + 2],
                                        sa[:, s % 2, :, 0:(i + 1) * P], AX.X, ALU.max,
                                        negate=True).then_inc(sa_read, 1)

            def body(b, part):
                done[0] = 0
                for kind, k, ahead, g in schedule(part):
                    if kind == "A":
                        reduce_step(b + ahead, g, k)
                    elif kind == "pad" and k < G // 2:
                        pad_key(b + ahead, g, k)
                    elif kind == "ln":
                        dve.wait_ge(x_rest, 16 * (BATCHES - 1))
                        statistics(b + 1, stats, mv, rstd, b, var1_done)
                    elif kind == "xn":
                        normalise(b + 1, xn, mv, rstd, rstd1_done, ln1_done)
                    elif kind in ("Q", "K"):
                        low_part(kind, b)
                    elif kind == "OT":
                        dve.wait_ge(misc_written, use(f"OT{g}", b))
                        ot = misc[:, :].rearrange("p (i j c) -> p i j c", i=NT, j=G)
                        link(nc.vector.reciprocal(rden[:, :, :], ot[:, :, :, HD]), b)
                        for c in range(2):
                            half = slice(c * (P // 2), (c + 1) * (P // 2))
                            dst = o_masked[half, :, G * g:G * g + G, :, c].rearrange("p h j i -> p i j h")
                            last = nc.vector.tensor_tensor(
                                dst, ot[half, :, :, 0:HD],
                                rden[half, :, :].unsqueeze(3).broadcast_to([P // 2, NT, G, HD]), ALU.mult)
                        last.then_inc(om_done, 1)
                        dve.wait_ge(om_done, b * NG + g + 1)
                        dve.sem_inc(misc_read, 1)
                    elif kind == "out":
                        dve.wait_ge(misc_written, use("out0", b))
                        rows = x_all[:, bass.ds(b * NT, NT), :]
                        nc.vector.tensor_tensor(rows, misc[:, :].rearrange("p (i d) -> p i d", i=NT),
                                                rows, ALU.add).then_inc(x1_done, 1)
                        wait_apart(dve, x1_done, b + 1)
                        dve.sem_inc(misc_read, 1)
                        statistics(b, stats2, mv2, rstd2, b, var2_done)
                    elif kind == "zn":
                        dve.wait_ge(xn2_stored, 16 * b + 1)
                        normalise(b, xn2, mv2, rstd2, rstd2_done, ln2_done)
                    elif kind == "LG":
                        dve.wait_ge(misc_written, use(f"LG{ahead}", b))
                        nc.vector.tensor_tensor(logits_all[:, bass.ds((b + ahead) * NT, NT), :],
                                                misc[:, 0:NT * E].rearrange("p (i e) -> p i e", i=NT),
                                                br_bc[:, :].unsqueeze(1).broadcast_to([P, NT, E]),
                                                ALU.add).then_inc(logits_done, 1)
                        dve.wait_ge(logits_done, b + ahead + 1)
                        dve.sem_inc(misc_read, 1)
                assert part != "loop" or done[0] == PER_PASS, done

            dve.wait_ge(x_first, 16)
            statistics(0, stats, mv, rstd, -1, var1_done)
            normalise(0, xn, mv, rstd, rstd1_done, ln1_done)
            low_part("Q", -1)
            low_part("K", -1)
            dve.wait_ge(vconst, 1)
            nc.vector.tensor_copy(wsum[:, :], st[:, 1, 0:1]).then_inc(consts, 1)
            for g in range(2):
                for j in range(G // 2):
                    pad_key(0, g, j)
            for s in range(NA):
                reduce_step(0, 0, s)
            passes(dve, body, BATCHES)

        attention.close()
        part = ctx
        logits = logits_all[:, NT:, :]
        TT = BATCHES * NT
        NTOK = TT * P
        UNROLL = 8
        BR = 2 * P
        BLOCKS = -(-(TT + E - 1) // UNROLL) * UNROLL
        TILES = 2 * BLOCKS
        FC = F // P
        BIG = 2.0 * E
        OH, NOH = 4, 4

        y2_d = nc.dram_tensor("y2_scratch", (2 * NTOK + TILES * P, D), F32).ap()

        w_hi = [sb(n, [P, E * F], F32R) for n in ("wi_hi", "wg_hi")]
        w_lo = [sb(n, [P, E * F], F32R) for n in ("wi_lo", "wg_lo")]
        wo_sb = sb("wo_sb", [P, E * FC * D])
        b_stack = sb("b_stack", [P, 3 * D], BF16)
        b_sel = sb("b_sel", [P, E * P], BF16)
        b_up = sb("b_up", [P, 2, E * FC])
        upper = sb("upper", [P, P], BF16)
        onesb = sb("onesb", [P, P], BF16)
        iota_e = sb("iota_e", [P, E])
        iota_p = sb("iota_p", [P, P])
        iota_s = sb("iota_s", [P, TILES])
        iota_t = sb("iota_t", [P, TT])
        value = sb("value", [P, TT, 2])
        slot_id = sb("slot_id", [P, TILES])
        weight = sb("weight", [P, TT, 2])
        row_f = sb("row_f", [P, TT * 2])
        tile_f = sb("tile_f", [P, TT * 2])
        table = sb("table", [P, TILES, 2], I32)
        expert = sb("expert", [P, BLOCKS], I32)

        route = part = ExitStack()
        b_rows = sb("b_rows", [2 * E * FC, P])
        one_r = sb("one_r", [P, NOH, OH, P])
        one_s = sb("one_s", [P, NOH, OH, TILES], BF16)
        one_v = sb("one_v", [P, NOH, OH, TILES])
        b_all = sb("b_all", [P, 3 * D])
        b_part = sb("b_part", [P, 3, 3 * D], BF16)
        b_rest = sb("b_rest", [P, 3 * D])
        stage = sb("stage", [P, 4, F])
        iota_i = sb("iota_i", [P, max(2 * TT, TILES, P)], I32)
        shifted = sb("shifted", [P, TT, E])
        ex = sb("ex", [P, TT, E])
        pr = sb("pr", [P, TT, E])
        pr2 = sb("pr2", [P, TT, E])
        tmp = sb("tmp", [P, TT, E])
        oh = [sb(f"oh{c}", [P, TT, E]) for c in range(2)]
        chosen = sb("chosen", [P, TT, E], BF16)
        mx = sb("mx", [P, TT])
        sm = sb("sm", [P, TT])
        pm = sb("pm", [P, TT, 2])
        first = sb("first", [P, TT])
        tot = sb("tot", [P, E, TT])
        cum = sb("cum", [P, E, TT])
        cmp_ = sb("cmp_", [P, E, TT])
        one_t = sb("one_t", [P, E * TT])
        slot = sb("slot", [P, E, TT])
        count = sb("count", [P, E])
        start = sb("start", [P, E])
        ntile = sb("ntile", [P, E])
        tend = sb("tend", [P, E])
        base = sb("base", [P, E])
        slot2 = sb("slot2", [P, TT, 2])
        slot_i = sb("slot_i", [P, TT, 2], I32)
        part_i = sb("part_i", [P, TT, 2], I32)
        cmp_s = sb("cmp_s", [P, BLOCKS, E])
        exp_f = sb("exp_f", [P, BLOCKS])
        tab_f = sb("tab_f", [P, 3, TILES])
        tab_i = sb("tab_i", [P, TILES], I32)

        counts_ps = pb("counts_ps", [P, 2, TT * E])
        table_ps = pb("table_ps", [P, TILES])
        b_up_ps = pb("b_up_ps", [P, 2 * E * FC])

        r_const = sem("r_const")
        stage_loaded = [sem(f"stage_loaded{k}") for k in range(4)]
        w_hi_done = sem("w_hi_done")
        w_lo_done = sem("w_lo_done")
        bias_loaded = sem("bias_loaded")
        ffn_loaded = sem("ffn_loaded")
        bias_done = sem("bias_done")
        r_chain = sem("r_chain")
        shifted_done = sem("shifted_done")
        exp_ready = sem("exp_ready")
        chosen_done = sem("chosen_done")
        counts_done = sem("counts_done")
        onehot_done = sem("onehot_done")
        onehot_scaled = sem("onehot_scaled")
        b_rows_loaded, b_up_written = sem("b_rows_loaded"), sem("b_up_written")
        onehot_used = sem("onehot_used")
        table_done = sem("table_done")
        table_zero = sem("table_zero")

        made = {}

        block = route.enter_context(nc.Block())

        @block.sync
        def _(sp):
            for m, src in enumerate((bi, bg)):
                sp.dma_start(b_rows[m * E * FC:(m + 1) * E * FC, :], src.rearrange("e (c p) -> (e c) p", p=P))\
                    .then_inc(b_rows_loaded, 16)
            for k in range(2 * E):
                m, e = k // E, k % E
                if k >= 4:
                    sp.wait_ge(w_lo_done, k - 3)
                sp.dma_start(stage[:, k % 4, :], (wi, wg)[m][e, :, :]).then_inc(stage_loaded[k % 4], 16)
                if k == 3:
                    sp.wait_ge(bias_done, 1)
                    for c in range(3):
                        for m, src in enumerate((bo, gamma, beta)):
                            sp.dma_start(b_all[32 * c:32 * c + E, m * D:(m + 1) * D], src).then_inc(bias_loaded, 16)
            for e in range(E):
                sp.dma_start(wo_sb[:, e * FC * D:(e + 1) * FC * D].rearrange("p (c d) -> p c d", c=FC),
                             wo[e, :, :].rearrange("(c p) d -> p c d", p=P)).then_inc(ffn_loaded, 16)
            sp.wait_ge(ffn_loaded, 16 * E)

        @block.gpsimd
        def _(pool):
            n = 0

            def c_(ins):
                nonlocal n
                n += 1
                ins.then_inc(r_const, 1)
                pool.wait_ge(r_const, n)

            def iota(dst, width, step, base_, mult):
                c_(pool.iota(iota_i[:, 0:width], pattern=[[step, width]], base=base_, channel_multiplier=mult))
                c_(pool.tensor_copy(dst, iota_i[:, 0:width]))

            iota(iota_e[:, :], E, 1, 0, 0)
            made["iota_e"] = n
            c_(pool.memset(upper[:, :], 1.0))
            c_(pool.affine_select(out=upper[:, :], in_=upper[:, :], compare_op=ALU.is_gt, fill=0.0, base=0,
                                  pattern=[[1, P]], channel_multiplier=-1))
            c_(pool.memset(onesb[:, :], 1.0))
            made["upper, onesb"] = n
            c_(pool.memset(one_t[:, :], 1.0))
            iota(iota_t[:, :], TT, BR, 0, 0)
            made["one_t, iota_t"] = n
            iota(iota_p[:, :], P, 1, 0, 0)
            iota(iota_s[:, :], TILES, 1, 0, 0)
            c_(pool.iota(iota_i[:, 0:2 * TT], pattern=[[2 * P, TT], [1, 2]], base=1, channel_multiplier=2))
            c_(pool.tensor_copy(value[:, :, :].rearrange("p t c -> p (t c)"), iota_i[:, 0:2 * TT]))
            made["iota_p, iota_s, value"] = n
            for k in range(2 * E):
                m, e = k // E, k % E
                pool.wait_ge(w_hi_done, k + 1)
                pool.tensor_tensor(w_lo[m][:, e * F:(e + 1) * F], stage[:, k % 4, :],
                                   w_hi[m][:, e * F:(e + 1) * F].bitcast(F32), ALU.subtract).then_inc(w_lo_done, 1)
            c_(pool.memset(b_stack[:, :], 0.0))
            pool.wait_ge(bias_loaded, 16 * 9)
            c_(pool.tensor_scalar(b_all[:, 0:D], b_all[:, 0:D], 2.0, None, ALU.mult))
            c_(pool.tensor_copy(b_part[:, 0, :], b_all[:, :]))
            c_(pool.tensor_tensor(b_rest[:, :], b_all[:, :], b_part[:, 0, :], ALU.subtract))
            c_(pool.tensor_copy(b_part[:, 1, :], b_rest[:, :]))
            c_(pool.tensor_tensor(b_all[:, :], b_rest[:, :], b_part[:, 1, :], ALU.subtract))
            c_(pool.tensor_copy(b_part[:, 2, :], b_all[:, :]))
            for c in range(3):
                c_(pool.tensor_copy(b_stack[32 * c:32 * c + E, :], b_part[32 * c:32 * c + E, c, :]))
            c_(pool.memset(b_sel[:, :], 0.0))
            for c in range(3):
                rows = b_sel[32 * c:32 * c + 32, :].rearrange("r (m q) -> r m q", q=P)
                c_(pool.affine_select(out=rows, in_=rows, compare_op=ALU.not_equal, fill=1.0, base=0,
                                      pattern=[[-1, E], [0, P]], channel_multiplier=1))
            iota(slot_id[:, :], TILES, P, 2 * NTOK + 1, 1)
            made["slot_id"] = n

        @block.scalar
        def _(act):
            act.wait_ge(shifted_done, 1)
            nc.scalar.activation(ex[:, :, :], shifted[:, :, :], ACT.Exp).then_inc(exp_ready, 1)

            def high_part(k):
                m, e = k // E, k % E
                act.wait_ge(stage_loaded[k % 4], 16 * (k // 4 + 1))
                nc.scalar.activation(w_hi[m][:, e * F:(e + 1) * F], stage[:, k % 4, :],
                                     ACT.Copy).then_inc(w_hi_done, 1)

            for k in range(2 * E):
                high_part(k)
            vals = value[:, :, :].rearrange("p t c -> p (t c)")
            with act.Fori(0, 2 * TT // (NOH * OH)) as t:
                for u in range(NOH):
                    act.wait_ge(onehot_done, NOH * t + (u + 1))
                    for j in range(OH):
                        last = nc.scalar.activation(one_v[:, u, j, :], one_s[:, u, j, :], ACT.Copy,
                                                    scale=vals[:, bass.ds(t * (NOH * OH) + (u * OH + j), 1)])
                    last.then_inc(onehot_scaled, 1)

        @block.tensor
        def _(pe):
            pe.wait_ge(b_rows_loaded, 32)
            nc.tensor.transpose(b_up_ps[:, :], b_rows[:, :], ident[0:2 * E * FC, 0:2 * E * FC])\
                .then_inc(b_up_written, 1)
            pe.wait_ge(r_const, made["upper, onesb"])
            pe.wait_ge(chosen_done, 1)
            rhs = chosen[:, :, :].rearrange("p t e -> p (t e)")
            nc.tensor.matmul(counts_ps[:, 0, :], upper[:, :], rhs, start=True, stop=True)
            nc.tensor.matmul(counts_ps[:, 1, :], onesb[:, :], rhs, start=True, stop=True).then_inc(counts_done, 1)
            pe.wait_ge(table_zero, 1)
            for u in range(NOH):
                nc.tensor.matmul(table_ps[:, :], one_r[:, 0, 0, :], one_v[:, 0, 0, :], start=(u == 0), stop=True,
                                 skip_group_check=True).then_inc(onehot_used, 1)
            with pe.Fori(0, 2 * TT // (NOH * OH)) as t:
                for u in range(NOH):
                    pe.wait_ge(onehot_scaled, NOH * t + (u + 1))
                    for j in range(OH):
                        last = nc.tensor.matmul(table_ps[:, :], one_r[:, u, j, :], one_v[:, u, j, :], start=False,
                                                stop=True, skip_group_check=True)
                    last.then_inc(onehot_used, 1)

        @block.vector
        def _(dve):
            V = nc.vector
            n = 0

            def link(ins):
                nonlocal n
                n += 1
                ins.then_inc(r_chain, 1)
                dve.wait_ge(r_chain, n)

            def over_e(ap):
                return ap.unsqueeze(2).broadcast_to([P, TT, E])

            ie = iota_e[:, :].unsqueeze(1).broadcast_to([P, TT, E])
            V.memset(b_all[:, :], 0.0).then_inc(bias_done, 1)
            link(V.tensor_reduce(mx[:, :], logits[:, :, :], AX.X, ALU.max))
            V.tensor_tensor(shifted[:, :, :], logits[:, :, :], over_e(mx[:, :]), ALU.subtract).then_inc(shifted_done, 1)
            dve.wait_ge(r_const, made["iota_e"])
            dve.wait_ge(exp_ready, 1)
            link(V.tensor_reduce(sm[:, :], ex[:, :, :], AX.X, ALU.add))
            link(V.reciprocal(sm[:, :], sm[:, :]))
            link(V.tensor_tensor(pr[:, :, :], ex[:, :, :], over_e(sm[:, :]), ALU.mult))
            src = pr
            for c in range(2):
                link(V.tensor_reduce(pm[:, :, c], src[:, :, :], AX.X, ALU.max))
                link(V.tensor_tensor(tmp[:, :, :], src[:, :, :], over_e(pm[:, :, c]), ALU.is_lt))
                link(V.scalar_tensor_tensor(tmp[:, :, :], tmp[:, :, :], BIG, ie, ALU.mult, ALU.add))
                link(V.tensor_reduce(first[:, :], tmp[:, :, :], AX.X, ALU.min))
                link(V.tensor_tensor(oh[c][:, :, :], ie, over_e(first[:, :]), ALU.is_equal))
                if c == 0:
                    link(V.scalar_tensor_tensor(pr2[:, :, :], oh[0][:, :, :], -2.0, pr[:, :, :], ALU.mult, ALU.add))
                    src = pr2
            V.tensor_tensor(chosen[:, :, :], oh[0][:, :, :], oh[1][:, :, :], ALU.add).then_inc(chosen_done, 1)
            link(V.tensor_tensor(sm[:, :], pm[:, :, 0], pm[:, :, 1], ALU.add))
            link(V.reciprocal(sm[:, :], sm[:, :]))
            V.tensor_tensor(weight[:, :, :], pm[:, :, :], sm[:, :].unsqueeze(2).broadcast_to([P, TT, 2]), ALU.mult)
            dve.wait_ge(b_up_written, 1)
            for m, factor in enumerate((1.0, 0.5)):
                V.tensor_scalar(b_up[:, m, :], b_up_ps[:, m * E * FC:(m + 1) * E * FC], factor, None, ALU.mult)
            dve.wait_ge(r_const, made["one_t, iota_t"])
            dve.wait_ge(counts_done, 1)
            within = counts_ps[:, 0, :].rearrange("p (t e) -> p e t", e=E)
            total = counts_ps[:, 1, :].rearrange("p (t e) -> p e t", e=E)
            link(V.tensor_copy(tot[:, :, :], total))
            flat = "p e t -> p (e t)"
            link(V.tensor_tensor_scan(cum[:, :, :].rearrange(flat), one_t[:, :], tot[:, :, :].rearrange(flat), 0.0,
                                      ALU.mult, ALU.add))
            link(V.memset(start[:, 0:1], 0.0))
            link(V.tensor_copy(start[:, 1:E], cum[:, 0:E - 1, TT - 1]))
            link(V.tensor_tensor(count[:, :], cum[:, :, TT - 1], start[:, :], ALU.subtract))
            link(V.tensor_tensor(cmp_[:, :, :], count[:, :].unsqueeze(2).broadcast_to([P, E, TT]),
                                 iota_t[:, :].unsqueeze(1).broadcast_to([P, E, TT]), ALU.is_gt))
            link(V.tensor_reduce(ntile[:, :], cmp_[:, :, :], AX.X, ALU.add))
            link(V.tensor_tensor_scan(tend[:, :], one_t[:, 0:E], ntile[:, :], 0.0, ALU.mult, ALU.add))
            link(V.tensor_tensor(base[:, :], tend[:, :], ntile[:, :], ALU.subtract))
            link(V.scalar_tensor_tensor(base[:, :], base[:, :], float(BR), start[:, :], ALU.mult, ALU.subtract))
            link(V.tensor_tensor(slot[:, :, :], cum[:, :, :], tot[:, :, :], ALU.subtract))
            link(V.tensor_tensor(slot[:, :, :], slot[:, :, :], base[:, :].unsqueeze(2).broadcast_to([P, E, TT]),
                                 ALU.add))
            link(V.tensor_tensor(slot[:, :, :], slot[:, :, :], within, ALU.add))
            for c in range(2):
                link(V.tensor_tensor(tmp[:, :, :], oh[c][:, :, :], slot[:, :, :].rearrange("p e t -> p t e"), ALU.mult))
                link(V.tensor_reduce(slot2[:, :, c], tmp[:, :, :], AX.X, ALU.add))
            link(V.tensor_copy(slot_i[:, :, :], slot2[:, :, :]))
            link(V.tensor_single_scalar(part_i[:, :, :], slot_i[:, :, :], P - 1, ALU.bitwise_and))
            link(V.tensor_copy(row_f[:, :], part_i[:, :, :].rearrange("p t c -> p (t c)")))
            link(V.tensor_single_scalar(part_i[:, :, :], slot_i[:, :, :], P.bit_length() - 1, ALU.logical_shift_right))
            link(V.tensor_copy(tile_f[:, :], part_i[:, :, :].rearrange("p t c -> p (t c)")))
            dve.wait_ge(r_const, made["iota_p, iota_s, value"])
            link(V.tensor_tensor(cmp_s[:, :, :], iota_s[:, 0:BLOCKS].unsqueeze(2).broadcast_to([P, BLOCKS, E]),
                                 tend[:, :].unsqueeze(1).broadcast_to([P, BLOCKS, E]), ALU.is_ge))
            link(V.tensor_reduce(exp_f[:, :], cmp_s[:, :, :], AX.X, ALU.add))
            link(V.tensor_scalar(exp_f[:, :], exp_f[:, :], float(E - 1), None, ALU.min))
            link(V.tensor_copy(expert[:, :], exp_f[:, :]))
            link(V.memset(one_r[:, 0, 0, :], 0.0))
            V.memset(one_v[:, 0, 0, :], 0.0).then_inc(table_zero, 1)

            dve.wait_ge(onehot_used, NOH)
            with dve.Fori(0, 2 * TT // (NOH * OH)) as t:
                for u in range(NOH):
                    dve.wait_ge(onehot_used, NOH * t + (u + 1))
                    for dst, ids, of, width in ((one_r, iota_p, row_f, P), (one_s, iota_s, tile_f, TILES)):
                        last = V.tensor_tensor(dst[:, u, :, :],
                                               ids[:, :].unsqueeze(1).broadcast_to([P, OH, width]),
                                               of[:, bass.ds(t * (NOH * OH) + u * OH, OH)].unsqueeze(2)
                                               .broadcast_to([P, OH, width]), ALU.is_equal)
                    last.then_inc(onehot_done, 1)

            dve.wait_ge(r_const, made["slot_id"])
            dve.wait_ge(onehot_used, 2 * TT // OH + NOH)
            link(V.tensor_copy(tab_f[:, 0, :], table_ps[:, :]))
            link(V.tensor_scalar(tab_f[:, 1, :], tab_f[:, 0, :], 0.5, None, ALU.is_lt))
            link(V.tensor_tensor(tab_f[:, 1, :], tab_f[:, 1, :], slot_id[:, :], ALU.mult))
            link(V.tensor_scalar(tab_f[:, 0, :], tab_f[:, 0, :], 1.0, None, ALU.subtract))
            link(V.tensor_tensor(tab_f[:, 1, :], tab_f[:, 0, :], tab_f[:, 1, :], ALU.add))
            link(V.tensor_copy(table[:, :, 1], tab_f[:, 1, :]))
            link(V.tensor_scalar(tab_f[:, 2, :], tab_f[:, 0, :], 0.0, None, ALU.max))
            link(V.tensor_copy(tab_i[:, :], tab_f[:, 2, :]))
            V.tensor_single_scalar(table[:, :, 0], tab_i[:, :], 1, ALU.logical_shift_right).then_inc(table_done, 1)
            dve.wait_ge(table_done, 1)

        route.close()
        part = ctx

        NX, NR = 8, 4
        NY = 4
        from_row = sb("from_row", [P, NX, 2], I32)
        to_row = sb("to_row", [P, NR, 2], I32)
        xg = sb("xg", [P, NX, 2, D])
        xt_hi = sb("xt_hi", [P, 2, BR], F32R)
        xt_lo = sb("xt_lo", [P, 2, BR], F32R)
        w_cur = sb("w_cur", [P, 2, 4, F], F32R)
        b_cur = sb("b_cur", [P, 2, 2, FC])
        gelu = sb("gelu", [P, 2, FC, BR])
        gate = sb("gate", [P, 2, FC, BR])
        hid = sb("hid", [P, 2, FC, BR])
        res = sb("res", [P, NR, 2, D])
        st6 = sb("st6", [P, 2, 2, 6])
        mean_var = sb("mean_var", [P, NR, 2, 2])
        inv_dev = sb("inv_dev", [P, NR, 2])
        z = sb("z", [P, NR, 2, D])
        y2 = sb("y2", [P, NY, NT, 2 * D])

        up = pb("up", [P, 4, F])
        y_ps = [pb(f"y_ps{h}", [P, D]) for h in range(2)]
        xt_ps = pb("xt_ps", [P, BR])
        gb_ps = pb("gb_ps", [P, 2 * D])

        idx_done = sem("idx_done")
        gathered = [sem(f"gathered{u}") for u in range(NX)]
        scattered = [sem(f"scattered{u}") for u in range(NR)]
        xt_written, xhi_done, xlo_done = sem("xt_written"), sem("xhi_done"), sem("xlo_done")
        wi_copied, wg_copied = sem("wi_copied"), sem("wg_copied")
        up_written, up_read = sem("up_written"), sem("up_read")
        hid_done, gb_written = sem("hid_done"), sem("gb_written")
        y_written, res_done, ve_done, dev_done = sem("y_written"), sem("res_done"), sem("ve_done"), sem("dev_done")
        z_done, x_chain, z_chain = sem("z_done"), sem("x_chain"), sem("z_chain")
        comb_loaded = [sem(f"comb_loaded{u}") for u in range(NY)]
        comb_done, c_chain, out_stored = sem("comb_done"), sem("c_chain"), sem("out_stored")

        experts = ExitStack()
        block = experts.enter_context(nc.Block())

        def rounds(s, u, n):
            return 32 * (s // n + 1) if isinstance(s, int) else (s - u % n) * (32 // n) + 32

        def stages(eng, stage_fns):
            most = max(lag for lag, _ in stage_fns)

            def step(s, u):
                for lag, fn in stage_fns:
                    if isinstance(s, int) and not 0 <= s - lag < BLOCKS:
                        continue
                    fn(s - lag, (u - lag) % UNROLL)

            least = min(lag for lag, _ in stage_fns)
            for u in range(least, UNROLL):
                step(u, u % UNROLL)
            full = BLOCKS // UNROLL - (1 if least < 0 else 0)
            if full > 1:
                with eng.Fori(1, full) as k:
                    for u in range(UNROLL):
                        step(k * UNROLL + u, u)
            for s in range(max(full, 1) * UNROLL, BLOCKS + most):
                step(s, s % UNROLL)

        def expert_registers(eng, name):
            regs = [eng.alloc_register(f"{name}_expert{u}") for u in range(UNROLL)]

            def load(s, u):
                eng.reg_load(regs[u], expert[0:1, bass.ds(s, 1)])

            return load, lambda u: eng.snap(regs[u], min_val=0, max_val=E - 1)

        def before(s, n):
            return isinstance(s, int) and s < n

        @block.gpsimd
        def _(pool):
            def gather(s, u):
                wait_apart(pool, idx_done, s + 1)
                for h in range(2):
                    pool.indirect_dma_start(xg[:, u, h, :], None, xn2_d[0:NTOK, :],
                                            bass.IndirectOffsetOnAxis(from_row[:, u, h:h + 1], 0))\
                        .then_inc(gathered[u], 16)

            def deviation(s, u):
                pool.wait_ge(ve_done, s + 1)
                r = u % NR
                pool.tensor_tensor(inv_dev[:, r, :], inv_dev[:, r, :], minus_half[:, 0:2],
                                   ALU.pow).then_inc(dev_done, 1)

            def scatter(s, u):
                wait_apart(pool, z_done, s + 1)
                for h in range(2):
                    pool.indirect_dma_start(y2_d, bass.IndirectOffsetOnAxis(to_row[:, u % NR, h:h + 1], 0),
                                            z[:, u % NR, h, :], None).then_inc(scattered[u % NR], 16)

            stages(pool, [(2, deviation), (3, scatter), (-4, gather)])
            for r in range(NR):
                pool.wait_ge(scattered[r], 32 * (BLOCKS // NR))

        @block.tensor
        def _(pe):
            load_expert, expert_of = expert_registers(pe, "pe")

            def transpose_x(s, u):
                pe.wait_ge(gathered[u], rounds(s, u, NX))
                if not before(s, 1):
                    pe.wait_ge(xlo_done, s)
                for h in range(2):
                    last = nc.tensor.transpose(xt_ps[:, h * P:(h + 1) * P], xg[:, u, h, :], ident[:, :])
                last.then_inc(xt_written, 1)

            def up_projections(s, u):
                b2 = u % 2
                pe.wait_ge(wi_copied, s + 1)
                pe.wait_ge(wg_copied, s + 1)
                pe.wait_ge(xlo_done, s + 1)
                pe.wait_ge(xhi_done, s + 1)
                for bank in range(4):
                    m = bank % 2
                    if not before(s, 1):
                        pe.wait_ge(up_read, 4 * s + (bank - 3))
                    for half in range(2):
                        c = 2 * (bank // 2) + half
                        hi = w_cur[:, b2, 2 * m, c * P:(c + 1) * P]
                        lo = w_cur[:, b2, 2 * m + 1, c * P:(c + 1) * P]
                        dst = up[:, bank, half * BR:(half + 1) * BR]
                        nc.tensor.matmul(dst, lo, xt_hi[:, b2, :], start=True, stop=False)
                        nc.tensor.matmul(dst, hi, xt_lo[:, b2, :], start=False, stop=False)
                        last = nc.tensor.matmul(dst, hi, xt_hi[:, b2, :], start=False, stop=True)
                    last.then_inc(up_written, 1)

            def down(s, u):
                e = expert_of(u)
                pe.wait_ge(hid_done, 2 * s + 2)
                if not before(s, 1):
                    pe.wait_ge(res_done, s)
                for h in range(2):
                    nc.tensor.matmul(y_ps[h][:, :], b_sel[:, bass.ds(e * P, P)], b_stack[:, 0:D],
                                     start=True, stop=False)
                    for c in range(FC):
                        last = nc.tensor.matmul(y_ps[h][:, :], hid[:, u % 2, c, h * P:(h + 1) * P],
                                                wo_sb[:, bass.ds(e * (FC * D) + c * D, D)],
                                                start=False, stop=(c == FC - 1))
                last.then_inc(y_written, 1)

            def gamma_beta(s, u):
                e = expert_of(u)
                if not before(s, 1):
                    pe.wait_ge(z_done, s)
                nc.tensor.matmul(gb_ps[:, :], b_sel[:, bass.ds(e * P, P)], b_stack[:, D:3 * D],
                                 start=True, stop=True).then_inc(gb_written, 1)

            stages(pe, [(0, up_projections), (0, load_expert), (1, down), (-2, transpose_x), (2, gamma_beta)])

        @block.scalar
        def _(act):
            load_expert, expert_of = expert_registers(act, "act")

            def copy_weights(s, u):
                e = expert_of(u)
                if not before(s, 2):
                    act.wait_ge(up_written, 4 * s - 4)
                nc.scalar.activation(w_cur[:, u % 2, 0, :], w_hi[0][:, bass.ds(e * F, F)], ACT.Copy)
                nc.scalar.activation(w_cur[:, u % 2, 1, :], w_lo[0][:, bass.ds(e * F, F)],
                                     ACT.Copy).then_inc(wi_copied, 1)

            def activations(s, u):
                if not before(s, 2):
                    act.wait_ge(hid_done, 2 * s - 2)
                for bank in range(4):
                    m = bank % 2
                    act.wait_ge(up_written, 4 * s + (bank + 1))
                    for half in range(2):
                        c = 2 * (bank // 2) + half
                        src = up[:, bank, half * BR:(half + 1) * BR]
                        bias = b_cur[:, u % 2, m, c:c + 1]
                        if m == 0:
                            last = nc.scalar.activation(gelu[:, u % 2, c, :], src, ACT.Gelu, bias=bias)
                        else:
                            last = nc.scalar.activation(gate[:, u % 2, c, :], src, ACT.Tanh, bias=bias, scale=0.5)
                    last.then_inc(up_read, 1)

            def high_x(s, u):
                act.wait_ge(xt_written, s + 1)
                if not before(s, 2):
                    act.wait_ge(up_written, 4 * s - 4)
                nc.scalar.activation(xt_hi[:, u % 2, :], xt_ps[:, :], ACT.Copy).then_inc(xhi_done, 1)

            stages(act, [(-1, copy_weights), (0, activations), (-2, load_expert), (-2, high_x)])

        @block.vector
        def _(dve):
            V = nc.vector
            load_expert, expert_of = expert_registers(dve, "dve")

            def copy_weights(s, u):
                e = expert_of(u)
                if not before(s, 2):
                    dve.wait_ge(up_read, 4 * s - 4)
                V.tensor_copy(b_cur[:, u % 2, :, :], b_up[:, :, bass.ds(e * FC, FC)])
                V.tensor_copy(w_cur[:, u % 2, 2, :], w_hi[1][:, bass.ds(e * F, F)])
                V.tensor_copy(w_cur[:, u % 2, 3, :], w_lo[1][:, bass.ds(e * F, F)]).then_inc(wg_copied, 1)

            def product(s, u):
                if not before(s, 2):
                    dve.wait_ge(y_written, s - 1)
                for half in range(2):
                    dve.wait_ge(up_read, 4 * s + (2 * half + 2))
                    c = slice(2 * half, 2 * half + 2)
                    V.scalar_tensor_tensor(hid[:, u % 2, c, :], gate[:, u % 2, c, :], 1.0, gelu[:, u % 2, c, :],
                                           ALU.add, ALU.mult).then_inc(hid_done, 1)

            def low_x(s, u):
                dve.wait_ge(xhi_done, s + 1)
                if not before(s, 2):
                    dve.wait_ge(up_written, 4 * s - 4)
                V.tensor_tensor(xt_lo[:, u % 2, :], xt_ps[:, :], xt_hi[:, u % 2, :].bitcast(F32),
                                ALU.subtract).then_inc(xlo_done, 1)

            def take_rows(s, u):
                V.tensor_copy(from_row[:, u, :], table[:, bass.ds(2 * s, 2), 0]).then_inc(idx_done, 1)

            def residual(s, u):
                dve.wait_ge(gathered[u], rounds(s, u, NX))
                dve.wait_ge(y_written, s + 1)
                for h in range(2):
                    last = V.scalar_tensor_tensor(res[:, u % NR, h, :], y_ps[h][:, :], 0.5, xg[:, u, h, :],
                                                  ALU.mult, ALU.add)
                last.then_inc(res_done, 1)

            def statistics(s, u):
                wait_apart(dve, res_done, s + 1)
                for h in range(2):
                    last = V.bn_stats(st6[:, u % 2, h, :], res[:, u % NR, h, :])
                last.then_inc(x_chain, 1)

            def mean_and_variance(s, u):
                wait_apart(dve, x_chain, 2 * s + 1)
                for h in range(2):
                    last = V.bn_aggr(mean_var[:, u % NR, h, :], st6[:, u % 2, h, :])
                last.then_inc(x_chain, 1)

            def add_epsilon(s, u):
                dve.wait_ge(x_chain, 2 * s + 2)
                V.tensor_scalar(inv_dev[:, u % NR, :], mean_var[:, u % NR, :, 1], EXPERT_EPS, None, ALU.add)\
                    .then_inc(ve_done, 1)

            def scale(s, u):
                r = u % NR
                if not before(s, NR):
                    dve.wait_ge(scattered[r], rounds(s, u, NR) - 32)
                V.tensor_copy(to_row[:, r, :], table[:, bass.ds(2 * s, 2), 1])
                dve.wait_ge(gb_written, s + 1)
                for h in range(2):
                    last = V.scalar_tensor_tensor(z[:, r, h, :], res[:, r, h, :], mean_var[:, r, h, 0:1],
                                                  gb_ps[:, 0:D], ALU.subtract, ALU.mult)
                last.then_inc(z_chain, 1)

            def shift(s, u):
                r = u % NR
                dve.wait_ge(z_chain, s + 1)
                dve.wait_ge(dev_done, s + 1)
                for h in range(2):
                    last = V.scalar_tensor_tensor(z[:, r, h, :], z[:, r, h, :], inv_dev[:, r, h:h + 1],
                                                  gb_ps[:, D:2 * D], ALU.mult, ALU.add)
                last.then_inc(z_done, 1)

            stages(dve, [(-1, copy_weights), (3, scale), (-5, take_rows), (2, mean_and_variance), (3, shift),
                         (2, add_epsilon), (0, product), (-2, load_expert), (1, residual), (-2, low_x),
                         (1, statistics)])

        experts.close()
        block2 = ctx.enter_context(nc.Block())
        GROUPS = TT // NT

        @block2.sync
        def _(sp):
            y2_v = y2_d[0:2 * NTOK, :].rearrange("(g i p c) d -> g p i (c d)", p=P, i=NT, c=2)
            for g in range(GROUPS):
                if g >= NY:
                    sp.wait_ge(comb_done, g - NY + 1)
                sp.dma_start(y2[:, g % NY, :, :], y2_v[g, :, :, :]).then_inc(comb_loaded[g % NY], 16)

        @block2.scalar
        def _(act):
            out_v = out.rearrange("b (i p) d -> b p i d", p=P)
            for g in range(GROUPS):
                act.wait_ge(comb_done, g + 1)
                act.dma_start(out_v[g, :, :, :], x_all[:, g * NT:(g + 1) * NT, :]).then_inc(out_stored, 16)
            act.wait_ge(out_stored, 16 * GROUPS)

        @block2.vector
        def _(dve):
            for g in range(GROUPS):
                dve.wait_ge(comb_loaded[g % NY], 16 * (g // NY + 1))
                for c in range(2):
                    for t in range(g * NT, (g + 1) * NT):
                        last = nc.vector.scalar_tensor_tensor(
                            x_all[:, t, :], y2[:, g % NY, t % NT, c * D:(c + 1) * D], weight[:, t, c:c + 1],
                            x_all[:, t, :], ALU.mult, ALU.add)
                    if c == 0:
                        last.then_inc(c_chain, 1)
                        dve.wait_ge(c_chain, g + 1)
                last.then_inc(comb_done, 1)


_INS = ["L0_attn_x", "L0_attn_W_qkv", "L0_attn_W_out", "L0_ffn_Wr", "L0_ffn_br", "L0_ffn_Wi", "L0_ffn_bi",
        "L0_ffn_Wg", "L0_ffn_bg", "L0_ffn_Wo", "L0_ffn_bo", "L0_ffn_gamma", "L0_ffn_beta"]


def kernel(**inputs):
    import numpy as _np
    import concourse.bacc as _bacc
    from concourse import mybir as _mybir
    from concourse.bass_utils import run_bass_kernel_spmd as _run

    nc = _bacc.Bacc("TRN2", target_bir_lowering=False, num_devices=1)
    arrays, args = {}, []
    for name in _INS:
        a = _np.ascontiguousarray(inputs[name])
        arrays[name] = a
        args.append(nc.dram_tensor(name, a.shape, _mybir.dt.from_np(a.dtype), kind="ExternalInput").ap())
    shape = arrays["L0_attn_x"].shape
    out = nc.dram_tensor("out", shape, _mybir.dt.float32, kind="ExternalOutput").ap()
    attention_and_routed_experts(nc, *args, out)
    r = _run(nc, [arrays], core_ids=[0])
    return r.results[0]["out"]
```
